# Optimizing a Trainium2 kernel written in Bass

```python
import numpy as np
import jax
import jax.numpy as jnp

def _softmax(x, axis=-1):
    return jax.nn.softmax(x, axis=axis)

def _gelu(x):
    return jax.nn.gelu(x, approximate=True)

def _silu(x):
    return jax.nn.silu(x)

def _sigmoid(x):
    return jax.nn.sigmoid(x)

def _layernorm(x, axis=-1, eps=1e-05):
    m = jnp.mean(x, axis=axis, keepdims=True)
    v = jnp.var(x, axis=axis, keepdims=True)
    return (x - m) / jnp.sqrt(v + eps)

def _scatter_add(tgt, idx, src, axis=0):
    return tgt.at[idx].add(src)

def _segment_sum(src, seg, n):
    return jax.ops.segment_sum(src, seg, n)
kernel_name = 'mk_gnn_resnorm_d2_gnn_r32_ee1699'

def setup_inputs(seed: int=0):
    np.random.seed(seed)
    _w = jnp.asarray

    def _rec_inputs():
        import jax
        import jax.numpy as jnp
        _gk = jax.random.key(seed)
        x = 0.0001712 + 1 * jax.random.normal(jax.random.fold_in(_gk, 1), (3125, 16), jnp.float32)
        _s = jax.random.randint(jax.random.fold_in(_gk, 2), (50000,), 0, 3125, jnp.int32)
        _d = jax.random.randint(jax.random.fold_in(_gk, 3), (50000,), 0, 3125, jnp.int32)
        _loop = jnp.arange(3125, dtype=jnp.int32)
        src = jnp.concatenate([_s, _d, _loop])
        dst = jnp.concatenate([_d, _s, _loop])
        _o = jnp.argsort(dst, stable=True)
        src = src[_o]
        dst = dst[_o]
        edge_attr_8 = -0.00019784 + 0.999804 * jax.random.normal(jax.random.fold_in(_gk, 12), (103125, 8), jnp.float32)
        return (x, src, dst, edge_attr_8)
    x, src, dst, edge_attr_8 = _rec_inputs()

    def _L0_gnn_setup():
        import jax, jax.numpy as jnp
        import numpy as np
        N = 50000
        E = 25000
        S = 2
        D_NODE_IN, D_EDGE_IN, D, H, D_OUT = (16, 8, 64, 64, 16)
        LN_EPS = 1e-05

        def _mlp(x, w0, b0, w1, b1):
            return jax.nn.silu(x @ w0 + b0) @ w1 + b1

        def _ln(x, g, b):
            m = jnp.mean(x, axis=-1, keepdims=True)
            v = jnp.var(x, axis=-1, keepdims=True)
            return (x - m) * jax.lax.rsqrt(v + LN_EPS) * g + b
        key = jax.random.key(seed)
        ks = iter(jax.random.split(key, 40))
        p = lambda shape: jax.random.normal(next(ks), shape, dtype=jnp.float32) * 0.1
        inp = {'node_feat': jax.random.normal(next(ks), (N, D_NODE_IN), dtype=jnp.float32), 'edge_feat': jax.random.normal(next(ks), (E, D_EDGE_IN), dtype=jnp.float32), 'senders': jax.random.randint(next(ks), (E,), 0, N, dtype=jnp.int32), 'receivers': jax.random.randint(next(ks), (E,), 0, N, dtype=jnp.int32), 'node_enc_w0': p((D_NODE_IN, H)), 'node_enc_b0': p((H,)), 'node_enc_w1': p((H, D)), 'node_enc_b1': p((D,)), 'node_enc_g': jnp.ones((D,), jnp.float32), 'node_enc_beta': jnp.zeros((D,), jnp.float32), 'edge_enc_w0': p((D_EDGE_IN, H)), 'edge_enc_b0': p((H,)), 'edge_enc_w1': p((H, D)), 'edge_enc_b1': p((D,)), 'edge_enc_g': jnp.ones((D,), jnp.float32), 'edge_enc_beta': jnp.zeros((D,), jnp.float32), 'edge_blk_w0': p((S, 3 * D, H)), 'edge_blk_b0': p((S, H)), 'edge_blk_w1': p((S, H, D)), 'edge_blk_b1': p((S, D)), 'edge_blk_g': jnp.ones((S, D), jnp.float32), 'edge_blk_beta': jnp.zeros((S, D), jnp.float32), 'node_blk_w0': p((S, 2 * D, H)), 'node_blk_b0': p((S, H)), 'node_blk_w1': p((S, H, D)), 'node_blk_b1': p((S, D)), 'node_blk_g': jnp.ones((S, D), jnp.float32), 'node_blk_beta': jnp.zeros((S, D), jnp.float32), 'dec_w0': p((D, H)), 'dec_b0': p((H,)), 'dec_w1': p((H, D_OUT)), 'dec_b1': p((D_OUT,))}
        return inp
    _L0_gnn_all = _L0_gnn_setup()
    _L0_gnn_in = {k: v for k, v in _L0_gnn_all.items() if k in ('node_enc_w0', 'node_enc_b0', 'node_enc_w1', 'node_enc_b1', 'node_enc_g', 'node_enc_beta', 'edge_enc_w0', 'edge_enc_b0', 'edge_enc_w1', 'edge_enc_b1', 'edge_enc_g', 'edge_enc_beta', 'edge_blk_w0', 'edge_blk_b0', 'edge_blk_w1', 'edge_blk_b1', 'edge_blk_g', 'edge_blk_beta', 'node_blk_w0', 'node_blk_b0', 'node_blk_w1', 'node_blk_b1', 'node_blk_g', 'node_blk_beta', 'dec_w0', 'dec_b0', 'dec_w1', 'dec_b1')}
    del _L0_gnn_all

    def _L1_gnn_setup():
        import jax, jax.numpy as jnp
        import numpy as np
        N_NODES = 3125
        N_EDGES = 50000

        def _sage_conv(x, edge_index, W_l, b, W_r, num_nodes):
            src, dst = (edge_index[0], edge_index[1])
            msg_sum = jax.ops.segment_sum(x[src], dst, num_segments=num_nodes)
            deg = jax.ops.segment_sum(jnp.ones((edge_index.shape[1],), x.dtype), dst, num_segments=num_nodes)
            agg = msg_sum / jnp.maximum(deg, 1.0)[:, None]
            return agg @ W_l + b + x @ W_r
        key = jax.random.key(seed)
        ks = jax.random.split(key, 8)
        x = jax.random.normal(ks[0], (N_NODES, 16), dtype=jnp.float32)
        edge_index = jax.random.randint(ks[1], (2, N_EDGES), 0, N_NODES, dtype=jnp.int64)
        s1 = 1.0 / np.sqrt(16.0)
        s2 = 1.0 / np.sqrt(32.0)
        W1_l = jax.random.normal(ks[2], (16, 32), dtype=jnp.float32) * s1
        b1 = jax.random.normal(ks[3], (32,), dtype=jnp.float32) * s1
        W1_r = jax.random.normal(ks[4], (16, 32), dtype=jnp.float32) * s1
        W2_l = jax.random.normal(ks[5], (32, 16), dtype=jnp.float32) * s2
        b2 = jax.random.normal(ks[6], (16,), dtype=jnp.float32) * s2
        W2_r = jax.random.normal(ks[7], (32, 16), dtype=jnp.float32) * s2
        return {'x': x, 'edge_index': edge_index, 'W1_l': W1_l, 'b1': b1, 'W1_r': W1_r, 'W2_l': W2_l, 'b2': b2, 'W2_r': W2_r}
    _L1_gnn_all = _L1_gnn_setup()
    _L1_gnn_in = {k: v for k, v in _L1_gnn_all.items() if k in ('W1_l', 'b1', 'W1_r', 'W2_l', 'b2', 'W2_r')}
    del _L1_gnn_all
    return {'x': x, 'src': src, 'dst': dst, 'edge_attr_8': edge_attr_8, 'L0_gnn_node_enc_w0': _L0_gnn_in['node_enc_w0'], 'L0_gnn_node_enc_b0': _L0_gnn_in['node_enc_b0'], 'L0_gnn_node_enc_w1': _L0_gnn_in['node_enc_w1'], 'L0_gnn_node_enc_b1': _L0_gnn_in['node_enc_b1'], 'L0_gnn_node_enc_g': _L0_gnn_in['node_enc_g'], 'L0_gnn_node_enc_beta': _L0_gnn_in['node_enc_beta'], 'L0_gnn_edge_enc_w0': _L0_gnn_in['edge_enc_w0'], 'L0_gnn_edge_enc_b0': _L0_gnn_in['edge_enc_b0'], 'L0_gnn_edge_enc_w1': _L0_gnn_in['edge_enc_w1'], 'L0_gnn_edge_enc_b1': _L0_gnn_in['edge_enc_b1'], 'L0_gnn_edge_enc_g': _L0_gnn_in['edge_enc_g'], 'L0_gnn_edge_enc_beta': _L0_gnn_in['edge_enc_beta'], 'L0_gnn_edge_blk_w0': _L0_gnn_in['edge_blk_w0'], 'L0_gnn_edge_blk_b0': _L0_gnn_in['edge_blk_b0'], 'L0_gnn_edge_blk_w1': _L0_gnn_in['edge_blk_w1'], 'L0_gnn_edge_blk_b1': _L0_gnn_in['edge_blk_b1'], 'L0_gnn_edge_blk_g': _L0_gnn_in['edge_blk_g'], 'L0_gnn_edge_blk_beta': _L0_gnn_in['edge_blk_beta'], 'L0_gnn_node_blk_w0': _L0_gnn_in['node_blk_w0'], 'L0_gnn_node_blk_b0': _L0_gnn_in['node_blk_b0'], 'L0_gnn_node_blk_w1': _L0_gnn_in['node_blk_w1'], 'L0_gnn_node_blk_b1': _L0_gnn_in['node_blk_b1'], 'L0_gnn_node_blk_g': _L0_gnn_in['node_blk_g'], 'L0_gnn_node_blk_beta': _L0_gnn_in['node_blk_beta'], 'L0_gnn_dec_w0': _L0_gnn_in['dec_w0'], 'L0_gnn_dec_b0': _L0_gnn_in['dec_b0'], 'L0_gnn_dec_w1': _L0_gnn_in['dec_w1'], 'L0_gnn_dec_b1': _L0_gnn_in['dec_b1'], 'L1_gnn_W1_l': _L1_gnn_in['W1_l'], 'L1_gnn_b1': _L1_gnn_in['b1'], 'L1_gnn_W1_r': _L1_gnn_in['W1_r'], 'L1_gnn_W2_l': _L1_gnn_in['W2_l'], 'L1_gnn_b2': _L1_gnn_in['b2'], 'L1_gnn_W2_r': _L1_gnn_in['W2_r']}

def reference(x, src, dst, edge_attr_8, L0_gnn_node_enc_w0, L0_gnn_node_enc_b0, L0_gnn_node_enc_w1, L0_gnn_node_enc_b1, L0_gnn_node_enc_g, L0_gnn_node_enc_beta, L0_gnn_edge_enc_w0, L0_gnn_edge_enc_b0, L0_gnn_edge_enc_w1, L0_gnn_edge_enc_b1, L0_gnn_edge_enc_g, L0_gnn_edge_enc_beta, L0_gnn_edge_blk_w0, L0_gnn_edge_blk_b0, L0_gnn_edge_blk_w1, L0_gnn_edge_blk_b1, L0_gnn_edge_blk_g, L0_gnn_edge_blk_beta, L0_gnn_node_blk_w0, L0_gnn_node_blk_b0, L0_gnn_node_blk_w1, L0_gnn_node_blk_b1, L0_gnn_node_blk_g, L0_gnn_node_blk_beta, L0_gnn_dec_w0, L0_gnn_dec_b0, L0_gnn_dec_w1, L0_gnn_dec_b1, L1_gnn_W1_l, L1_gnn_b1, L1_gnn_W1_r, L1_gnn_W2_l, L1_gnn_b2, L1_gnn_W2_r):
    import jax
    import jax.numpy as jnp

    def _L0_gnn_ref(node_feat, edge_feat, senders, receivers, node_enc_w0, node_enc_b0, node_enc_w1, node_enc_b1, node_enc_g, node_enc_beta, edge_enc_w0, edge_enc_b0, edge_enc_w1, edge_enc_b1, edge_enc_g, edge_enc_beta, edge_blk_w0, edge_blk_b0, edge_blk_w1, edge_blk_b1, edge_blk_g, edge_blk_beta, node_blk_w0, node_blk_b0, node_blk_w1, node_blk_b1, node_blk_g, node_blk_beta, dec_w0, dec_b0, dec_w1, dec_b1):
        import jax, jax.numpy as jnp
        import numpy as np
        N = 50000
        E = 25000
        S = 2
        D_NODE_IN, D_EDGE_IN, D, H, D_OUT = (16, 8, 64, 64, 16)
        LN_EPS = 1e-05

        def _mlp(x, w0, b0, w1, b1):
            return jax.nn.silu(x @ w0 + b0) @ w1 + b1

        def _ln(x, g, b):
            m = jnp.mean(x, axis=-1, keepdims=True)
            v = jnp.var(x, axis=-1, keepdims=True)
            return (x - m) * jax.lax.rsqrt(v + LN_EPS) * g + b
        num_nodes = node_feat.shape[0]
        n = _ln(_mlp(node_feat, node_enc_w0, node_enc_b0, node_enc_w1, node_enc_b1), node_enc_g, node_enc_beta)
        e = _ln(_mlp(edge_feat, edge_enc_w0, edge_enc_b0, edge_enc_w1, edge_enc_b1), edge_enc_g, edge_enc_beta)
        for s in range(S):
            ce = jnp.concatenate([e, n[senders], n[receivers]], axis=-1)
            e = e + _ln(_mlp(ce, edge_blk_w0[s], edge_blk_b0[s], edge_blk_w1[s], edge_blk_b1[s]), edge_blk_g[s], edge_blk_beta[s])
            agg = jax.ops.segment_sum(e.astype(jnp.float32), receivers, num_segments=num_nodes)
            cn = jnp.concatenate([n, agg.astype(n.dtype)], axis=-1)
            n = n + _ln(_mlp(cn, node_blk_w0[s], node_blk_b0[s], node_blk_w1[s], node_blk_b1[s]), node_blk_g[s], node_blk_beta[s])
        return _mlp(n, dec_w0, dec_b0, dec_w1, dec_b1)

    def _L1_gnn_ref(x, edge_index, W1_l, b1, W1_r, W2_l, b2, W2_r):
        import jax, jax.numpy as jnp
        import numpy as np
        N_NODES = 3125
        N_EDGES = 50000

        def _sage_conv(x, edge_index, W_l, b, W_r, num_nodes):
            src, dst = (edge_index[0], edge_index[1])
            msg_sum = jax.ops.segment_sum(x[src], dst, num_segments=num_nodes)
            deg = jax.ops.segment_sum(jnp.ones((edge_index.shape[1],), x.dtype), dst, num_segments=num_nodes)
            agg = msg_sum / jnp.maximum(deg, 1.0)[:, None]
            return agg @ W_l + b + x @ W_r
        n = x.shape[0]
        h = _sage_conv(x, edge_index, W1_l, b1, W1_r, n)
        h = jax.nn.relu(h)
        out = _sage_conv(h, edge_index, W2_l, b2, W2_r, n)
        return out
    edge_index = jnp.stack([src, dst])
    x = _layernorm(x + _L0_gnn_ref(x, edge_attr_8, src, dst, L0_gnn_node_enc_w0, L0_gnn_node_enc_b0, L0_gnn_node_enc_w1, L0_gnn_node_enc_b1, L0_gnn_node_enc_g, L0_gnn_node_enc_beta, L0_gnn_edge_enc_w0, L0_gnn_edge_enc_b0, L0_gnn_edge_enc_w1, L0_gnn_edge_enc_b1, L0_gnn_edge_enc_g, L0_gnn_edge_enc_beta, L0_gnn_edge_blk_w0, L0_gnn_edge_blk_b0, L0_gnn_edge_blk_w1, L0_gnn_edge_blk_b1, L0_gnn_edge_blk_g, L0_gnn_edge_blk_beta, L0_gnn_node_blk_w0, L0_gnn_node_blk_b0, L0_gnn_node_blk_w1, L0_gnn_node_blk_b1, L0_gnn_node_blk_g, L0_gnn_node_blk_beta, L0_gnn_dec_w0, L0_gnn_dec_b0, L0_gnn_dec_w1, L0_gnn_dec_b1), axis=-1)
    x = _layernorm(x + _L1_gnn_ref(x, edge_index, L1_gnn_W1_l, L1_gnn_b1, L1_gnn_W1_r, L1_gnn_W2_l, L1_gnn_b2, L1_gnn_W2_r), axis=-1)
    return x

_drawn_inputs = setup_inputs


def setup_inputs(seed=0):
    import zlib

    import numpy as np

    out = dict(_drawn_inputs(seed))
    spreads = {'L0_gnn_node_enc_g': (1.0, 0.2),
     'L0_gnn_node_enc_beta': (0.0, 0.1),
     'L0_gnn_edge_enc_g': (1.0, 0.2),
     'L0_gnn_edge_enc_beta': (0.0, 0.274),
     'L0_gnn_edge_blk_g': (1.0, 0.2),
     'L0_gnn_edge_blk_beta': (0.0, 0.1),
     'L0_gnn_node_blk_g': (1.0, 0.2),
     'L0_gnn_node_blk_beta': (0.0, 0.1)}
    factors = {'L0_gnn_node_blk_b0': 35.644, 'L0_gnn_node_blk_b1': 23.089}
    for name, (base, spread) in spreads.items():
        noise = np.random.default_rng([zlib.crc32(name.encode()), seed]).standard_normal(out[name].shape)
        drawn = base * np.exp(spread * noise) if base else spread * noise
        out[name] = jnp.asarray(drawn.astype(out[name].dtype))
    for name, factor in factors.items():
        out[name] = (out[name] * factor).astype(out[name].dtype)
    return out
```

```python
from contextlib import ExitStack

import concourse.bass as bass
from concourse import mybir
from concourse.alu_op_type import AluOpType as ALU

N_NODES = 3125
N_EDGES = 103125
D = 64
D_NODE, D_EDGE, D_SAGE = 16, 8, 32
EPS = 1e-5

P = 128
HALF = 512
CHUNK = 2 * HALF
TILES = CHUNK // P
J = HALF // P
NCH = -(-N_EDGES // CHUNK)
PARTS = 3
WIN = P // PARTS
WROWS = PARTS * WIN
NBLK = 512
NB = -(-N_NODES // NBLK)
NPAD = NB * NBLK
SWEEP = 256
NSW = NPAD // SWEEP
DEPTH = 2

assert NCH % 2 == 1 and NCH >= 7


def build(nc, I, out):
    f32, bf16, i32 = mybir.dt.float32, mybir.dt.bfloat16, mybir.dt.int32
    ACT = mybir.ActivationFunctionType
    AX = mybir.AxisListType
    ctx = ExitStack()
    with ctx:
        def sb(name, shape, dt=f32):
            return ctx.enter_context(nc.sbuf_tensor(name, shape, dt))

        def bank(name):
            return ctx.enter_context(nc.psum_tensor(name, [P, 512], f32))

        def sem(name):
            return ctx.enter_context(nc.semaphore(name))

        def sems(prefix, names):
            return {n: sem(f"{prefix}_{n}") for n in names.split()}

        def dram(name, shape, dt=f32):
            return nc.dram_tensor(name, shape, dt, kind="Internal").ap()

        def bc(ap, shape):
            return ap.to_broadcast(shape)

        send_tab = [dram(f"send_tab{s}", (NPAD, D)) for s in range(2)]
        recv_tab = [dram(f"recv_tab{s}", (NPAD, D)) for s in range(2)]
        recv_parts = [dram(f"recv_parts{s}", (NPAD * PARTS, D), bf16) for s in range(2)]
        sage_tab = [dram(f"sage_tab{s}", (NPAD, D_NODE)) for s in range(2)]
        e1_dram = dram("e1_dram", (NCH, P, HALF))
        rel_dram = dram("rel_dram", (NCH, CHUNK), bf16)
        base_dram = dram("base_dram", (NCH, 2))
        span_dram = dram("span_dram", (NCH, 2))
        bias_dram = dram("bias_dram", (3, PARTS, D), bf16)

        ident = sb("ident", [P, P])
        ones = sb("ones", [P, P])
        ones_bf = sb("ones_bf", [PARTS, P], bf16)
        neg_half = sb("neg_half", [P, TILES])
        node_iota = sb("node_iota", [P, NPAD])
        win_row = sb("win_row", [WROWS, 1])
        flag = sb("flag", [1, 1], i32)
        base_i = sb("base_i", [1, NCH * 2], i32)
        dst_em = sb("dst_em", [P, NCH * TILES])
        rel_em = sb("rel_em", [P, NCH * TILES])
        n_fm = sb("n_fm", [D, NPAD])
        agg = sb("agg", [P, 2, NPAD])
        agg2 = sb("agg2", [D, NPAD])
        x1_em = sb("x1_em", [P, NB, J * D_NODE])
        h_fm = sb("h_fm", [D_SAGE, NPAD])
        rdeg = n_fm[0:D_NODE, :]
        x1_fm = agg[0:D_NODE, 0, :]
        x_fm = h_fm[0:D_NODE, :]
        x_em = sb("x_em", [P, NB, J * D_NODE])

        enc_w0 = sb("enc_w0", [2 * D_EDGE, P])
        w_e = [sb(f"w_e{s}", [P, P]) for s in range(2)]
        w1 = [sb(f"w1_{s}", [P, D]) for s in range(3)]
        w1_bd = [sb(f"w1_bd{s}", [P, P]) for s in range(3)]
        b1 = [sb(f"b1_{s}", [1, D]) for s in range(3)]
        b0 = [sb(f"b0_{s}", [P, 1]) for s in range(3)]
        gam = [sb(f"gam{s}", [P, 1]) for s in range(3)]
        bet = [sb(f"bet{s}", [P, 1]) for s in range(3)]
        b1_part = [sb(f"b1_part{s}", [1, PARTS, D], bf16) for s in range(3)]
        b1_rest = [sb(f"b1_rest{s}", [1, D]) for s in range(3)]
        b1_rows = [sb(f"b1_rows{s}", [PARTS, TILES, D], bf16) for s in range(3)]
        row_mean = sb("row_mean", [P, 12])
        w_sr = [sb(f"w_sr{s}", [D, 2 * D]) for s in range(2)]
        nenc_w0 = sb("nenc_w0", [D_NODE, D])
        nb0 = [sb(f"nb0_{s}", [D, 1]) for s in range(3)]
        nw1 = [sb(f"nw1_{s}", [D, D]) for s in range(3)]
        nb1 = [sb(f"nb1_{s}", [1, D]) for s in range(3)]
        ngam = [sb(f"ngam{s}", [D, 1]) for s in range(3)]
        nbet = [sb(f"nbet{s}", [D, 1]) for s in range(3)]
        nb1_row = [sb(f"nb1_row{s}", [1, J, D]) for s in range(3)]
        w_n = [sb(f"w_n{s}", [D, D]) for s in range(2)]
        w_a = [sb(f"w_a{s}", [P, D]) for s in range(2)]
        w_ag = [sb(f"w_ag{s}", [P, D]) for s in range(2)]
        w_ag2 = sb("w_ag2", [D, D])
        gam_stack = sb("gam_stack", [P, 1])
        bet_sum = sb("bet_sum", [D, 2])
        w_deg = sb("w_deg", [1, 2, D])
        dec_w0 = sb("dec_w0", [D, D])
        dec_b0 = sb("dec_b0", [D, 1])
        dec_w1 = sb("dec_w1", [D, D_NODE])
        dec_b1 = sb("dec_b1", [1, J, D_NODE])
        s_w1l = sb("s_w1l", [D_NODE, D_SAGE])
        s_w1r = sb("s_w1r", [D_NODE, D_SAGE])
        s_b1 = sb("s_b1", [D_SAGE, 1])
        s_w2l = sb("s_w2l", [D_SAGE, D_NODE])
        s_w2r = sb("s_w2r", [D_SAGE, D_NODE])
        s_b2 = sb("s_b2", [1, J, D_NODE])

        idx_ring = [sb(f"idx_ring{u}", [P, TILES], i32) for u in range(DEPTH)]
        idxd_ring = [sb(f"idxd_ring{u}", [P, TILES], i32) for u in range(DEPTH)]
        g_ring = [sb(f"g_ring{u}", [P, TILES, D]) for u in range(DEPTH)]
        gd_ring = [sb(f"gd_ring{u}", [P, TILES, D]) for u in range(DEPTH)]
        gs_ring = [sb(f"gs_ring{u}", [P, TILES, D_NODE]) for u in range(DEPTH)]
        attr_ring = [sb(f"attr_ring{u}", [2 * D_EDGE, HALF]) for u in range(DEPTH)]
        relb_ring = [sb(f"relb_ring{u}", [WROWS, CHUNK], bf16) for u in range(DEPTH)]
        prw_ring = [sb(f"prw_ring{u}", [WROWS, 2, D], bf16) for u in range(DEPTH)]
        ohf_ring = [sb(f"ohf_ring{u}", [WROWS, CHUNK], bf16) for u in range(DEPTH)]
        ohe_ring = [sb(f"ohe_ring{u}", [P, TILES, WIN]) for u in range(DEPTH)]
        z_ring = [sb(f"z_ring{u}", [P, 2, TILES, D]) for u in range(DEPTH)]
        e0_ring = [sb(f"e0_ring{u}", [P, HALF]) for u in range(DEPTH)]
        e1_ring = [sb(f"e1_ring{u}", [P, HALF]) for u in range(DEPTH)]
        sweep_oh = sb("sweep_oh", [P, TILES, SWEEP])
        h_buf = [sb(f"h_buf{i}", [P, HALF]) for i in range(2)]
        sq_buf = [sb(f"sq_buf{i}", [P, TILES, D + 1]) for i in range(2)]
        var_buf = [sb(f"var_buf{i}", [P, TILES]) for i in range(2)]
        rstd_buf = [sb(f"rstd_buf{i}", [P, TILES]) for i in range(2)]

        hn = sb("hn", [D, NBLK])
        x_blk = sb("x_blk", [D_NODE, NBLK])
        agg_blk = sb("agg_blk", [P, 2, NBLK])
        agg2_blk = sb("agg2_blk", [D, NBLK])
        n_blk = sb("n_blk", [D, NBLK])
        h_blk = sb("h_blk", [D_SAGE, NBLK])
        sqn = sb("sqn", [P, J, D + 1])
        varn = sb("varn", [P, J])
        rstdn = sb("rstdn", [P, J])
        zn = sb("zn", [P, J, D])
        tabn = sb("tabn", [P, J, 2, D])
        partn = sb("partn", [P, J, PARTS, D], bf16)
        restn = sb("restn", [P, J, D])
        xs = sb("xs", [P, J, D_NODE])
        xc = sb("xc", [P, J, D_NODE])
        xq = sb("xq", [P, J, D_NODE])
        xm = sb("xm", [P, J])
        t2n = sb("t2n", [P, J, D_NODE])
        aggd = sb("aggd", [D_NODE, NBLK])
        outn = sb("outn", [P, J, D_NODE])

        spare = sweep_oh[0:NCH, :, :].rearrange("c t w -> c (t w)")
        dst_rows = spare[:, 0:CHUNK].rearrange("c (h e) -> c h e", h=2)
        dst_rows_i = spare[:, CHUNK:2 * CHUNK].bitcast(i32)
        rel_rows = sb("rel_rows", [NCH, 2, HALF], bf16)
        dst_em_i = sb("dst_em_i", [P, NCH * TILES], i32)
        base_f = sb("base_f", [NCH, 2])
        top_f = sb("top_f", [NCH, 2])
        span_f = sb("span_f", [NCH, 2])
        span_row = sb("span_row", [1, NCH * 2])
        span_max = sb("span_max", [1, 1])
        base_row = sb("base_row", [1, NCH * 2])
        base_all = sb("base_all", [P, NCH, 2])

        ps_pre = [bank("ps_pre0"), bank("ps_pre1")]
        ps_y = [bank("ps_y0"), bank("ps_y1")]
        ps_zt = [bank("ps_zt0"), bank("ps_zt1")]
        ps_seg = bank("ps_seg")
        ps_misc = bank("ps_misc")

        st = sems("st", "loads consts ident chain rel_ready base_out base_in em_ready biases biasrow_in "
                        "mm folded flag_ready sent pool_iota ready rows_out")
        names = ("attr_in0 attr_in1 idx_in0 idx_in1 idxd_in0 idxd_in1 relb_in0 relb_in1 prw_in0 prw_in1 "
                 "gathered0 gathered1 gathered_d0 gathered_d1 e1_in0 e1_in1 e1_out0 e1_out1 "
                 "enc_pre enc_h enc_y enc_sq enc_var enc_rstd enc_z enc_zt enc_e "
                 "ohf ohe blk_pre blk_h blk_y blk_sq blk_var blk_rstd blk_z blk_zt blk_e1 seg added swept_oh")
        short = "idx_in0 idx_in1 gathered0 gathered1 ohe seg added swept_oh"
        bnames = " ".join(n for n in names.split() if not n.startswith(("attr", "enc", "e1_out", "blk_zt", "blk_e1")))
        PH = [sems(f"p{p}", (names, bnames, short, short)[p]) for p in range(4)]
        edges_done = [sem(f"edges_done{p}") for p in range(4)]
        mlp = sems("mlp", "block_in pre h y sq var rstd z zt n tab evac parts")
        ND = [{**(mlp if i < 3 else {}), "first": NB * i if i < 3 else 0, **sems(f"n{i}", own)}
              for i, own in enumerate(("split stored", "scaled split stored", "scaled copied blk lnv lnr own x1 x1t stored",
                                       "aggd pre h tab x1 stored", "aggd parts lnv lnr own x1"))]
        s_final = sem("s_final")

        block = ctx.enter_context(nc.Block())

        def slot(s, name, u):
            return s[f"{name}{u}"]

        def wait(eng, s, v):
            if not (isinstance(v, int) and v <= 0):
                eng.wait_ge(s, v)

        def value(eng, v):
            return v if isinstance(v, int) else eng.to_reg(v)

        W_LOADS = []

        def load(dst, src):
            W_LOADS.append((dst, src))

        def col(name, s=None):
            a = I[name] if s is None else I[name][s]
            return a.rearrange("(a b) -> a b", b=1)

        def row(name, s=None):
            a = I[name] if s is None else I[name][s]
            return a.rearrange("(a b) -> a b", a=1)

        for h in range(2):
            load(enc_w0[h * D_EDGE:(h + 1) * D_EDGE, h * D:(h + 1) * D], I["edge_enc_w0"])
            for s in range(2):
                load(w_e[s][h * D:(h + 1) * D, h * D:(h + 1) * D], I["edge_blk_w0"][s, 0:D, :])
                load(w1[1 + s][h * D:(h + 1) * D, :], I["edge_blk_w1"][s])
                load(b0[1 + s][h * D:(h + 1) * D, :], col("edge_blk_b0", s))
                load(gam[1 + s][h * D:(h + 1) * D, :], col("edge_blk_g", s))
                load(bet[1 + s][h * D:(h + 1) * D, :], col("edge_blk_beta", s))
                load(w_a[s][h * D:(h + 1) * D, :], I["node_blk_w0"][s, D:2 * D, :])
                load(w_sr[s][:, h * D:(h + 1) * D], I["edge_blk_w0"][s, (1 + h) * D:(2 + h) * D, :])
            load(w1[0][h * D:(h + 1) * D, :], I["edge_enc_w1"])
            load(b0[0][h * D:(h + 1) * D, :], col("edge_enc_b0"))
            load(gam[0][h * D:(h + 1) * D, :], col("edge_enc_g"))
            load(bet[0][h * D:(h + 1) * D, :], col("edge_enc_beta"))
        load(gam_stack[0:D, :], col("edge_enc_g"))
        load(gam_stack[D:P, :], col("edge_blk_g", 0))
        load(b1[0][:, :], row("edge_enc_b1"))
        for s in range(2):
            load(b1[1 + s][:, :], row("edge_blk_b1", s))
            load(w_n[s][:, :], I["node_blk_w0"][s, 0:D, :])
            load(nb0[1 + s][:, :], col("node_blk_b0", s))
            load(nw1[1 + s][:, :], I["node_blk_w1"][s])
            load(nb1[1 + s][:, :], row("node_blk_b1", s))
            load(ngam[1 + s][:, :], col("node_blk_g", s))
            load(nbet[1 + s][:, :], col("node_blk_beta", s))
        load(nenc_w0[:, :], I["node_enc_w0"])
        load(nb0[0][:, :], col("node_enc_b0"))
        load(nw1[0][:, :], I["node_enc_w1"])
        load(nb1[0][:, :], row("node_enc_b1"))
        load(ngam[0][:, :], col("node_enc_g"))
        load(nbet[0][:, :], col("node_enc_beta"))
        load(dec_w0[:, :], I["dec_w0"])
        load(dec_b0[:, :], col("dec_b0"))
        load(dec_w1[:, :], I["dec_w1"])
        load(s_w1l[:, :], I["W1_l"])
        load(s_w1r[:, :], I["W1_r"])
        load(s_b1[:, :], col("sage_b1"))
        load(s_w2l[:, :], I["W2_l"])
        load(s_w2r[:, :], I["W2_r"])
        for j in range(J):
            load(dec_b1[:, j, :], row("dec_b1"))
            load(s_b2[:, j, :], row("sage_b2"))
        load(x_fm[:, :], I["x_fm"])
        load(x_em[:, :, :], I["x_em"])
        load(win_row[:, :], I["win_row"])
        LOADED = 16 * (len(W_LOADS) + 2)

        def rounds(eng, body):
            body(0, 0, 0, False)
            body(1, 0, 1, False)
            with eng.Fori(1, NCH // 2) as k:
                body(2 * k, k, 0, False)
                body(2 * k + 1, k, 1, False)
            body(NCH - 1, NCH // 2, 0, True)

        @block.sync
        def _(sp):
            sp.dma_start(dst_rows_i[:, :], I["dst_rows"]).then_inc(st["loads"], 16)
            sp.dma_start(dst_em_i[:, :], I["dst_em"]).then_inc(st["loads"], 16)
            sp.wait_ge(st["consts"], 1)
            for dst, src in W_LOADS:
                sp.dma_start(dst, src).then_inc(st["loads"], 16)
            sp.wait_ge(st["rel_ready"], 1)
            sp.dma_start(rel_dram, rel_rows[:, :, :].rearrange("c h e -> c (h e)")).then_inc(st["rows_out"], 16)
            sp.dma_start(base_dram, base_f[:, :]).then_inc(st["base_out"], 16)
            sp.dma_start(span_dram, span_f[:, :]).then_inc(st["base_out"], 16)
            sp.wait_ge(st["base_out"], 32)
            sp.dma_start(base_row[:, :], base_dram.rearrange("(a c) h -> a (c h)", a=1)).then_inc(st["base_in"], 16)
            sp.dma_start(span_row[:, :], span_dram.rearrange("(a c) h -> a (c h)", a=1)).then_inc(st["base_in"], 16)
            sp.dma_start(base_all[:, :, :].rearrange("p c h -> p (c h)"),
                         base_dram.rearrange("(a c) h -> a (c h)", a=1).to_broadcast([P, NCH * 2])
                         ).then_inc(st["base_in"], 16)
            sp.wait_ge(st["biases"], 1)
            for s in range(3):
                sp.dma_start(bias_dram[s:s + 1], b1_part[s][:, :, :]).then_inc(st["sent"], 16)
            sp.wait_ge(st["sent"], 48)
            for s in range(3):
                for t in range(TILES):
                    sp.dma_start(b1_rows[s][:, t, :], bias_dram[s]).then_inc(st["biasrow_in"], 16)
            sp.wait_ge(st["rows_out"], 16)
            sp.wait_ge(st["flag_ready"], 1)
            general = sp.value_load(flag[0:1, 0:1], min_val=0, max_val=1)

            def store_tables(s):
                nd = ND[s]
                with sp.Fori(0, NB) as b:
                    sp.wait_ge(nd["parts"], nd["first"] + b + 1)
                    sp.dma_start(send_tab[s].rearrange("(b j p) d -> b p j d", j=J, p=P)[bass.ds(b, 1)]
                                 .rearrange("a p j d -> (a p) j d"), tabn[:, :, 0, :]).then_inc(nd["stored"], 16)
                    sp.dma_start(recv_tab[s].rearrange("(b j p) d -> b p j d", j=J, p=P)[bass.ds(b, 1)]
                                 .rearrange("a p j d -> (a p) j d"), tabn[:, :, 1, :]).then_inc(nd["stored"], 16)
                    sp.dma_start(recv_parts[s].rearrange("(b j p t) d -> b p j (t d)", j=J, p=P, t=PARTS)[bass.ds(b, 1)]
                                 .rearrange("a p j d -> (a p) j d"),
                                 partn[:, :, :, :].rearrange("p j t d -> p j (t d)")).then_inc(nd["stored"], 16)

            def store_sage(s, nd, src):
                with sp.Fori(0, NB) as b:
                    sp.wait_ge(nd["x1"], b + 1)
                    sp.dma_start(sage_tab[s].rearrange("(b j p) d -> b p j d", j=J, p=P)[bass.ds(b, 1)]
                                 .rearrange("a p j d -> (a p) j d"), src).then_inc(nd["stored"], 16)

            def edge_phase(p, g):
                s = PH[p]
                tab = p

                def windows(c, k, u):
                    h0 = sp.value_load(base_i[0:1, bass.ds(2 * c, 1)], min_val=0, max_val=N_NODES - 1)
                    h1 = sp.value_load(base_i[0:1, bass.ds(2 * c + 1, 1)], min_val=0, max_val=N_NODES - 1)
                    sp.wait_ge(st["ready"], 1)
                    wait(sp, s["ohf"], value(sp, c - 1))
                    sp.dma_start(relb_ring[u][:, :], rel_dram[bass.ds(c, 1)].to_broadcast([WROWS, CHUNK])
                                 ).then_inc(slot(s, "relb_in", u), 16)
                    wait(sp, s["blk_pre"], c - 1)
                    for h, v in enumerate((h0, h1)):
                        sp.dma_start(prw_ring[u][:, h, :], recv_parts[tab][bass.ds(v * PARTS, WROWS)]
                                     ).then_inc(slot(s, "prw_in", u), 16)

                def indices(c, k, u):
                    wait(sp, slot(s, "gathered", u), 128 * k)
                    sp.dma_start(idx_ring[u][:, :], I["src_em"][bass.ds(c, 1)].rearrange("a p t -> (a p) t")
                                 ).then_inc(slot(s, "idx_in", u), 16)
                    if g and p < 2:
                        wait(sp, slot(s, "gathered_d", u), 128 * k)
                        sp.dma_start(idxd_ring[u][:, :], I["dst_idx"][bass.ds(c, 1)].rearrange("a p t -> (a p) t")
                                     ).then_inc(slot(s, "idxd_in", u), 16)

                def attrs(c, k, u):
                    wait(sp, s["enc_pre"], c - 1)
                    sp.dma_start(attr_ring[u][:, :], I["attr_fm"][bass.ds(c, 1)].rearrange("a p t -> (a p) t")
                                 ).then_inc(slot(s, "attr_in", u), 16)

                def load_e1(c, k, u):
                    wait(sp, s["blk_pre"], c - 1)
                    sp.dma_start(e1_ring[u][:, :], e1_dram[bass.ds(c, 1)].rearrange("a p t -> (a p) t")
                                 ).then_inc(slot(s, "e1_in", u), 16)

                def store_e1(c, k, u):
                    sp.wait_ge(s["blk_e1"], c + 1)
                    sp.dma_start(e1_dram[bass.ds(c, 1)].rearrange("a p t -> (a p) t"), e1_ring[u][:, :]
                                 ).then_inc(slot(s, "e1_out", u), 16)

                def body(c, k, u, last):
                    indices(c, k, u)
                    if p == 0:
                        attrs(c, k, u)
                    if p == 1:
                        load_e1(c, k, u)
                    if p < 2 and not g:
                        windows(c, k, u)
                    if p == 0 and not (isinstance(c, int) and c < 2):
                        store_e1(c - 2, k - 1, u)

                rounds(sp, body)
                if p == 0:
                    store_e1(NCH - 2, NCH // 2 - 1, 1)
                    store_e1(NCH - 1, NCH // 2, 0)
                    sp.wait_ge(s["e1_out0"], 16 * (NCH // 2 + 1))
                    sp.wait_ge(s["e1_out1"], 16 * (NCH // 2))

            def either(p):
                with sp.If(general):
                    edge_phase(p, 1)
                with sp.Else():
                    edge_phase(p, 0)
                sp.nop()

            store_tables(0)
            either(0)
            store_tables(1)
            either(1)
            store_sage(0, ND[2], xs[:, :, :])
            either(2)
            store_sage(1, ND[3], t2n[:, :, :])
            either(3)
            with sp.Fori(0, NB) as b:
                sp.wait_ge(ND[4]["x1"], b + 1)
                sp.dma_start(out.rearrange("(b j p) d -> b p j d", j=J, p=P)[bass.ds(b, 1)]
                             .rearrange("a p j d -> (a p) j d"), outn[:, :, :]).then_inc(s_final, 16)
            sp.wait_ge(s_final, 16 * NB)

        @block.gpsimd
        def _(pool):
            nc.gpsimd.memset(ident[:, :], 0.0).then_inc(st["ident"], 1)
            pool.wait_ge(st["ident"], 1)
            nc.gpsimd.affine_select(out=ident[:, :], in_=ident[:, :], compare_op=ALU.not_equal, fill=1.0,
                                    base=0, pattern=[[-1, P]], channel_multiplier=1).then_inc(st["ident"], 1)
            nc.gpsimd.iota(node_iota[:, :], pattern=[[1, NPAD]], base=0, channel_multiplier=0,
                           allow_small_or_imprecise_dtypes=True).then_inc(st["pool_iota"], 1)
            pool.wait_ge(st["flag_ready"], 1)
            general = pool.value_load(flag[0:1, 0:1], min_val=0, max_val=1)

            def node_rstd(nd):
                with pool.Fori(0, NB) as b:
                    pool.wait_ge(nd["var"], nd["first"] + b + 1)
                    nc.gpsimd.tensor_tensor(out=rstdn[:, :], in0=varn[:, :], in1=neg_half[:, 0:J],
                                            op=ALU.pow).then_inc(nd["rstd"], 1)

            def edge_phase(p, g):
                s = PH[p]
                tab = (send_tab + sage_tab)[p]
                ring = g_ring if p < 2 else gs_ring
                used = s["blk_pre"] if p < 2 else s["seg"]
                per = NSW if g and p >= 2 else 1
                stored = ND[p]["stored"]
                stored_n = 16 * NB * (PARTS if p < 2 else 1)

                def gather(c, k, u):
                    n_idx, n_used = value(pool, 16 * k + 16), value(pool, (c - 1) * per)
                    pool.wait_ge(stored, stored_n)
                    pool.wait_ge(slot(s, "idx_in", u), n_idx)
                    wait(pool, used, n_used)
                    for t in range(TILES):
                        nc.gpsimd.indirect_dma_start(
                            out=ring[u][:, t, :], out_offset=None, in_=tab,
                            in_offset=bass.IndirectOffsetOnAxis(ap=idx_ring[u][:, t:t + 1], axis=0),
                        ).then_inc(slot(s, "gathered", u), 16)
                    if g and p < 2:
                        pool.wait_ge(stored, stored_n)
                        pool.wait_ge(slot(s, "idxd_in", u), n_idx)
                        for t in range(TILES):
                            nc.gpsimd.indirect_dma_start(
                                out=gd_ring[u][:, t, :], out_offset=None, in_=recv_tab[p],
                                in_offset=bass.IndirectOffsetOnAxis(ap=idxd_ring[u][:, t:t + 1], axis=0),
                            ).then_inc(slot(s, "gathered_d", u), 16)

                def rstd(i, var, done, c):
                    pool.wait_ge(var, c + 1)
                    nc.gpsimd.tensor_tensor(out=rstd_buf[i][:, :], in0=var_buf[i][:, :], in1=neg_half[:, :],
                                            op=ALU.pow).then_inc(done, 1)

                gather(0, 0, 0)
                if p == 0:
                    rstd(0, s["enc_var"], s["enc_rstd"], 0)

                def body(c, k, u, last):
                    if not last:
                        gather(c + 1, k + u, 1 - u)
                    if p == 0 and not last:
                        rstd(0, s["enc_var"], s["enc_rstd"], c + 1)
                    if p < 2:
                        rstd(1, s["blk_var"], s["blk_rstd"], c)

                rounds(pool, body)

            def either(p):
                with pool.If(general):
                    edge_phase(p, 1)
                with pool.Else():
                    edge_phase(p, 0)
                pool.nop()

            node_rstd(ND[0])
            either(0)
            node_rstd(ND[1])
            either(1)
            nd = ND[2]
            with pool.Fori(0, NB) as b:
                pool.wait_ge(nd["var"], nd["first"] + b + 1)
                nc.gpsimd.tensor_tensor(out=rstdn[:, :], in0=varn[:, :], in1=neg_half[:, 0:J],
                                        op=ALU.pow).then_inc(nd["rstd"], 1)
                pool.wait_ge(nd["lnv"], b + 1)
                nc.gpsimd.tensor_tensor(out=rstdn[:, :], in0=varn[:, :], in1=neg_half[:, 0:J],
                                        op=ALU.pow).then_inc(nd["lnr"], 1)
            either(2)
            either(3)
            nd = ND[4]
            with pool.Fori(0, NB) as b:
                pool.wait_ge(nd["lnv"], b + 1)
                nc.gpsimd.tensor_tensor(out=rstdn[:, :], in0=varn[:, :], in1=neg_half[:, 0:J],
                                        op=ALU.pow).then_inc(nd["lnr"], 1)

        @block.scalar
        def _(act):
            act.wait_ge(st["flag_ready"], 1)
            general = act.value_load(flag[0:1, 0:1], min_val=0, max_val=1)
            act.wait_ge(st["ready"], 1)

            def node_mlp(nd, bias, b):
                act.wait_ge(nd["pre"], nd["first"] + b + 1)
                nc.scalar.activation(hn[:, :], ps_pre[0][0:D, :], ACT.Silu, bias=bias).then_inc(nd["h"], 1)
                act.wait_ge(nd["y"], nd["first"] + b + 1)
                nc.scalar.activation(sqn[:, :, 0:D], ps_y[0][:, 0:J * D].rearrange("p (j d) -> p j d", d=D),
                                     ACT.Square, scale=D ** -0.5).then_inc(nd["sq"], 1)

            def tables(nd, b):
                act.wait_ge(nd["tab"], nd["first"] + b + 1)
                nc.scalar.activation(tabn[:, :, :, :], ps_zt[1][:, :].rearrange("p (j s d) -> p j s d", s=2, d=D),
                                     ACT.Copy).then_inc(nd["evac"], 1)

            def edge_phase(p, g):
                s = PH[p]

                def silu(i, pre, h, hfree, bias, c):
                    wait(act, hfree, c)
                    act.wait_ge(pre, c + 1)
                    nc.scalar.activation(h_buf[i][:, :], ps_pre[i][:, :], ACT.Silu, bias=bias).then_inc(h, 1)

                def square(i, y, sq, free, c):
                    wait(act, free, c)
                    act.wait_ge(y, c + 1)
                    nc.scalar.activation(sq_buf[i][:, :, 0:D], ps_y[i][:, :].rearrange("p (t d) -> p t d", d=D),
                                         ACT.Square, scale=D ** -0.5).then_inc(sq, 1)

                def to_e0(c, u):
                    wait(act, s["blk_e1"], c - 1)
                    act.wait_ge(s["enc_zt"], c + 1)
                    nc.scalar.activation(e0_ring[u][:, :], ps_zt[0][:, :], ACT.Identity,
                                         bias=bet[0][:, :], scale=gam[0][:, :]).then_inc(s["enc_e"], 1)

                if p == 0:
                    silu(0, s["enc_pre"], s["enc_h"], s["enc_y"], b0[0][:, :], 0)
                    square(0, s["enc_y"], s["enc_sq"], s["enc_var"], 0)
                    to_e0(0, 0)

                def body(c, k, u, last):
                    enc = p == 0 and not last
                    if enc:
                        silu(0, s["enc_pre"], s["enc_h"], s["enc_y"], b0[0][:, :], c + 1)
                    silu(1, s["blk_pre"], s["blk_h"], s["blk_y"], b0[1 + p][:, :], c)
                    if enc:
                        square(0, s["enc_y"], s["enc_sq"], s["enc_var"], c + 1)
                    square(1, s["blk_y"], s["blk_sq"], s["blk_var"], c)
                    if enc:
                        to_e0(c + 1, 1 - u)

                if p < 2:
                    rounds(act, body)

            def either(p):
                with act.If(general):
                    edge_phase(p, 1)
                with act.Else():
                    edge_phase(p, 0)
                act.nop()

            for s in range(2):
                with act.Fori(0, NB) as b:
                    node_mlp(ND[s], nb0[s][:, :], b)
                    tables(ND[s], b)
                either(s)
            nd = ND[2]
            with act.Fori(0, NB) as b:
                node_mlp(nd, nb0[2][:, :], b)
                act.wait_ge(nd["tab"], nd["first"] + b + 1)
                nc.scalar.activation(hn[:, :], ps_pre[1][0:D, :], ACT.Silu, bias=dec_b0[:, :]).then_inc(nd["evac"], 1)
            nd = ND[3]
            with act.Fori(0, NB) as b:
                act.wait_ge(nd["pre"], nd["first"] + b + 1)
                for dst in (h_blk[:, :], h_fm[:, bass.ds(b * NBLK, NBLK)]):
                    last = nc.scalar.activation(dst, ps_pre[0][0:D_SAGE, :], ACT.Relu, bias=s_b1[:, :])
                last.then_inc(nd["h"], 1)

        @block.tensor
        def _(pe):
            mm = nc.tensor.matmul
            pe.wait_ge(st["ident"], 2)
            pe.wait_ge(st["folded"], 1)
            for s in range(2):
                mm(ps_misc[0:1, s * D:(s + 1) * D], bet_sum[:, s:s + 1], w_a[s][0:D, :], start=True, stop=True)
            mm(ps_misc[:, P:P + 1], w_e[1][:, :], bet[1][:, :], start=True, stop=True).then_inc(st["mm"], 1)
            pe.wait_ge(st["flag_ready"], 1)
            general = pe.value_load(flag[0:1, 0:1], min_val=0, max_val=1)
            pe.wait_ge(st["biasrow_in"], 16 * 3 * TILES)
            pe.wait_ge(st["ready"], 1)

            def node_tail(nd, s, b):
                pe.wait_ge(nd["h"], nd["first"] + b + 1)
                mm(ps_y[0][:, 0:J * D], ones[0:1, :], nb1_row[s][:, :, :].rearrange("a j d -> a (j d)"),
                   start=True, stop=False)
                for j in range(J):
                    last = mm(ps_y[0][:, j * D:(j + 1) * D], hn[:, j * P:(j + 1) * P], nw1[s][:, :],
                              start=False, stop=j == J - 1)
                last.then_inc(nd["y"], 1)
                pe.wait_ge(st["ready"], 1)
                pe.wait_ge(nd["z"], nd["first"] + b + 1)
                for j in range(J):
                    last = nc.tensor.transpose(ps_zt[0][0:D, j * P:(j + 1) * P], zn[:, j, :], ident[:, :])
                last.then_inc(nd["zt"], 1)

            def tables(nd, s, b):
                pe.wait_ge(nd["n"], nd["first"] + b + 1)
                for j in range(J):
                    last = mm(ps_zt[1][:, j * 2 * D:(j + 1) * 2 * D], n_blk[:, j * P:(j + 1) * P],
                              w_sr[s][:, :], start=True, stop=True)
                last.then_inc(nd["tab"], 1)

            def node_update(nd, s, b):
                n_in = value(pe, nd["first"] + b + 1)
                pe.wait_ge(st["ready"], 1)
                pe.wait_ge(nd["block_in"], n_in)
                mm(ps_pre[0][0:D, :], w_n[s][:, :], n_blk[:, :], start=True, stop=False)
                mm(ps_pre[0][0:D, :], w_ag[s][:, :], agg_blk[:, 0, :], start=False, stop=False)
                if s == 1:
                    mm(ps_pre[0][0:D, :], w_ag2[:, :], agg2_blk[:, :], start=False, stop=False)
                mm(ps_pre[0][0:D, :], w_deg[:, s, :], agg_blk[0:1, 1, :], start=False, stop=True).then_inc(nd["pre"], 1)

            def edge_phase(p, g):
                s = PH[p]
                def enc_pre(c, k, u):
                    wait(pe, s["enc_h"], c)
                    pe.wait_ge(slot(s, "attr_in", u), 16 * k + 16)
                    mm(ps_pre[0][:, :], enc_w0[:, :], attr_ring[u][:, :], start=True, stop=True).then_inc(s["enc_pre"], 1)

                def second(i, h, z, done, c):
                    wait(pe, z, c)
                    pe.wait_ge(h, c + 1)
                    w = 0 if i == 0 else 1 + p
                    mm(ps_y[i][:, :], ones_bf[:, :], b1_rows[w][:, :, :].rearrange("a t d -> a (t d)"),
                       start=True, stop=False)
                    for j in range(J):
                        last = mm(ps_y[i][:, j * P:(j + 1) * P], h_buf[i][:, j * P:(j + 1) * P], w1_bd[w][:, :],
                                  start=False, stop=j == J - 1)
                    last.then_inc(done, 1)

                def back(i, z, free, done, c, u):
                    wait(pe, free, c)
                    pe.wait_ge(z, c + 1)
                    for j in range(J):
                        last = nc.tensor.transpose(
                            ps_zt[i][:, j * P:(j + 1) * P],
                            z_ring[u][:, i, 2 * j:2 * j + 2, :].rearrange("p t d -> p (t d)"), ident[:, :])
                    last.then_inc(done, 1)

                def blk_pre(c, k, u):
                    wait(pe, s["blk_h"], c)
                    if p == 0:
                        pe.wait_ge(s["enc_e"], c + 1)
                        mm(ps_pre[1][:, :], w_e[0][:, :], e0_ring[u][:, :], start=True, stop=False)
                    else:
                        pe.wait_ge(slot(s, "e1_in", u), 16 * k + 16)
                        mm(ps_pre[1][:, :], w_e[1][:, :], e1_ring[u][:, :], start=True, stop=False)
                    if not g:
                        pe.wait_ge(slot(s, "prw_in", u), 32 * k + 32)
                        pe.wait_ge(s["ohf"], c + 1)
                        for hf in range(2):
                            mm(ps_pre[1][hf * D:(hf + 1) * D, :], prw_ring[u][:, hf, :],
                               ohf_ring[u][:, hf * HALF:(hf + 1) * HALF], start=False, stop=False)
                    rings = [g_ring, gd_ring] if g else [g_ring]
                    if g:
                        pe.wait_ge(slot(s, "gathered_d", u), 128 * k + 128)
                    pe.wait_ge(slot(s, "gathered", u), 128 * k + 128)
                    for ring in rings:
                        for j in range(J):
                            last = mm(ps_pre[1][:, j * P:(j + 1) * P],
                                      ring[u][:, 2 * j:2 * j + 2, :].rearrange("p t d -> p (t d)"), ident[:, :],
                                      start=False, stop=ring is rings[-1] and j == J - 1)
                    last.then_inc(s["blk_pre"], 1)

                def summed(u, t):
                    if p == 0:
                        return [(0, z_ring[u][:, 0, t, :]), (D, z_ring[u][:, 1, t, :])]
                    return [(0, z_ring[u][:, 1, t, :] if p == 1 else gs_ring[u][:, t, :])]

                rows = D if p < 2 else D_NODE

                def seg(c, k, u):
                    if g:
                        return seg_sweep(c, k, u)
                    wait(pe, s["added"], 2 * c)
                    if p < 2:
                        pe.wait_ge(s["blk_z"], c + 1)
                    else:
                        pe.wait_ge(slot(s, "gathered", u), 128 * k + 128)
                    pe.wait_ge(s["ohe"], c + 1)
                    for hf in range(2):
                        for n in range(len(summed(u, 0))):
                            for j in range(J):
                                t = 2 * j + hf
                                at, z = summed(u, t)[n]
                                last = mm(ps_seg[at:at + rows, hf * 2 * WIN:hf * 2 * WIN + WIN], z,
                                          ohe_ring[u][:, t, :], start=j == 0, stop=j == J - 1)
                        if p == 0:
                            for j in range(J):
                                t = 2 * j + hf
                                last = mm(ps_seg[:, hf * 2 * WIN + WIN:(hf + 1) * 2 * WIN], ones[:, :],
                                          ohe_ring[u][:, t, :], start=j == 0, stop=j == J - 1)
                    last.then_inc(s["seg"], 1)

                def seg_sweep(c, k, u):
                    with pe.Fori(0, NSW) as w:
                        if p < 2:
                            pe.wait_ge(s["blk_z"], c + 1)
                        else:
                            pe.wait_ge(slot(s, "gathered", u), 128 * k + 128)
                        pe.wait_ge(s["swept_oh"], c * NSW + w + 1)
                        for n in range(len(summed(u, 0))):
                            for t in range(TILES):
                                at, z = summed(u, t)[n]
                                last = mm(ps_seg[at:at + rows, 0:SWEEP], z, sweep_oh[:, t, :],
                                          start=t == 0, stop=t == TILES - 1)
                        if p == 0:
                            for t in range(TILES):
                                last = mm(ps_seg[:, SWEEP:2 * SWEEP], ones[:, :], sweep_oh[:, t, :],
                                          start=t == 0, stop=t == TILES - 1)
                        last.then_inc(s["seg"], 1)

                if p == 0:
                    enc_pre(0, 0, 0)
                    second(0, s["enc_h"], s["enc_z"], s["enc_y"], 0)
                    back(0, s["enc_z"], s["enc_e"], s["enc_zt"], 0, 0)

                def body(c, k, u, last):
                    enc = p == 0 and not last
                    if enc:
                        enc_pre(c + 1, k + u, 1 - u)
                    if p < 2:
                        blk_pre(c, k, u)
                    if enc:
                        second(0, s["enc_h"], s["enc_z"], s["enc_y"], c + 1)
                    if p < 2:
                        second(1, s["blk_h"], s["blk_z"], s["blk_y"], c)
                    if enc:
                        back(0, s["enc_z"], s["enc_e"], s["enc_zt"], c + 1, 1 - u)
                    if p == 0:
                        back(1, s["blk_z"], s["blk_e1"], s["blk_zt"], c, u)
                    seg(c, k, u)

                rounds(pe, body)

            def either(p):
                with pe.If(general):
                    edge_phase(p, 1)
                with pe.Else():
                    edge_phase(p, 0)
                pe.nop()

            nd = ND[0]
            with pe.Fori(0, NB) as b:
                pe.wait_ge(nd["block_in"], nd["first"] + b + 1)
                mm(ps_pre[0][0:D, :], nenc_w0[:, :], x_blk[:, :], start=True, stop=True).then_inc(nd["pre"], 1)
                node_tail(nd, 0, b)
                tables(nd, 0, b)
                pe.wait_ge(nd["parts"], nd["first"] + b + 1)
            either(0)
            nd = ND[1]
            pe.wait_ge(edges_done[0], 1)
            with pe.Fori(0, NB) as b:
                node_update(nd, 0, b)
                node_tail(nd, 1, b)
                tables(nd, 1, b)
                pe.wait_ge(nd["parts"], nd["first"] + b + 1)
            either(1)
            nd = ND[2]
            pe.wait_ge(edges_done[1], 1)
            with pe.Fori(0, NB) as b:
                node_update(nd, 1, b)
                node_tail(nd, 2, b)
                pe.wait_ge(st["ready"], 1)
                pe.wait_ge(nd["n"], nd["first"] + b + 1)
                mm(ps_pre[1][0:D, :], dec_w0[:, :], n_blk[:, :],
                   start=True, stop=True).then_inc(nd["tab"], 1)
                pe.wait_ge(nd["evac"], nd["first"] + b + 1)
                mm(ps_y[1][:, 0:J * D_NODE], ones[0:1, :], dec_b1[:, :, :].rearrange("a j d -> a (j d)"),
                   start=True, stop=False)
                for j in range(J):
                    last = mm(ps_y[1][:, j * D_NODE:(j + 1) * D_NODE], hn[:, j * P:(j + 1) * P], dec_w1[:, :],
                              start=False, stop=j == J - 1)
                last.then_inc(nd["parts"], 1)
                pe.wait_ge(nd["x1"], b + 1)
                for j in range(J):
                    last = nc.tensor.transpose(ps_zt[1][0:D_NODE, j * P:(j + 1) * P], xs[:, j, :], ident[:, :])
                last.then_inc(nd["x1t"], 1)
                pe.wait_ge(nd["blk"], b + 1)
            either(2)
            nd = ND[3]
            pe.wait_ge(edges_done[2], 1)
            with pe.Fori(0, NB) as b:
                n_in = value(pe, b + 1)
                pe.wait_ge(st["ready"], 1)
                pe.wait_ge(nd["aggd"], n_in)
                mm(ps_pre[0][0:D_SAGE, :], s_w1r[:, :], x_blk[:, :], start=True, stop=False)
                mm(ps_pre[0][0:D_SAGE, :], s_w1l[:, :], aggd[:, :], start=False, stop=True).then_inc(nd["pre"], 1)
                pe.wait_ge(nd["h"], nd["first"] + b + 1)
                for j in range(J):
                    last = mm(ps_y[0][:, j * D_NODE:(j + 1) * D_NODE], h_blk[:, j * P:(j + 1) * P],
                              s_w2l[:, :], start=True, stop=True)
                last.then_inc(nd["tab"], 1)
                pe.wait_ge(nd["x1"], b + 1)
            either(3)
            nd = ND[4]
            pe.wait_ge(edges_done[3], 1)
            with pe.Fori(0, NB) as b:
                mm(ps_y[0][:, 0:J * D_NODE], ones[0:1, :], s_b2[:, :, :].rearrange("a j d -> a (j d)"),
                   start=True, stop=False)
                pe.wait_ge(nd["aggd"], b + 1)
                for j in range(J):
                    y = ps_y[0][:, j * D_NODE:(j + 1) * D_NODE]
                    mm(y, aggd[:, j * P:(j + 1) * P], ident[0:D_NODE, 0:D_NODE], start=False, stop=False)
                    last = mm(y, h_blk[:, j * P:(j + 1) * P], s_w2r[:, :], start=False, stop=j == J - 1)
                last.then_inc(nd["parts"], 1)
                pe.wait_ge(nd["x1"], b + 1)

        @block.vector
        def _(dve):
            v = nc.vector
            chain = [0]

            def link(ins):
                chain[0] += 1
                ins.then_inc(st["chain"], 1)
                dve.wait_ge(st["chain"], chain[0])

            for t in [enc_w0] + w_e + w1_bd:
                link(v.memset(t[:, :], 0.0))
            v.memset(agg[:, :, :], 0.0)
            v.memset(agg2[:, :], 0.0)
            for t in sq_buf:
                v.memset(t[:, :, D:D + 1], EPS)
            v.memset(sqn[:, :, D:D + 1], EPS)
            v.memset(neg_half[:, :], -0.5)
            v.memset(ones_bf[:, :], 1.0)
            v.memset(ones[:, :], 1.0).then_inc(st["consts"], 1)
            dve.wait_ge(st["loads"], LOADED)
            link(v.tensor_copy(dst_rows[:, :, :].rearrange("c h e -> c (h e)"), dst_rows_i[:, :]))
            link(v.tensor_reduce(out=base_f[:, :], in_=dst_rows[:, :, :], axis=AX.X, op=ALU.min))
            link(v.tensor_reduce(out=top_f[:, :], in_=dst_rows[:, :, :], axis=AX.X, op=ALU.max))
            link(v.tensor_tensor(span_f[:, :], top_f[:, :], base_f[:, :], ALU.subtract))
            for h in range(2):
                last = v.tensor_scalar(rel_rows[:, h, :], dst_rows[:, h, :], base_f[:, h:h + 1], None, ALU.subtract)
            last.then_inc(st["rel_ready"], 1)
            for i, (w, n) in enumerate([(w, P) for w in w1] + [(w, D) for w in nw1] +
                                       [(w, 1) for w in b1] + [(w, 1) for w in nb1]):
                link(v.tensor_reduce(out=row_mean[0:n, i:i + 1], in_=w[:, :], axis=AX.X, op=ALU.add))
                link(v.tensor_scalar(row_mean[0:n, i:i + 1], row_mean[0:n, i:i + 1], 1.0 / D, None, ALU.mult))
                link(v.tensor_scalar(w[:, :], w[:, :], row_mean[0:n, i:i + 1], None, ALU.subtract))
            for s in range(3):
                for h in range(2):
                    link(v.tensor_copy(w1_bd[s][h * D:(h + 1) * D, h * D:(h + 1) * D], w1[s][h * D:(h + 1) * D, :]))
                link(v.tensor_copy(b1_part[s][:, 0, :], b1[s][:, :]))
                link(v.tensor_tensor(b1_rest[s][:, :], b1[s][:, :], b1_part[s][:, 0, :], ALU.subtract))
                link(v.tensor_copy(b1_part[s][:, 1, :], b1_rest[s][:, :]))
                link(v.tensor_tensor(b1_rest[s][:, :], b1_rest[s][:, :], b1_part[s][:, 1, :], ALU.subtract))
                link(v.tensor_copy(b1_part[s][:, 2, :], b1_rest[s][:, :]))
                for j in range(J):
                    link(v.tensor_copy(nb1_row[s][:, j, :], nb1[s][:, :]))
            v.nop().then_inc(st["biases"], 1)
            for s in range(2):
                link(v.tensor_scalar(w_ag[s][:, :], w_a[s][:, :], gam_stack[:, :], None, ALU.mult))
            link(v.tensor_scalar(w_ag2[:, :], w_a[1][0:D, :], gam[2][0:D, :], None, ALU.mult))
            link(v.tensor_tensor(bet_sum[:, 0:1], bet[0][0:D, :], bet[1][0:D, :], ALU.add))
            link(v.tensor_tensor(bet_sum[:, 1:2], bet_sum[:, 0:1], bet[2][0:D, :], ALU.add))
            v.nop().then_inc(st["folded"], 1)
            dve.wait_ge(st["mm"], 1)
            link(v.tensor_copy(w_deg[:, :, :].rearrange("a s d -> a (s d)"), ps_misc[0:1, 0:P]))
            link(v.tensor_tensor(b0[2][:, :], b0[2][:, :], ps_misc[:, P:P + 1], ALU.add))
            dve.wait_ge(st["base_in"], 48)
            link(v.tensor_copy(dst_em[:, :], dst_em_i[:, :]))
            link(v.tensor_copy(base_i[:, :], base_row[:, :]))
            for h in range(2):
                link(v.tensor_tensor(
                    rel_em[:, :].rearrange("p (c j h) -> p c j h", j=J, h=2)[:, :, :, h],
                    dst_em[:, :].rearrange("p (c j h) -> p c j h", j=J, h=2)[:, :, :, h],
                    bc(base_all[:, :, h:h + 1], [P, NCH, J]), ALU.subtract))
            link(v.tensor_reduce(out=span_max[:, :], in_=span_row[:, :], axis=AX.X, op=ALU.max))
            link(v.tensor_scalar(flag[:, :], span_max[:, :], float(WIN), None, ALU.is_ge))
            dve.wait_ge(st["pool_iota"], 1)
            v.nop().then_inc(st["ready"], 1)
            v.nop().then_inc(st["flag_ready"], 1)
            general = dve.value_load(flag[0:1, 0:1], min_val=0, max_val=1)

            def node_norm(nd, b):
                dve.wait_ge(nd["sq"], nd["first"] + b + 1)
                v.tensor_reduce(out=varn[:, :], in_=sqn[:, :, :], axis=AX.X, op=ALU.add).then_inc(nd["var"], 1)
                dve.wait_ge(nd["rstd"], nd["first"] + b + 1)
                v.tensor_tensor(zn[:, :, :], ps_y[0][:, 0:J * D].rearrange("p (j d) -> p j d", d=D),
                                bc(rstdn[:, :].unsqueeze(2), [P, J, D]), ALU.mult).then_inc(nd["z"], 1)
                dve.wait_ge(nd["zt"], nd["first"] + b + 1)

            def tables(nd, b):
                dve.wait_ge(nd["evac"], nd["first"] + b + 1)
                v.tensor_copy(partn[:, :, 0, :], tabn[:, :, 1, :]).then_inc(nd["split"], 1)
                dve.wait_ge(nd["split"], 4 * b + 1)
                v.tensor_tensor(restn[:, :, :], tabn[:, :, 1, :], partn[:, :, 0, :], ALU.subtract).then_inc(nd["split"], 1)
                dve.wait_ge(nd["split"], 4 * b + 2)
                v.tensor_copy(partn[:, :, 1, :], restn[:, :, :]).then_inc(nd["split"], 1)
                dve.wait_ge(nd["split"], 4 * b + 3)
                v.tensor_tensor(restn[:, :, :], restn[:, :, :], partn[:, :, 1, :], ALU.subtract).then_inc(nd["split"], 1)
                dve.wait_ge(nd["split"], 4 * b + 4)
                v.tensor_copy(partn[:, :, 2, :], restn[:, :, :]).then_inc(nd["parts"], 1)
                dve.wait_ge(nd["stored"], 48 * b + 48)

            def new_nodes(nd, s, b):
                cols = n_fm[:, bass.ds(b * NBLK, NBLK)]
                v.tensor_copy(agg_blk[:, :, :], agg[:, :, bass.ds(b * NBLK, NBLK)])
                if s == 2:
                    v.tensor_copy(agg2_blk[:, :], agg2[:, bass.ds(b * NBLK, NBLK)])
                v.tensor_copy(n_blk[:, :], cols).then_inc(nd["block_in"], 1)
                node_norm(nd, b)
                v.scalar_tensor_tensor(out=cols, in0=ps_zt[0][0:D, :], scalar=ngam[s][:, :], in1=cols,
                                       op0=ALU.mult, op1=ALU.add).then_inc(nd["scaled"], 1)
                dve.wait_ge(nd["scaled"], b + 1)
                v.tensor_scalar(n_blk[:, :], cols, nbet[s][:, :], None, ALU.add)
                v.tensor_scalar(cols, cols, nbet[s][:, :], None, ALU.add).then_inc(nd["n"], 1)

            def layer_norm(nd, b, src, resid, dst):
                n = [0]

                def step(ins):
                    n[0] += 1
                    ins.then_inc(nd["own"], 1)
                    dve.wait_ge(nd["own"], STEPS * b + n[0])

                step(v.tensor_tensor(xs[:, :, :], src, resid, ALU.add))
                step(v.tensor_reduce(out=xm[:, :], in_=xs[:, :, :], axis=AX.X, op=ALU.add))
                step(v.tensor_scalar(xm[:, :], xm[:, :], 1.0 / D_NODE, None, ALU.mult))
                step(v.tensor_tensor(xc[:, :, :], xs[:, :, :], bc(xm[:, :].unsqueeze(2), [P, J, D_NODE]), ALU.subtract))
                step(v.tensor_tensor(xq[:, :, :], xc[:, :, :], xc[:, :, :], ALU.mult))
                step(v.tensor_reduce(out=varn[:, :], in_=xq[:, :, :], axis=AX.X, op=ALU.add))
                v.tensor_scalar(varn[:, :], varn[:, :], 1.0 / D_NODE, EPS, ALU.mult, ALU.add).then_inc(nd["lnv"], 1)
                dve.wait_ge(nd["lnr"], b + 1)
                return v.tensor_tensor(dst, xc[:, :, :], bc(rstdn[:, :].unsqueeze(2), [P, J, D_NODE]), ALU.mult)

            STEPS = 6

            def edge_phase(p, g):
                s = PH[p]
                rows = (P, D, D_NODE, D_NODE)[p]

                def one_hots(c, k, u):
                    if not g:
                        wait(dve, s["seg"], c - 1)
                        v.tensor_tensor(ohe_ring[u][:, :, :], bc(node_iota[:, 0:WIN].unsqueeze(1), [P, TILES, WIN]),
                                        bc(rel_em[:, bass.ds(c * TILES, TILES)].unsqueeze(2), [P, TILES, WIN]),
                                        ALU.is_equal).then_inc(s["ohe"], 1)
                    if not g and p < 2:
                        wait(dve, s["blk_pre"], c - 1)
                        dve.wait_ge(slot(s, "relb_in", u), 16 * k + 16)
                        v.tensor_scalar(ohf_ring[u][:, :], relb_ring[u][:, :], win_row[:, :], None,
                                        ALU.is_equal).then_inc(s["ohf"], 1)

                def variance(i, sq, rstd_free, done, c):
                    wait(dve, rstd_free, c)
                    dve.wait_ge(sq, c + 1)
                    v.tensor_reduce(out=var_buf[i][:, :], in_=sq_buf[i][:, :, :], axis=AX.X,
                                    op=ALU.add).then_inc(done, 1)

                def normalise(i, rstd, done, c, u):
                    if g:
                        wait(dve, s["seg"], (c - 1) * NSW)
                    else:
                        wait(dve, s["seg"], c - 1)
                    dve.wait_ge(rstd, c + 1)
                    v.tensor_tensor(z_ring[u][:, i, :, :], ps_y[i][:, :].rearrange("p (t d) -> p t d", d=D),
                                    bc(rstd_buf[i][:, :].unsqueeze(2), [P, TILES, D]), ALU.mult).then_inc(done, 1)

                def make_e1(c, k, u):
                    wait(dve, slot(s, "e1_out", u), 16 * k)
                    dve.wait_ge(s["blk_zt"], c + 1)
                    v.scalar_tensor_tensor(out=e1_ring[u][:, :], in0=ps_zt[1][:, :], scalar=gam[1][:, :],
                                           in1=e0_ring[u][:, :], op0=ALU.mult, op1=ALU.add).then_inc(s["blk_e1"], 1)

                def target(cols):
                    return agg[:, :, cols] if p == 0 else agg2[0:rows, cols]

                def add_up(c):
                    if g:
                        return add_sweep(c)
                    b_at = [dve.value_load(base_i[0:1, bass.ds(2 * c + h, 1)], min_val=0, max_val=N_NODES - 1)
                            for h in range(2)]
                    dve.wait_ge(s["seg"], c + 1)
                    for h in range(2):
                        src = ps_seg[0:rows, h * 2 * WIN:h * 2 * WIN + WIN]
                        if p == 0:
                            src = ps_seg[:, h * 2 * WIN:(h + 1) * 2 * WIN].rearrange("p (a w) -> p a w", a=2)
                        tgt = target(bass.ds(b_at[h], WIN))
                        wait(dve, s["added"], 2 * c + h)
                        v.tensor_tensor(tgt, tgt, src, ALU.add).then_inc(s["added"], 1)

                def add_sweep(c):
                    with dve.Fori(0, NSW) as w:
                        v.tensor_tensor(sweep_oh[:, :, :],
                                        bc(node_iota[:, bass.ds(w * SWEEP, SWEEP)].unsqueeze(1), [P, TILES, SWEEP]),
                                        bc(dst_em[:, bass.ds(c * TILES, TILES)].unsqueeze(2), [P, TILES, SWEEP]),
                                        ALU.is_equal).then_inc(s["swept_oh"], 1)
                        dve.wait_ge(s["seg"], c * NSW + w + 1)
                        src = ps_seg[0:rows, 0:SWEEP]
                        if p == 0:
                            src = ps_seg[:, :].rearrange("p (a w) -> p a w", a=2)
                        tgt = target(bass.ds(w * SWEEP, SWEEP))
                        v.tensor_tensor(tgt, tgt, src, ALU.add).then_inc(s["added"], 1)
                        dve.wait_ge(s["added"], c * NSW + w + 1)

                if p == 0:
                    variance(0, s["enc_sq"], s["enc_rstd"], s["enc_var"], 0)
                    normalise(0, s["enc_rstd"], s["enc_z"], 0, 0)

                def body(c, k, u, last):
                    enc = p == 0 and not last
                    one_hots(c, k, u)
                    if enc:
                        variance(0, s["enc_sq"], s["enc_rstd"], s["enc_var"], c + 1)
                    if p < 2:
                        variance(1, s["blk_sq"], s["blk_rstd"], s["blk_var"], c)
                    if enc:
                        normalise(0, s["enc_rstd"], s["enc_z"], c + 1, 1 - u)
                    if p < 2:
                        normalise(1, s["blk_rstd"], s["blk_z"], c, u)
                    if p == 0:
                        make_e1(c, k, u)
                    add_up(c)

                rounds(dve, body)
                dve.wait_ge(s["added"], NCH * NSW if g else 2 * NCH)

            def either(p):
                with dve.If(general):
                    edge_phase(p, 1)
                with dve.Else():
                    edge_phase(p, 0)
                v.nop().then_inc(edges_done[p], 1)

            nd = ND[0]
            with dve.Fori(0, NB) as b:
                v.tensor_copy(x_blk[:, :], x_fm[:, bass.ds(b * NBLK, NBLK)]).then_inc(nd["block_in"], 1)
                node_norm(nd, b)
                for dst in (n_blk[:, :], n_fm[:, bass.ds(b * NBLK, NBLK)]):
                    last = v.tensor_scalar(dst, ps_zt[0][0:D, :], ngam[0][:, :], nbet[0][:, :], ALU.mult, ALU.add)
                last.then_inc(nd["n"], 1)
                tables(nd, b)
            either(0)
            nd = ND[1]
            with dve.Fori(0, NB) as b:
                new_nodes(nd, 1, b)
                tables(nd, b)
            either(1)
            nd = ND[2]
            with dve.Fori(0, NB) as b:
                new_nodes(nd, 2, b)
                dve.wait_ge(nd["parts"], nd["first"] + b + 1)
                layer_norm(nd, b, ps_y[1][:, 0:J * D_NODE].rearrange("p (j d) -> p j d", d=D_NODE),
                           x_em[:, bass.ds(b, 1), :].rearrange("p a (j d) -> p (a j) d", d=D_NODE),
                           xs[:, :, :]).then_inc(nd["x1"], 1)
                dve.wait_ge(nd["x1"], b + 1)
                v.tensor_copy(x1_em[:, bass.ds(b, 1), :].rearrange("p a (j d) -> p (a j) d", d=D_NODE),
                              xs[:, :, :])
                dve.wait_ge(nd["x1t"], b + 1)
                v.tensor_copy(x_blk[:, :], ps_zt[1][0:D_NODE, :]).then_inc(nd["copied"], 1)
                dve.wait_ge(st["chain"], chain[0])
                dve.wait_ge(nd["copied"], b + 1)
                v.tensor_copy(x1_fm[:, bass.ds(b * NBLK, NBLK)], x_blk[:, :]).then_inc(nd["blk"], 1)
                dve.wait_ge(nd["stored"], 16 * b + 16)
            link(v.tensor_scalar(rdeg[:, :], agg[0:D_NODE, 1, :], 1.0, None, ALU.max))
            v.reciprocal(rdeg[:, :], rdeg[:, :])
            link(v.memset(agg2[:, :], 0.0))
            either(2)
            nd = ND[3]
            with dve.Fori(0, NB) as b:
                cols = bass.ds(b * NBLK, NBLK)
                v.tensor_copy(x_blk[:, :], x1_fm[:, cols])
                v.tensor_tensor(aggd[:, :], agg2[0:D_NODE, cols], rdeg[:, cols], ALU.mult).then_inc(nd["aggd"], 1)
                dve.wait_ge(nd["tab"], nd["first"] + b + 1)
                v.tensor_copy(t2n[:, :, :].rearrange("p j d -> p (j d)"), ps_y[0][:, 0:J * D_NODE]).then_inc(nd["x1"], 1)
                dve.wait_ge(nd["stored"], 16 * b + 16)
            link(v.memset(agg2[:, :], 0.0))
            either(3)
            nd = ND[4]
            with dve.Fori(0, NB) as b:
                cols = bass.ds(b * NBLK, NBLK)
                v.tensor_copy(h_blk[:, :], h_fm[:, cols])
                v.tensor_tensor(aggd[:, :], agg2[0:D_NODE, cols], rdeg[:, cols], ALU.mult).then_inc(nd["aggd"], 1)
                dve.wait_ge(nd["parts"], nd["first"] + b + 1)
                layer_norm(nd, b, ps_y[0][:, 0:J * D_NODE].rearrange("p (j d) -> p j d", d=D_NODE),
                           x1_em[:, bass.ds(b, 1), :].rearrange("p a (j d) -> p (a j) d", d=D_NODE),
                           outn[:, :, :]).then_inc(nd["x1"], 1)
                dve.wait_ge(s_final, 16 * b + 16)


IN = {
    "edge_enc_w0": "L0_gnn_edge_enc_w0", "edge_enc_b0": "L0_gnn_edge_enc_b0", "edge_enc_w1": "L0_gnn_edge_enc_w1",
    "edge_enc_b1": "L0_gnn_edge_enc_b1", "edge_enc_g": "L0_gnn_edge_enc_g", "edge_enc_beta": "L0_gnn_edge_enc_beta",
    "node_enc_w0": "L0_gnn_node_enc_w0", "node_enc_b0": "L0_gnn_node_enc_b0", "node_enc_w1": "L0_gnn_node_enc_w1",
    "node_enc_b1": "L0_gnn_node_enc_b1", "node_enc_g": "L0_gnn_node_enc_g", "node_enc_beta": "L0_gnn_node_enc_beta",
    "edge_blk_w0": "L0_gnn_edge_blk_w0", "edge_blk_b0": "L0_gnn_edge_blk_b0", "edge_blk_w1": "L0_gnn_edge_blk_w1",
    "edge_blk_b1": "L0_gnn_edge_blk_b1", "edge_blk_g": "L0_gnn_edge_blk_g", "edge_blk_beta": "L0_gnn_edge_blk_beta",
    "node_blk_w0": "L0_gnn_node_blk_w0", "node_blk_b0": "L0_gnn_node_blk_b0", "node_blk_w1": "L0_gnn_node_blk_w1",
    "node_blk_b1": "L0_gnn_node_blk_b1", "node_blk_g": "L0_gnn_node_blk_g", "node_blk_beta": "L0_gnn_node_blk_beta",
    "dec_w0": "L0_gnn_dec_w0", "dec_b0": "L0_gnn_dec_b0", "dec_w1": "L0_gnn_dec_w1", "dec_b1": "L0_gnn_dec_b1",
    "W1_l": "L1_gnn_W1_l", "sage_b1": "L1_gnn_b1", "W1_r": "L1_gnn_W1_r", "W2_l": "L1_gnn_W2_l",
    "sage_b2": "L1_gnn_b2", "W2_r": "L1_gnn_W2_r",
}


def kernel(**inputs):
    import numpy as np
    import concourse.bacc as bacc
    from concourse.bass_utils import run_bass_kernel_spmd

    a = {n: np.ascontiguousarray(inputs[full]) for n, full in IN.items()}
    x, src, dst = (np.asarray(inputs[n]) for n in ("x", "src", "dst"))
    attr = np.asarray(inputs["edge_attr_8"])
    E = NCH * CHUNK
    pad = E - N_EDGES
    far = np.full(pad, 1 << 20, dst.dtype)
    zero = np.zeros(pad, src.dtype)

    def edge_major(v):
        return np.ascontiguousarray(v.reshape(NCH, 2, J, P).transpose(0, 3, 2, 1).reshape(NCH, P, TILES))

    a["src_em"] = edge_major(np.concatenate([src, zero]))
    a["dst_idx"] = edge_major(np.concatenate([dst, zero]))
    a["dst_em"] = np.ascontiguousarray(edge_major(np.concatenate([dst, far])).transpose(1, 0, 2).reshape(P, -1))
    a["dst_rows"] = np.concatenate([dst, np.repeat(dst[-1:], pad)]).reshape(NCH, CHUNK)
    attr = np.concatenate([attr, np.zeros((pad, D_EDGE), attr.dtype)])
    a["attr_fm"] = np.ascontiguousarray(attr.reshape(NCH, 2, HALF, D_EDGE).transpose(0, 1, 3, 2)
                                        .reshape(NCH, 2 * D_EDGE, HALF))
    xp = np.concatenate([x, np.zeros((NPAD - N_NODES, D_NODE), x.dtype)])
    a["x_fm"] = np.ascontiguousarray(xp.T)
    a["x_em"] = np.ascontiguousarray(xp.reshape(NB, J, P, D_NODE).transpose(2, 0, 1, 3).reshape(P, NB, J * D_NODE))
    a["win_row"] = (np.arange(WROWS) // PARTS).astype(np.float32).reshape(WROWS, 1)

    nc = bacc.Bacc("TRN2", target_bir_lowering=False, num_devices=1)
    aps, arrays = {}, {}
    for n, v in a.items():
        arrays[f"in_{n}"] = v
        aps[n] = nc.dram_tensor(f"in_{n}", v.shape, mybir.dt.from_np(v.dtype), kind="ExternalInput").ap()
    out = nc.dram_tensor("out_nodes", (NPAD, D_NODE), mybir.dt.float32, kind="ExternalOutput").ap()
    build(nc, aps, out)
    r = run_bass_kernel_spmd(nc, [arrays], core_ids=[0])
    return r.results[0]["out_nodes"][:N_NODES]
```

```python
from contextlib import ExitStack

import concourse.bass as bass
from concourse import mybir
from concourse.alu_op_type import AluOpType as ALU

N_NODES = 3125
N_EDGES = 103125
D = 64
D_NODE, D_EDGE, D_SAGE = 16, 8, 32
EPS = 1e-5

P = 128
HALF = 512
CHUNK = 2 * HALF
TILES = CHUNK // P
J = HALF // P
NCH = -(-N_EDGES // CHUNK)
PARTS = 3
WIN = 38
WROWS = PARTS * WIN
WCOLS = 64
NBLK = 512
NB = -(-N_NODES // NBLK)
NPAD = NB * NBLK
SWEEP = 256
NSW = NPAD // SWEEP
HI = -(-N_NODES // P)
PAIRS = HI * WIN
HI0 = -(-HI // 2)
GROUP = TILES // 2
LOADS = 4
DEPTH = 2
NEWTON = 3
NSTEP = 2 + 3 * NEWTON

assert HI0 * WIN <= 512 and WROWS <= P
assert NCH % 2 == 1 and NCH >= 7


def build(nc, I, out):
    f32, bf16, f16, i32 = mybir.dt.float32, mybir.dt.bfloat16, mybir.dt.float16, mybir.dt.int32
    ACT = mybir.ActivationFunctionType
    AX = mybir.AxisListType
    ctx = ExitStack()
    with ctx:
        def sb(name, shape, dt=f32):
            return ctx.enter_context(nc.sbuf_tensor(name, shape, dt))

        def bank(name):
            return ctx.enter_context(nc.psum_tensor(name, [P, 512], f32))

        def sem(name):
            return ctx.enter_context(nc.semaphore(name))

        def sems(prefix, names):
            return {n: sem(f"{prefix}_{n}") for n in names.split()}

        def dram(name, shape, dt=f32):
            return nc.dram_tensor(name, shape, dt, kind="Internal").ap()

        def bc(ap, shape):
            return ap.to_broadcast(shape)

        send_tab = [dram(f"send_tab{s}", (NPAD, D)) for s in range(2)]
        recv_tab = [dram(f"recv_tab{s}", (NPAD, D)) for s in range(2)]
        recv_parts = [dram(f"recv_parts{s}", (NPAD * PARTS, D), bf16) for s in range(2)]
        sage_tab = [dram(f"sage_tab{s}", (NPAD, D_NODE)) for s in range(2)]
        e1_dram = dram("e1_dram", (NCH, P, HALF))
        rel_dram = dram("rel_dram", (NCH, CHUNK), bf16)
        pairs_dram = dram("pairs_dram", (NCH, P, PAIRS), f16)
        base_dram = dram("base_dram", (NCH, 2))
        span_dram = dram("span_dram", (NCH, 4))
        bias_dram = dram("bias_dram", (3, PARTS, D), bf16)

        ident = sb("ident", [P, P])
        ones = sb("ones", [P, P])
        ones_bf = sb("ones_bf", [P, P], bf16)
        node_iota = sb("node_iota", [P, NPAD])
        win_row = sb("win_row", [WROWS, 1])
        flag = sb("flag", [1, 1], i32)
        base_i = sb("base_i", [1, NCH * 2], i32)
        dst_em = sb("dst_em", [P, NCH * TILES])
        rel_em = sb("rel_em", [P, NCH * TILES])
        n_fm = sb("n_fm", [D, NPAD])
        agg = sb("agg", [P, 2, NPAD])
        agg2 = sb("agg2", [D, NPAD])
        x1_em = sb("x1_em", [P, NB, J * D_NODE])
        h_fm = sb("h_fm", [D_SAGE, NPAD])
        rdeg = n_fm[0:D_NODE, :]
        x1_fm = agg[0:D_NODE, 0, :]
        x_fm = h_fm[0:D_NODE, :]
        x_em = sb("x_em", [P, NB, J * D_NODE])
        t2_em = x_em

        enc_w0 = sb("enc_w0", [2 * D_EDGE, P])
        w_e = [sb(f"w_e{s}", [P, P]) for s in range(2)]
        w1 = [sb(f"w1_{s}", [P, D]) for s in range(3)]
        w1_bd = [sb(f"w1_bd{s}", [P, P]) for s in range(3)]
        b1 = [sb(f"b1_{s}", [1, D]) for s in range(3)]
        b0 = [sb(f"b0_{s}", [P, 1]) for s in range(3)]
        gam = [sb(f"gam{s}", [P, 1]) for s in range(3)]
        bet = [sb(f"bet{s}", [P, 1]) for s in range(3)]
        b1_part = [sb(f"b1_part{s}", [1, PARTS, D], bf16) for s in range(3)]
        b1_rest = [sb(f"b1_rest{s}", [1, D]) for s in range(3)]
        b1_rows = [sb(f"b1_rows{s}", [PARTS, TILES, D], bf16) for s in range(3)]
        row_mean = sb("row_mean", [P, 12])
        w_sr = [sb(f"w_sr{s}", [D, 2 * D]) for s in range(2)]
        nenc_w0 = sb("nenc_w0", [D_NODE, D])
        nb0 = [sb(f"nb0_{s}", [D, 1]) for s in range(3)]
        nw1 = [sb(f"nw1_{s}", [D, D]) for s in range(3)]
        nb1 = [sb(f"nb1_{s}", [1, D]) for s in range(3)]
        ngam = [sb(f"ngam{s}", [D, 1]) for s in range(3)]
        nbet = [sb(f"nbet{s}", [D, 1]) for s in range(3)]
        nb1_row = [sb(f"nb1_row{s}", [1, J, D]) for s in range(3)]
        w_n = [sb(f"w_n{s}", [D, D]) for s in range(2)]
        w_a = [sb(f"w_a{s}", [P, D]) for s in range(2)]
        w_ag = [sb(f"w_ag{s}", [P, D]) for s in range(2)]
        w_ag2 = sb("w_ag2", [D, D])
        gam_stack = sb("gam_stack", [P, 1])
        bet_sum = sb("bet_sum", [D, 2])
        w_deg = sb("w_deg", [1, 2, D])
        dec_w0 = sb("dec_w0", [D, D])
        dec_b0 = sb("dec_b0", [D, 1])
        dec_w1 = sb("dec_w1", [D, D_NODE])
        dec_b1 = sb("dec_b1", [1, J, D_NODE])
        s_w1l = sb("s_w1l", [D_NODE, D_SAGE])
        s_w1r = sb("s_w1r", [D_NODE, D_SAGE])
        s_b1 = sb("s_b1", [D_SAGE, 1])
        s_w2l = sb("s_w2l", [D_SAGE, D_NODE])
        s_w2r = sb("s_w2r", [D_SAGE, D_NODE])
        s_b2 = sb("s_b2", [1, J, D_NODE])

        idx_ring = [sb(f"idx_ring{u}", [P, TILES], i32) for u in range(DEPTH)]
        idxd_ring = [sb(f"idxd_ring{u}", [P, TILES], i32) for u in range(DEPTH)]
        edge_space = sb("edge_space", [P, 10, TILES * D])
        edge_slots = [edge_space[:, i, :].rearrange("p (t d) -> p t d", d=D) for i in range(10)]
        g_ring, gd_ring, z_enc, z_blk = edge_slots[0:2], edge_slots[2:4], edge_slots[4:8], edge_slots[8:10]
        gs_ring = [sb(f"gs_ring{u}", [P, TILES, D_NODE]) for u in range(DEPTH)]
        attr_ring = [sb(f"attr_ring{u}", [2 * D_EDGE, HALF]) for u in range(DEPTH)]
        relb_full = [sb(f"relb_ring{u}", [P, CHUNK], bf16) for u in range(DEPTH)]
        relb_ring = [r[0:WROWS, :] for r in relb_full]
        prw_ring = [sb(f"prw_ring{u}", [WROWS, 2, D], bf16) for u in range(DEPTH)]
        ohf_full = [sb(f"ohf_ring{u}", [P, CHUNK], bf16) for u in range(DEPTH)]
        ohf_ring = [r[0:WROWS, :] for r in ohf_full]
        ohe_ring = [sb(f"ohe_ring{u}", [P, TILES, WCOLS]) for u in range(DEPTH)]
        e0_ring = [sb(f"e0_ring{u}", [P, HALF]) for u in range(DEPTH)]
        e1_ring = [sb(f"e1_ring{u}", [P, HALF]) for u in range(DEPTH)]
        (idx_ring, idxd_ring, g_ring, gd_ring, gs_ring, attr_ring, relb_ring, prw_ring, ohf_ring, ohe_ring,
         z_blk, e0_ring, e1_ring) = (2 * ring for ring in (
             idx_ring, idxd_ring, g_ring, gd_ring, gs_ring, attr_ring, relb_ring, prw_ring, ohf_ring, ohe_ring,
             z_blk, e0_ring, e1_ring))
        sweep_oh = sb("sweep_oh", [P, TILES, SWEEP])
        h_buf_all = sb("h_buf", [P, 2, HALF])
        h_buf = [h_buf_all[:, i, :] for i in range(2)]
        sq_buf = [sb(f"sq_buf{i}", [P, TILES, D + 1]) for i in range(2)]
        var_buf = sb("var_buf", [P, 2, TILES])
        rstd_buf = sb("rstd_buf", [P, 2, TILES])
        newton_t = sb("newton_t", [P, 2 * TILES])
        newton_i = sb("newton_i", [P, 2 * TILES], i32)

        hn = sb("hn", [D, NBLK])
        x_blk = sb("x_blk", [D_NODE, NBLK])
        agg_blk = sb("agg_blk", [P, 2, NBLK])
        agg2_blk = sb("agg2_blk", [D, NBLK])
        n_blk = sb("n_blk", [D, NBLK])
        h_blk = sb("h_blk", [D_SAGE, NBLK])
        sqn = sb("sqn", [P, J, D + 1])
        varn = sb("varn", [P, J])
        rstdn = sb("rstdn", [P, J])
        zn = sb("zn", [P, J, D])
        tabn = sb("tabn", [P, J, 2, D])
        partn = sb("partn", [P, J, PARTS, D], bf16)
        restn = sb("restn", [P, J, D])
        xs = sb("xs", [P, J, D_NODE])
        xc = sb("xc", [P, J, D_NODE])
        xq = sb("xq", [P, J, D_NODE])
        xm = sb("xm", [P, J])
        t2n = sb("t2n", [P, J, D_NODE])
        aggd = sb("aggd", [D_NODE, NBLK])
        outn = sb("outn", [P, J, D_NODE])

        words = edge_space[:, :, :].rearrange("p a w -> p (a w)")
        at = GROUP * PAIRS // 2
        pair_oh = [words[:, q * at:(q + 1) * at].bitcast(bf16).rearrange("p (t k) -> p t k", t=GROUP)
                   for q in range(2)]
        pairs_in = [words[:, i * PAIRS // 2:(i + 1) * PAIRS // 2].bitcast(f16) for i in range(LOADS)]
        pairs_out = [words[:, 2 * at + q * PAIRS // 2:2 * at + (q + 1) * PAIRS // 2].bitcast(f16) for q in range(2)]
        counts = [sweep_oh[:, :, :].rearrange("p t w -> p (t w)")[:, q * PAIRS:(q + 1) * PAIRS] for q in range(2)]
        lo_oh = [relb_full[q][:, :].rearrange("p (t l) -> p t l", t=TILES) for q in range(2)]
        pair_iota = ohf_full[0][:, 0:PAIRS].bitcast(f16)
        now_key = [sb(f"now_key{q}", [P, TILES]) for q in range(2)]
        src_all = agg_blk[:, :, :].rearrange("p a n -> p (a n)")[:, 0:NCH * TILES].bitcast(i32)
        src_bits = h_buf_all[:, :, :].rearrange("p a n -> p (a n)")[:, 0:NCH * TILES].bitcast(i32)
        lo_em, key_em = dst_em, rel_em

        spare = sweep_oh[0:NCH, :, :].rearrange("c t w -> c (t w)")
        dst_rows = spare[:, 0:CHUNK].rearrange("c (h e) -> c h e", h=2)
        dst_rows_i = spare[:, CHUNK:2 * CHUNK].bitcast(i32)
        rel_rows = sb("rel_rows", [NCH, 2, HALF], bf16)
        dst_em_i = agg_blk[:, :, :].rearrange("p a n -> p (a n)")[:, 0:NCH * TILES].bitcast(i32)
        base_f = sb("base_f", [NCH, 2])
        top_f = sb("top_f", [NCH, 2])
        span_f = sb("span_f", [NCH, 4])
        span_row = sb("span_row", [1, NCH * 4])
        span_max = sb("span_max", [1, 1])
        base_row = sb("base_row", [1, NCH * 2])
        base_all = sb("base_all", [P, NCH, 2])

        ps_pre = [bank("ps_pre0"), bank("ps_pre1")]
        ps_y = [bank("ps_y0"), bank("ps_y1")]
        ps_zt = [bank("ps_zt0"), bank("ps_zt1")]
        ps_seg = bank("ps_seg")
        ps_misc = bank("ps_misc")

        st = sems("st", "loads consts ident chain rel_ready base_out base_in em_ready biases biasrow_in "
                        "mm folded flag_ready sent pool_iota ready rows_out")
        names = ("attr_in0 attr_in1 idx_in0 idx_in1 idxd_in0 idxd_in1 relb_in0 relb_in1 prw_in0 prw_in1 "
                 "gathered0 gathered1 gathered_d0 gathered_d1 e1_out0 e1_out1 "
                 "enc_pre enc_h enc_y enc_sq enc_var enc_z enc_zt enc_e newton "
                 "ohf ohe rows_in blk_pre blk_h blk_y blk_sq blk_var blk_z blk_zt blk_e1 seg added swept_oh")
        short = "idx_in0 idx_in1 gathered0 gathered1 seg added swept_oh widened "
        bnames = "e1_in0 e1_in1 " + " ".join(n for n in names.split()
                                             if not n.startswith(("attr", "enc", "e1_out", "blk_zt", "blk_e1")))
        PH = [sems(f"p{p}", (names, bnames, short + "src_in keyed now lo pair_oh paired halved out0 out1",
                               short + "in0 in1 in2 in3")[p]) for p in range(4)]
        edges_done = [sem(f"edges_done{p}") for p in range(4)]
        mlp = sems("mlp", "block_in pre h y sq var newton z zt n tab evac parts")
        ND = [{**(mlp if i < 3 else {}), "first": NB * i if i < 3 else 0, **sems(f"n{i}", own)}
              for i, own in enumerate(("split stored", "scaled split stored", "scaled copied blk newton2 own x1 x1t stored",
                                       "aggd pre h tab x1 stored", "aggd parts newton2 own x1"))]
        s_final = sem("s_final")

        block = ctx.enter_context(nc.Block())

        def slot(s, name, u):
            return s[f"{name}{u % DEPTH}"]

        def wait(eng, s, v):
            if not (isinstance(v, int) and v <= 0):
                eng.wait_ge(s, v)

        def value(eng, v):
            return v if isinstance(v, int) else eng.to_reg(v)

        W_LOADS = []

        def load(dst, src):
            W_LOADS.append((dst, src))

        def col(name, s=None):
            a = I[name] if s is None else I[name][s]
            return a.rearrange("(a b) -> a b", b=1)

        def row(name, s=None):
            a = I[name] if s is None else I[name][s]
            return a.rearrange("(a b) -> a b", a=1)

        for h in range(2):
            load(enc_w0[h * D_EDGE:(h + 1) * D_EDGE, h * D:(h + 1) * D], I["edge_enc_w0"])
            for s in range(2):
                load(w_e[s][h * D:(h + 1) * D, h * D:(h + 1) * D], I["edge_blk_w0"][s, 0:D, :])
                load(w1[1 + s][h * D:(h + 1) * D, :], I["edge_blk_w1"][s])
                load(b0[1 + s][h * D:(h + 1) * D, :], col("edge_blk_b0", s))
                load(gam[1 + s][h * D:(h + 1) * D, :], col("edge_blk_g", s))
                load(bet[1 + s][h * D:(h + 1) * D, :], col("edge_blk_beta", s))
                load(w_a[s][h * D:(h + 1) * D, :], I["node_blk_w0"][s, D:2 * D, :])
                load(w_sr[s][:, h * D:(h + 1) * D], I["edge_blk_w0"][s, (1 + h) * D:(2 + h) * D, :])
            load(w1[0][h * D:(h + 1) * D, :], I["edge_enc_w1"])
            load(b0[0][h * D:(h + 1) * D, :], col("edge_enc_b0"))
            load(gam[0][h * D:(h + 1) * D, :], col("edge_enc_g"))
            load(bet[0][h * D:(h + 1) * D, :], col("edge_enc_beta"))
        load(gam_stack[0:D, :], col("edge_enc_g"))
        load(gam_stack[D:P, :], col("edge_blk_g", 0))
        load(b1[0][:, :], row("edge_enc_b1"))
        for s in range(2):
            load(b1[1 + s][:, :], row("edge_blk_b1", s))
            load(w_n[s][:, :], I["node_blk_w0"][s, 0:D, :])
            load(nb0[1 + s][:, :], col("node_blk_b0", s))
            load(nw1[1 + s][:, :], I["node_blk_w1"][s])
            load(nb1[1 + s][:, :], row("node_blk_b1", s))
            load(ngam[1 + s][:, :], col("node_blk_g", s))
            load(nbet[1 + s][:, :], col("node_blk_beta", s))
        load(nenc_w0[:, :], I["node_enc_w0"])
        load(nb0[0][:, :], col("node_enc_b0"))
        load(nw1[0][:, :], I["node_enc_w1"])
        load(nb1[0][:, :], row("node_enc_b1"))
        load(ngam[0][:, :], col("node_enc_g"))
        load(nbet[0][:, :], col("node_enc_beta"))
        load(dec_w0[:, :], I["dec_w0"])
        load(dec_b0[:, :], col("dec_b0"))
        load(dec_w1[:, :], I["dec_w1"])
        load(s_w1l[:, :], I["W1_l"])
        load(s_w1r[:, :], I["W1_r"])
        load(s_b1[:, :], col("sage_b1"))
        load(s_w2l[:, :], I["W2_l"])
        load(s_w2r[:, :], I["W2_r"])
        for j in range(J):
            load(dec_b1[:, j, :], row("dec_b1"))
            load(s_b2[:, j, :], row("sage_b2"))
        load(x_fm[:, :], I["x_fm"])
        load(x_em[:, :, :], I["x_em"])
        load(win_row[:, :], I["win_row"])
        LOADED = 16 * (len(W_LOADS) + 2)

        def rounds(eng, back, ahead, body, unroll=None):
            unroll = unroll or (4 if back else 2)
            for c in range(-ahead, unroll):
                body(c, c // 2, c % 4)
            top = (NCH - ahead) // unroll
            with eng.Fori(1, top) as k:
                for u in range(unroll):
                    body(unroll * k + u, unroll // 2 * k + u // 2, u)
            for c in range(unroll * top, NCH + back):
                body(c, c // 2, c % 4)

        def chunk(c, k, u, d):
            if isinstance(c, int) and not 0 <= c + d < NCH:
                return None
            return c + d, k + (u % 2 + d) // 2, (u + d) % 4

        def counts_in(s, c, u):
            return s[f"in{u}"], 4 * (c - u) + 16

        BANKS = [(0, HI0 * WIN), (HI0 * WIN, PAIRS)]

        def pair_bank(q, bk):
            return (ps_pre, ps_y)[q][bk]

        @block.sync
        def _(sp):
            sp.dma_start(dst_rows_i[:, :], I["dst_rows"]).then_inc(st["loads"], 16)
            sp.dma_start(dst_em_i, I["dst_em"]).then_inc(st["loads"], 16)
            sp.wait_ge(st["consts"], 1)
            for dst, src in W_LOADS:
                sp.dma_start(dst, src).then_inc(st["loads"], 16)
            sp.wait_ge(st["rel_ready"], 1)
            sp.dma_start(rel_dram, rel_rows[:, :, :].rearrange("c h e -> c (h e)")).then_inc(st["rows_out"], 16)
            sp.dma_start(base_dram, base_f[:, :]).then_inc(st["base_out"], 16)
            sp.dma_start(span_dram, span_f[:, :]).then_inc(st["base_out"], 16)
            sp.wait_ge(st["base_out"], 32)
            sp.dma_start(base_row[:, :], base_dram.rearrange("(a c) h -> a (c h)", a=1)).then_inc(st["base_in"], 16)
            sp.dma_start(span_row[:, :], span_dram.rearrange("(a c) h -> a (c h)", a=1)).then_inc(st["base_in"], 16)
            sp.dma_start(base_all[:, :, :].rearrange("p c h -> p (c h)"),
                         base_dram.rearrange("(a c) h -> a (c h)", a=1).to_broadcast([P, NCH * 2])
                         ).then_inc(st["base_in"], 16)
            sp.wait_ge(st["biases"], 1)
            for s in range(3):
                sp.dma_start(bias_dram[s:s + 1], b1_part[s][:, :, :]).then_inc(st["sent"], 16)
            sp.wait_ge(st["sent"], 48)
            for s in range(3):
                for t in range(TILES):
                    sp.dma_start(b1_rows[s][:, t, :], bias_dram[s]).then_inc(st["biasrow_in"], 16)
            sp.wait_ge(st["rows_out"], 16)
            sp.wait_ge(st["flag_ready"], 1)
            general = sp.value_load(flag[0:1, 0:1], min_val=0, max_val=1)

            def store_tables(s):
                nd = ND[s]
                with sp.Fori(0, NB) as b:
                    sp.wait_ge(nd["parts"], nd["first"] + b + 1)
                    sp.dma_start(send_tab[s].rearrange("(b j p) d -> b p j d", j=J, p=P)[bass.ds(b, 1)]
                                 .rearrange("a p j d -> (a p) j d"), tabn[:, :, 0, :]).then_inc(nd["stored"], 16)
                    sp.dma_start(recv_tab[s].rearrange("(b j p) d -> b p j d", j=J, p=P)[bass.ds(b, 1)]
                                 .rearrange("a p j d -> (a p) j d"), tabn[:, :, 1, :]).then_inc(nd["stored"], 16)
                    sp.dma_start(recv_parts[s].rearrange("(b j p t) d -> b p j (t d)", j=J, p=P, t=PARTS)[bass.ds(b, 1)]
                                 .rearrange("a p j d -> (a p) j d"),
                                 partn[:, :, :, :].rearrange("p j t d -> p j (t d)")).then_inc(nd["stored"], 16)

            def store_sage(s, nd, src):
                with sp.Fori(0, NB) as b:
                    sp.wait_ge(nd["x1"], b + 1)
                    sp.dma_start(sage_tab[s].rearrange("(b j p) d -> b p j d", j=J, p=P)[bass.ds(b, 1)]
                                 .rearrange("a p j d -> (a p) j d"), src).then_inc(nd["stored"], 16)

            def edge_phase(p, g):
                s = PH[p]
                tab = p

                def windows(c, k, u):
                    h0 = sp.value_load(base_i[0:1, bass.ds(2 * c, 1)], min_val=0, max_val=N_NODES - 1)
                    h1 = sp.value_load(base_i[0:1, bass.ds(2 * c + 1, 1)], min_val=0, max_val=N_NODES - 1)
                    sp.wait_ge(st["ready"], 1)
                    wait(sp, s["ohf"], value(sp, c - 1))
                    sp.dma_start(relb_ring[u][:, :], rel_dram[bass.ds(c, 1)].to_broadcast([WROWS, CHUNK])
                                 ).then_inc(slot(s, "relb_in", u), 16)
                    wait(sp, s["rows_in"], c - 1)
                    for h, v in enumerate((h0, h1)):
                        sp.dma_start(prw_ring[u][:, h, :], recv_parts[tab][bass.ds(v * PARTS, WROWS)]
                                     ).then_inc(slot(s, "prw_in", u), 16)

                def indices(c, k, u):
                    wait(sp, slot(s, "gathered", u), 128 * k)
                    sp.dma_start(idx_ring[u][:, :], I["src_em"][bass.ds(c, 1)].rearrange("a p t -> (a p) t")
                                 ).then_inc(slot(s, "idx_in", u), 16)
                    if g and p < 2:
                        wait(sp, slot(s, "gathered_d", u), 128 * k)
                        sp.dma_start(idxd_ring[u][:, :], I["dst_idx"][bass.ds(c, 1)].rearrange("a p t -> (a p) t")
                                     ).then_inc(slot(s, "idxd_in", u), 16)

                def attrs(c, k, u):
                    wait(sp, s["enc_pre"], c - 1)
                    sp.dma_start(attr_ring[u][:, :], I["attr_fm"][bass.ds(c, 1)].rearrange("a p t -> (a p) t")
                                 ).then_inc(slot(s, "attr_in", u), 16)

                def load_e1(c, k, u):
                    wait(sp, s["blk_pre"], c - 1)
                    sp.dma_start(e1_ring[u][:, :], e1_dram[bass.ds(c, 1)].rearrange("a p t -> (a p) t")
                                 ).then_inc(slot(s, "e1_in", u), 16)

                def store_e1(c, k, u):
                    sp.wait_ge(s["blk_e1"], c + 1)
                    sp.dma_start(e1_dram[bass.ds(c, 1)].rearrange("a p t -> (a p) t"), e1_ring[u][:, :]
                                 ).then_inc(slot(s, "e1_out", u), 16)

                def body(c, k, u):
                    if ahead := chunk(c, k, u, 2):
                        indices(*ahead)
                        if p == 0:
                            attrs(*ahead)
                        if p == 1:
                            load_e1(*ahead)
                        if p < 2 and not g:
                            windows(*ahead)
                    if p == 0 and (done := chunk(c, k, u, -2)):
                        store_e1(*done)

                rounds(sp, 1 if p == 0 else 0, 2, body)
                if p == 0:
                    store_e1(NCH - 1, NCH // 2, 0)
                    sp.wait_ge(s["e1_out0"], 16 * (NCH // 2 + 1))
                    sp.wait_ge(s["e1_out1"], 16 * (NCH // 2))

            def store_pairs():
                s = PH[2]
                sp.dma_start(src_all, I["src_all"]).then_inc(s["src_in"], 16)

                def body(c, k, u):
                    sp.wait_ge(s["halved"], c + 1)
                    sp.dma_start(pairs_dram[bass.ds(c, 1)].rearrange("a p t -> (a p) t"), pairs_out[u % 2]
                                 ).then_inc(s[f"out{u % 2}"], 16)

                rounds(sp, 0, 0, body)
                sp.wait_ge(s["out0"], 16 * (NCH // 2 + 1))
                sp.wait_ge(s["out1"], 16 * (NCH // 2))

            def load_pairs():
                s = PH[3]

                def body(c, k, u):
                    if n := chunk(c, k, u, LOADS - 1):
                        wait(sp, s["widened"], value(sp, c))
                        sem_in, _ = counts_in(s, n[0], n[2])
                        sp.dma_start(pairs_in[n[2]], pairs_dram[bass.ds(n[0], 1)].rearrange("a p t -> (a p) t")
                                     ).then_inc(sem_in, 16)

                rounds(sp, 0, LOADS - 1, body, LOADS)

            def either(p):
                with sp.If(general):
                    edge_phase(p, 1)
                with sp.Else():
                    if p < 2:
                        edge_phase(p, 0)
                    elif p == 2:
                        store_pairs()
                    else:
                        load_pairs()
                sp.nop()

            store_tables(0)
            either(0)
            store_tables(1)
            either(1)
            store_sage(0, ND[2], xs[:, :, :])
            either(2)
            store_sage(1, ND[3], t2n[:, :, :])
            either(3)
            with sp.Fori(0, NB) as b:
                sp.wait_ge(ND[4]["x1"], b + 1)
                sp.dma_start(out.rearrange("(b j p) d -> b p j d", j=J, p=P)[bass.ds(b, 1)]
                             .rearrange("a p j d -> (a p) j d"), outn[:, :, :]).then_inc(s_final, 16)
            sp.wait_ge(s_final, 16 * NB)

        @block.gpsimd
        def _(pool):
            nc.gpsimd.memset(ident[:, :], 0.0).then_inc(st["ident"], 1)
            pool.wait_ge(st["ident"], 1)
            nc.gpsimd.affine_select(out=ident[:, :], in_=ident[:, :], compare_op=ALU.not_equal, fill=1.0,
                                    base=0, pattern=[[-1, P]], channel_multiplier=1).then_inc(st["ident"], 1)
            nc.gpsimd.iota(node_iota[:, :], pattern=[[1, NPAD]], base=0, channel_multiplier=0,
                           allow_small_or_imprecise_dtypes=True).then_inc(st["pool_iota"], 1)
            pool.wait_ge(st["flag_ready"], 1)
            general = pool.value_load(flag[0:1, 0:1], min_val=0, max_val=1)

            def edge_phase(p, g):
                s = PH[p]
                tab = (send_tab + sage_tab)[p]
                ring = g_ring if p < 2 else gs_ring
                used = s["rows_in"] if p < 2 else s["seg"]
                per = NSW if g and p >= 2 else 1
                stored = ND[p]["stored"]
                stored_n = 16 * NB * (PARTS if p < 2 else 1)

                def gather(c, k, u):
                    n_idx, n_used = value(pool, 16 * k + 16), value(pool, (c - 1) * per)
                    pool.wait_ge(stored, stored_n)
                    pool.wait_ge(slot(s, "idx_in", u), n_idx)
                    wait(pool, used, n_used)
                    for t in range(TILES):
                        nc.gpsimd.indirect_dma_start(
                            out=ring[u][:, t, :], out_offset=None, in_=tab,
                            in_offset=bass.IndirectOffsetOnAxis(ap=idx_ring[u][:, t:t + 1], axis=0),
                        ).then_inc(slot(s, "gathered", u), 16)
                    if g and p < 2:
                        pool.wait_ge(stored, stored_n)
                        pool.wait_ge(slot(s, "idxd_in", u), n_idx)
                        for t in range(TILES):
                            nc.gpsimd.indirect_dma_start(
                                out=gd_ring[u][:, t, :], out_offset=None, in_=recv_tab[p],
                                in_offset=bass.IndirectOffsetOnAxis(ap=idxd_ring[u][:, t:t + 1], axis=0),
                            ).then_inc(slot(s, "gathered_d", u), 16)

                rounds(pool, 0, 0, gather)

            def either(p):
                with pool.If(general):
                    edge_phase(p, 1)
                with pool.Else():
                    if p < 2:
                        edge_phase(p, 0)
                pool.nop()

            for p in range(4):
                either(p)

        @block.scalar
        def _(act):
            act.wait_ge(st["flag_ready"], 1)
            general = act.value_load(flag[0:1, 0:1], min_val=0, max_val=1)
            act.wait_ge(st["ready"], 1)

            def node_mlp(nd, bias, b):
                act.wait_ge(nd["pre"], nd["first"] + b + 1)
                nc.scalar.activation(hn[:, :], ps_pre[0][0:D, :], ACT.Silu, bias=bias).then_inc(nd["h"], 1)
                act.wait_ge(nd["y"], nd["first"] + b + 1)
                nc.scalar.activation(sqn[:, :, 0:D], ps_y[0][:, 0:J * D].rearrange("p (j d) -> p j d", d=D),
                                     ACT.Square, scale=D ** -0.5).then_inc(nd["sq"], 1)

            def tables(nd, b):
                act.wait_ge(nd["tab"], nd["first"] + b + 1)
                nc.scalar.activation(tabn[:, :, :, :], ps_zt[1][:, :].rearrange("p (j s d) -> p j s d", s=2, d=D),
                                     ACT.Copy).then_inc(nd["evac"], 1)

            def edge_phase(p, g):
                s = PH[p]

                def silu(i, pre, h, hfree, bias, c):
                    wait(act, hfree, c)
                    act.wait_ge(pre, c + 1)
                    nc.scalar.activation(h_buf[i], ps_pre[i][:, :], ACT.Silu, bias=bias).then_inc(h, 1)

                def square(i, y, sq, free, c):
                    wait(act, free, c)
                    act.wait_ge(y, c + 1)
                    nc.scalar.activation(sq_buf[i][:, :, 0:D], ps_y[i][:, :].rearrange("p (t d) -> p t d", d=D),
                                         ACT.Square, scale=D ** -0.5).then_inc(sq, 1)

                def to_e0(c, k, u):
                    wait(act, s["blk_e1"], c - 1)
                    act.wait_ge(s["enc_zt"], c + 1)
                    nc.scalar.activation(e0_ring[u][:, :], ps_zt[0][:, :], ACT.Identity,
                                         bias=bet[0][:, :], scale=gam[0][:, :]).then_inc(s["enc_e"], 1)

                def body(c, k, u):
                    enc = chunk(c, k, u, 2) if p == 0 else None
                    nxt = chunk(c, k, u, 1)
                    now = chunk(c, k, u, 0)
                    if p == 0:
                        if enc:
                            silu(0, s["enc_pre"], s["enc_h"], s["enc_y"], b0[0][:, :], enc[0])
                        if now:
                            square(1, s["blk_y"], s["blk_sq"], s["blk_var"], c)
                        if enc:
                            square(0, s["enc_y"], s["enc_sq"], s["enc_var"], enc[0])
                        if nxt:
                            to_e0(*nxt)
                            silu(1, s["blk_pre"], s["blk_h"], s["blk_y"], b0[1][:, :], nxt[0])
                    elif nxt:
                        silu(1, s["blk_pre"], s["blk_h"], s["blk_y"], b0[2][:, :], nxt[0])
                        square(1, s["blk_y"], s["blk_sq"], s["blk_var"], nxt[0])

                if p < 2:
                    rounds(act, 1 - p, 2 - p, body)

            def keep_pairs(c, k, u):
                s, q = PH[2], u % 2
                wait(act, s["seg"], value(act, c - 1))
                act.wait_ge(s["paired"], 2 * c + 2)
                for bk, (lo, hi) in enumerate(BANKS):
                    last = nc.scalar.activation(counts[q][:, lo:hi], pair_bank(q, bk)[:, 0:hi - lo], ACT.Copy)
                last.then_inc(s["widened"], 1)
                wait(act, s[f"out{q}"], 16 * k)
                act.wait_ge(s["widened"], c + 1)
                nc.scalar.activation(pairs_out[q], counts[q], ACT.Copy).then_inc(s["halved"], 1)

            def widen_pairs(c, k, u):
                s = PH[3]
                wait(act, s["seg"], value(act, c - 1))
                act.wait_ge(*counts_in(s, c, u))
                nc.scalar.activation(counts[u % 2], pairs_in[u], ACT.Copy).then_inc(s["widened"], 1)

            def either(p):
                with act.If(general):
                    edge_phase(p, 1)
                with act.Else():
                    if p == 2:
                        rounds(act, 0, 0, keep_pairs)
                    elif p == 3:
                        rounds(act, 0, 0, widen_pairs, LOADS)
                    else:
                        edge_phase(p, 0)
                act.nop()

            for s in range(2):
                with act.Fori(0, NB) as b:
                    node_mlp(ND[s], nb0[s][:, :], b)
                    tables(ND[s], b)
                either(s)
            nd = ND[2]
            with act.Fori(0, NB) as b:
                node_mlp(nd, nb0[2][:, :], b)
                act.wait_ge(nd["tab"], nd["first"] + b + 1)
                nc.scalar.activation(hn[:, :], ps_pre[1][0:D, :], ACT.Silu, bias=dec_b0[:, :]).then_inc(nd["evac"], 1)
            either(2)
            nd = ND[3]
            with act.Fori(0, NB) as b:
                act.wait_ge(nd["pre"], nd["first"] + b + 1)
                for dst in (h_blk[:, :], h_fm[:, bass.ds(b * NBLK, NBLK)]):
                    last = nc.scalar.activation(dst, ps_pre[0][0:D_SAGE, :], ACT.Relu, bias=s_b1[:, :])
                last.then_inc(nd["h"], 1)
            either(3)

        @block.tensor
        def _(pe):
            mm = nc.tensor.matmul
            pe.wait_ge(st["ident"], 2)
            pe.wait_ge(st["folded"], 1)
            for s in range(2):
                mm(ps_misc[0:1, s * D:(s + 1) * D], bet_sum[:, s:s + 1], w_a[s][0:D, :], start=True, stop=True)
            mm(ps_misc[:, P:P + 1], w_e[1][:, :], bet[1][:, :], start=True, stop=True).then_inc(st["mm"], 1)
            pe.wait_ge(st["flag_ready"], 1)
            general = pe.value_load(flag[0:1, 0:1], min_val=0, max_val=1)
            pe.wait_ge(st["biasrow_in"], 16 * 3 * TILES)
            pe.wait_ge(st["ready"], 1)

            def node_tail(nd, s, b):
                pe.wait_ge(nd["h"], nd["first"] + b + 1)
                mm(ps_y[0][:, 0:J * D], ones[0:1, :], nb1_row[s][:, :, :].rearrange("a j d -> a (j d)"),
                   start=True, stop=False)
                for j in range(J):
                    last = mm(ps_y[0][:, j * D:(j + 1) * D], hn[:, j * P:(j + 1) * P], nw1[s][:, :],
                              start=False, stop=j == J - 1)
                last.then_inc(nd["y"], 1)
                pe.wait_ge(st["ready"], 1)
                pe.wait_ge(nd["z"], nd["first"] + b + 1)
                for j in range(J):
                    last = nc.tensor.transpose(ps_zt[0][0:D, j * P:(j + 1) * P], zn[:, j, :], ident[:, :])
                last.then_inc(nd["zt"], 1)

            def tables(nd, s, b):
                pe.wait_ge(nd["n"], nd["first"] + b + 1)
                for j in range(J):
                    last = mm(ps_zt[1][:, j * 2 * D:(j + 1) * 2 * D], n_blk[:, j * P:(j + 1) * P],
                              w_sr[s][:, :], start=True, stop=True)
                last.then_inc(nd["tab"], 1)

            def node_update(nd, s, b):
                n_in = value(pe, nd["first"] + b + 1)
                pe.wait_ge(st["ready"], 1)
                pe.wait_ge(nd["block_in"], n_in)
                mm(ps_pre[0][0:D, :], w_n[s][:, :], n_blk[:, :], start=True, stop=False)
                mm(ps_pre[0][0:D, :], w_ag[s][:, :], agg_blk[:, 0, :], start=False, stop=False)
                if s == 1:
                    mm(ps_pre[0][0:D, :], w_ag2[:, :], agg2_blk[:, :], start=False, stop=False)
                mm(ps_pre[0][0:D, :], w_deg[:, s, :], agg_blk[0:1, 1, :], start=False, stop=True).then_inc(nd["pre"], 1)

            def edge_phase(p, g):
                s = PH[p]
                def enc_pre(c, k, u):
                    wait(pe, s["enc_h"], c)
                    pe.wait_ge(slot(s, "attr_in", u), 16 * k + 16)
                    mm(ps_pre[0][:, :], enc_w0[:, :], attr_ring[u][:, :], start=True, stop=True).then_inc(s["enc_pre"], 1)

                def second(i, h, z, done, c):
                    wait(pe, z, c)
                    pe.wait_ge(h, c + 1)
                    w = 0 if i == 0 else 1 + p
                    mm(ps_y[i][:, :], ones_bf[0:PARTS, :], b1_rows[w][:, :, :].rearrange("a t d -> a (t d)"),
                       start=True, stop=False)
                    for j in range(J):
                        last = mm(ps_y[i][:, j * P:(j + 1) * P], h_buf[i][:, j * P:(j + 1) * P], w1_bd[w][:, :],
                                  start=False, stop=j == J - 1)
                    last.then_inc(done, 1)

                def back(i, z, free, done, c, z_tile):
                    wait(pe, free, c)
                    pe.wait_ge(z, c + 1)
                    for j in range(J):
                        last = nc.tensor.transpose(
                            ps_zt[i][:, j * P:(j + 1) * P],
                            z_tile[:, 2 * j:2 * j + 2, :].rearrange("p t d -> p (t d)"), ident[:, :])
                    last.then_inc(done, 1)

                def gathered_rows(c, k, u):
                    wait(pe, s["blk_h"], c)
                    pe.wait_ge(slot(s, "gathered", u), 128 * k + 128)
                    if g:
                        pe.wait_ge(slot(s, "gathered_d", u), 128 * k + 128)
                    for ring in ([g_ring, gd_ring] if g else [g_ring]):
                        for j in range(J):
                            last = mm(ps_pre[1][:, j * P:(j + 1) * P],
                                      ring[u][:, 2 * j:2 * j + 2, :].rearrange("p t d -> p (t d)"), ident[:, :],
                                      is_transpose=ring is g_ring, start=ring is g_ring and j == 0, stop=False)
                    if not g:
                        pe.wait_ge(slot(s, "prw_in", u), 32 * k + 32)
                        pe.wait_ge(s["ohf"], c + 1)
                        for hf in range(2):
                            last = mm(ps_pre[1][hf * D:(hf + 1) * D, :], prw_ring[u][:, hf, :],
                                      ohf_ring[u][:, hf * HALF:(hf + 1) * HALF], start=False, stop=False)
                    last.then_inc(s["rows_in"], 1)

                def edge_rows(c, k, u):
                    if p == 0:
                        pe.wait_ge(s["enc_e"], c + 1)
                        e = e0_ring[u]
                    else:
                        pe.wait_ge(slot(s, "e1_in", u), 16 * k + 16)
                        e = e1_ring[u]
                    mm(ps_pre[1][:, :], w_e[p][:, :], e[:, :], start=False, stop=True).then_inc(s["blk_pre"], 1)

                def summed(u, t):
                    if p == 0:
                        return [(0, z_enc[u][:, t, :]), (D, z_blk[u][:, t, :])]
                    return [(0, z_blk[u][:, t, :] if p == 1 else gs_ring[u][:, t, :])]

                rows = D if p < 2 else D_NODE

                def seg(c, k, u):
                    if g:
                        return seg_sweep(c, k, u)
                    wait(pe, s["added"], 2 * c)
                    if p < 2:
                        pe.wait_ge(s["blk_z"], c + 1)
                    else:
                        pe.wait_ge(slot(s, "gathered", u), 128 * k + 128)
                    pe.wait_ge(s["ohe"], c + 1)
                    for hf in range(2):
                        for n in range(len(summed(u, 0))):
                            for j in range(J):
                                t = 2 * j + hf
                                at, z = summed(u, t)[n]
                                last = mm(ps_seg[at:at + rows, 2 * hf * WCOLS:(2 * hf + 1) * WCOLS], z,
                                          ohe_ring[u][:, t, :], start=j == 0, stop=j == J - 1)
                        if p == 0:
                            for j in range(J):
                                t = 2 * j + hf
                                last = mm(ps_seg[:, (2 * hf + 1) * WCOLS:(2 * hf + 2) * WCOLS], ones_bf[:, :],
                                          ohe_ring[u][:, t, :].bitcast(bf16).rearrange("p (w h) -> p w h", h=2)[:, :, 1],
                                          start=j == 0, stop=j == J - 1)
                    last.then_inc(s["seg"], 1)

                def seg_sweep(c, k, u):
                    with pe.Fori(0, NSW) as w:
                        if p < 2:
                            pe.wait_ge(s["blk_z"], c + 1)
                        else:
                            pe.wait_ge(slot(s, "gathered", u), 128 * k + 128)
                        pe.wait_ge(s["swept_oh"], c * NSW + w + 1)
                        for n in range(len(summed(u, 0))):
                            for t in range(TILES):
                                at, z = summed(u, t)[n]
                                last = mm(ps_seg[at:at + rows, 0:SWEEP], z, sweep_oh[:, t, :],
                                          start=t == 0, stop=t == TILES - 1)
                        if p == 0:
                            for t in range(TILES):
                                last = mm(ps_seg[:, SWEEP:2 * SWEEP], ones[:, :], sweep_oh[:, t, :],
                                          start=t == 0, stop=t == TILES - 1)
                        last.then_inc(s["seg"], 1)

                def body(c, k, u):
                    enc = chunk(c, k, u, 2) if p == 0 else None
                    nxt = chunk(c, k, u, 1)
                    now = chunk(c, k, u, 0)
                    old = chunk(c, k, u, -1)
                    if p == 0:
                        if enc:
                            enc_pre(*enc)
                        if now:
                            second(1, s["blk_h"], s["blk_z"], s["blk_y"], c)
                        if nxt:
                            gathered_rows(*nxt)
                        if enc:
                            second(0, s["enc_h"], s["enc_z"], s["enc_y"], enc[0])
                        if nxt:
                            back(0, s["enc_z"], s["enc_e"], s["enc_zt"], nxt[0], z_enc[nxt[2]])
                        if old:
                            back(1, s["blk_z"], s["blk_e1"], s["blk_zt"], old[0], z_blk[old[2]])
                            seg(*old)
                        if nxt:
                            edge_rows(*nxt)
                        return
                    if p == 1 and nxt:
                        gathered_rows(*nxt)
                        edge_rows(*nxt)
                    if now:
                        seg(*now)
                    if p == 1 and nxt:
                        second(1, s["blk_h"], s["blk_z"], s["blk_y"], nxt[0])

                rounds(pe, *((1, 2), (0, 1), (0, 0), (0, 0))[p], body)

            def count_pairs(c, k, u):
                s, q = PH[2], u % 2
                wait(pe, s["widened"], value(pe, c - 1))
                pe.wait_ge(s["lo"], c + 1)
                for g in range(2):
                    pe.wait_ge(s["lo"], c + 1)
                    pe.wait_ge(s["pair_oh"], 2 * c + g + 1)
                    for i in range(GROUP):
                        t = g * GROUP + i
                        for bk, (lo, hi) in enumerate(BANKS):
                            last = mm(pair_bank(q, bk)[:, 0:hi - lo], lo_oh[q][:, t, :], pair_oh[g][:, i, lo:hi],
                                      start=t == 0, stop=t == TILES - 1)
                    last.then_inc(s["paired"], 1)

            def weigh(s, table, c, q):
                wait(pe, s["added"], value(pe, c - 1))
                pe.wait_ge(s["widened"], c + 1)
                rows_of = table[:, :, :].rearrange("p b (j d) -> p (b j) d", d=D_NODE)
                for hi in range(HI):
                    last = mm(ps_zt[q][0:D_NODE, 0:WIN], rows_of[:, hi, :], counts[q][:, hi * WIN:(hi + 1) * WIN],
                              start=hi == 0, stop=hi == HI - 1)
                last.then_inc(s["seg"], 1)

            def body_sage1(c, k, u):
                if now := chunk(c, k, u, 0):
                    count_pairs(*now)
                if old := chunk(c, k, u, -1):
                    weigh(PH[2], x1_em, old[0], old[2] % 2)

            def either(p):
                with pe.If(general):
                    edge_phase(p, 1)
                with pe.Else():
                    if p < 2:
                        edge_phase(p, 0)
                    elif p == 2:
                        rounds(pe, 1, 0, body_sage1)
                    else:
                        rounds(pe, 0, 0, lambda c, k, u: weigh(PH[3], t2_em, c, u % 2))
                pe.nop()

            nd = ND[0]
            with pe.Fori(0, NB) as b:
                pe.wait_ge(nd["block_in"], nd["first"] + b + 1)
                mm(ps_pre[0][0:D, :], nenc_w0[:, :], x_blk[:, :], start=True, stop=True).then_inc(nd["pre"], 1)
                node_tail(nd, 0, b)
                tables(nd, 0, b)
                pe.wait_ge(nd["parts"], nd["first"] + b + 1)
            either(0)
            nd = ND[1]
            pe.wait_ge(edges_done[0], 1)
            with pe.Fori(0, NB) as b:
                node_update(nd, 0, b)
                node_tail(nd, 1, b)
                tables(nd, 1, b)
                pe.wait_ge(nd["parts"], nd["first"] + b + 1)
            either(1)
            nd = ND[2]
            pe.wait_ge(edges_done[1], 1)
            with pe.Fori(0, NB) as b:
                node_update(nd, 1, b)
                node_tail(nd, 2, b)
                pe.wait_ge(st["ready"], 1)
                pe.wait_ge(nd["n"], nd["first"] + b + 1)
                mm(ps_pre[1][0:D, :], dec_w0[:, :], n_blk[:, :],
                   start=True, stop=True).then_inc(nd["tab"], 1)
                pe.wait_ge(nd["evac"], nd["first"] + b + 1)
                mm(ps_y[1][:, 0:J * D_NODE], ones[0:1, :], dec_b1[:, :, :].rearrange("a j d -> a (j d)"),
                   start=True, stop=False)
                for j in range(J):
                    last = mm(ps_y[1][:, j * D_NODE:(j + 1) * D_NODE], hn[:, j * P:(j + 1) * P], dec_w1[:, :],
                              start=False, stop=j == J - 1)
                last.then_inc(nd["parts"], 1)
                pe.wait_ge(nd["x1"], b + 1)
                for j in range(J):
                    last = nc.tensor.transpose(ps_zt[1][0:D_NODE, j * P:(j + 1) * P], xs[:, j, :], ident[:, :])
                last.then_inc(nd["x1t"], 1)
                pe.wait_ge(nd["blk"], b + 1)
            either(2)
            nd = ND[3]
            pe.wait_ge(edges_done[2], 1)
            with pe.Fori(0, NB) as b:
                n_in = value(pe, b + 1)
                pe.wait_ge(st["ready"], 1)
                pe.wait_ge(nd["aggd"], n_in)
                mm(ps_pre[0][0:D_SAGE, :], s_w1r[:, :], x_blk[:, :], start=True, stop=False)
                mm(ps_pre[0][0:D_SAGE, :], s_w1l[:, :], aggd[:, :], start=False, stop=True).then_inc(nd["pre"], 1)
                pe.wait_ge(nd["h"], nd["first"] + b + 1)
                for j in range(J):
                    last = mm(ps_y[0][:, j * D_NODE:(j + 1) * D_NODE], h_blk[:, j * P:(j + 1) * P],
                              s_w2l[:, :], start=True, stop=True)
                last.then_inc(nd["tab"], 1)
                pe.wait_ge(nd["x1"], b + 1)
            either(3)
            nd = ND[4]
            pe.wait_ge(edges_done[3], 1)
            with pe.Fori(0, NB) as b:
                mm(ps_y[0][:, 0:J * D_NODE], ones[0:1, :], s_b2[:, :, :].rearrange("a j d -> a (j d)"),
                   start=True, stop=False)
                pe.wait_ge(nd["aggd"], b + 1)
                for j in range(J):
                    y = ps_y[0][:, j * D_NODE:(j + 1) * D_NODE]
                    mm(y, aggd[:, j * P:(j + 1) * P], ident[0:D_NODE, 0:D_NODE], start=False, stop=False)
                    last = mm(y, h_blk[:, j * P:(j + 1) * P], s_w2r[:, :], start=False, stop=j == J - 1)
                last.then_inc(nd["parts"], 1)
                pe.wait_ge(nd["x1"], b + 1)

        @block.vector
        def _(dve):
            v = nc.vector
            chain = [0]

            def link(ins):
                chain[0] += 1
                ins.then_inc(st["chain"], 1)
                dve.wait_ge(st["chain"], chain[0])

            for t in [enc_w0] + w_e + w1_bd:
                link(v.memset(t[:, :], 0.0))
            v.memset(agg[:, :, :], 0.0)
            v.memset(agg2[:, :], 0.0)
            for t in sq_buf:
                v.memset(t[:, :, D:D + 1], EPS)
            v.memset(sqn[:, :, D:D + 1], EPS)
            v.memset(var_buf[:, :, :], 1.0)
            v.memset(ones_bf[:, :], 1.0)
            v.memset(ones[:, :], 1.0).then_inc(st["consts"], 1)
            dve.wait_ge(st["loads"], LOADED)
            link(v.tensor_copy(dst_rows[:, :, :].rearrange("c h e -> c (h e)"), dst_rows_i[:, :]))
            link(v.tensor_reduce(out=base_f[:, :], in_=dst_rows[:, :, :], axis=AX.X, op=ALU.min))
            link(v.tensor_reduce(out=top_f[:, :], in_=dst_rows[:, :, :], axis=AX.X, op=ALU.max))
            link(v.tensor_tensor(span_f[:, 0:2], top_f[:, :], base_f[:, :], ALU.subtract))
            link(v.tensor_tensor(span_f[:, 2:3], top_f[:, 1:2], base_f[:, 0:1], ALU.subtract))
            link(v.tensor_tensor(span_f[:, 3:4], base_f[:, 0:1], base_f[:, 1:2], ALU.subtract))
            link(v.tensor_scalar(span_f[:, 3:4], span_f[:, 3:4], float(WIN), None, ALU.mult))
            for h in range(2):
                last = v.tensor_scalar(rel_rows[:, h, :], dst_rows[:, h, :], base_f[:, h:h + 1], None, ALU.subtract)
            last.then_inc(st["rel_ready"], 1)
            for i, (w, n) in enumerate([(w, P) for w in w1] + [(w, D) for w in nw1] +
                                       [(w, 1) for w in b1] + [(w, 1) for w in nb1]):
                link(v.tensor_reduce(out=row_mean[0:n, i:i + 1], in_=w[:, :], axis=AX.X, op=ALU.add))
                link(v.tensor_scalar(row_mean[0:n, i:i + 1], row_mean[0:n, i:i + 1], 1.0 / D, None, ALU.mult))
                link(v.tensor_scalar(w[:, :], w[:, :], row_mean[0:n, i:i + 1], None, ALU.subtract))
            for s in range(3):
                for h in range(2):
                    link(v.tensor_copy(w1_bd[s][h * D:(h + 1) * D, h * D:(h + 1) * D], w1[s][h * D:(h + 1) * D, :]))
                link(v.tensor_copy(b1_part[s][:, 0, :], b1[s][:, :]))
                link(v.tensor_tensor(b1_rest[s][:, :], b1[s][:, :], b1_part[s][:, 0, :], ALU.subtract))
                link(v.tensor_copy(b1_part[s][:, 1, :], b1_rest[s][:, :]))
                link(v.tensor_tensor(b1_rest[s][:, :], b1_rest[s][:, :], b1_part[s][:, 1, :], ALU.subtract))
                link(v.tensor_copy(b1_part[s][:, 2, :], b1_rest[s][:, :]))
                for j in range(J):
                    link(v.tensor_copy(nb1_row[s][:, j, :], nb1[s][:, :]))
            v.nop().then_inc(st["biases"], 1)
            for s in range(2):
                link(v.tensor_scalar(w_ag[s][:, :], w_a[s][:, :], gam_stack[:, :], None, ALU.mult))
            link(v.tensor_scalar(w_ag2[:, :], w_a[1][0:D, :], gam[2][0:D, :], None, ALU.mult))
            link(v.tensor_tensor(bet_sum[:, 0:1], bet[0][0:D, :], bet[1][0:D, :], ALU.add))
            link(v.tensor_tensor(bet_sum[:, 1:2], bet_sum[:, 0:1], bet[2][0:D, :], ALU.add))
            v.nop().then_inc(st["folded"], 1)
            dve.wait_ge(st["mm"], 1)
            link(v.tensor_copy(w_deg[:, :, :].rearrange("a s d -> a (s d)"), ps_misc[0:1, 0:P]))
            link(v.tensor_tensor(b0[2][:, :], b0[2][:, :], ps_misc[:, P:P + 1], ALU.add))
            dve.wait_ge(st["base_in"], 48)
            link(v.tensor_copy(dst_em[:, :], dst_em_i))
            link(v.tensor_copy(base_i[:, :], base_row[:, :]))
            for h in range(2):
                link(v.tensor_tensor(
                    rel_em[:, :].rearrange("p (c j h) -> p c j h", j=J, h=2)[:, :, :, h],
                    dst_em[:, :].rearrange("p (c j h) -> p c j h", j=J, h=2)[:, :, :, h],
                    bc(base_all[:, :, h:h + 1], [P, NCH, J]), ALU.subtract))
            link(v.tensor_reduce(out=span_max[:, :], in_=span_row[:, :], axis=AX.X, op=ALU.max))
            link(v.tensor_scalar(flag[:, :], span_max[:, :], float(WIN), None, ALU.is_ge))
            dve.wait_ge(st["pool_iota"], 1)
            v.nop().then_inc(st["ready"], 1)
            v.nop().then_inc(st["flag_ready"], 1)
            general = dve.value_load(flag[0:1, 0:1], min_val=0, max_val=1)

            def inverse_sqrt(y, x, counter, at, between=()):
                n = [0]
                between = list(between)

                def step(ins):
                    n[0] += 1
                    ins.then_inc(counter, 1)
                    if between:
                        between.pop(0)()
                    dve.wait_ge(counter, at + n[0])

                width = y.free_size()
                t, bits = newton_t[:, 0:width], newton_i[:, 0:width]
                step(v.tensor_scalar(bits, x.bitcast(i32), 1, None, ALU.logical_shift_right))
                step(v.tensor_scalar(y.bitcast(i32), bits, -1.0, float(0x5f3759df), ALU.mult, ALU.add))
                for i in range(NEWTON):
                    step(v.tensor_tensor(t, y, y, ALU.mult))
                    step(v.scalar_tensor_tensor(out=t, in0=t, scalar=-0.5, in1=x, op0=ALU.mult, op1=ALU.mult))
                    step(v.scalar_tensor_tensor(out=y, in0=t, scalar=1.5, in1=y, op0=ALU.add, op1=ALU.mult))

            def node_norm(nd, b):
                dve.wait_ge(nd["sq"], nd["first"] + b + 1)
                v.tensor_reduce(out=varn[:, :], in_=sqn[:, :, :], axis=AX.X, op=ALU.add).then_inc(nd["var"], 1)
                dve.wait_ge(nd["var"], nd["first"] + b + 1)
                inverse_sqrt(rstdn[:, :], varn[:, :], nd["newton"], (nd["first"] + b) * NSTEP)
                v.tensor_tensor(zn[:, :, :], ps_y[0][:, 0:J * D].rearrange("p (j d) -> p j d", d=D),
                                bc(rstdn[:, :].unsqueeze(2), [P, J, D]), ALU.mult).then_inc(nd["z"], 1)
                dve.wait_ge(nd["zt"], nd["first"] + b + 1)

            def tables(nd, b):
                dve.wait_ge(nd["evac"], nd["first"] + b + 1)
                v.tensor_copy(partn[:, :, 0, :], tabn[:, :, 1, :]).then_inc(nd["split"], 1)
                dve.wait_ge(nd["split"], 4 * b + 1)
                v.tensor_tensor(restn[:, :, :], tabn[:, :, 1, :], partn[:, :, 0, :], ALU.subtract).then_inc(nd["split"], 1)
                dve.wait_ge(nd["split"], 4 * b + 2)
                v.tensor_copy(partn[:, :, 1, :], restn[:, :, :]).then_inc(nd["split"], 1)
                dve.wait_ge(nd["split"], 4 * b + 3)
                v.tensor_tensor(restn[:, :, :], restn[:, :, :], partn[:, :, 1, :], ALU.subtract).then_inc(nd["split"], 1)
                dve.wait_ge(nd["split"], 4 * b + 4)
                v.tensor_copy(partn[:, :, 2, :], restn[:, :, :]).then_inc(nd["parts"], 1)
                dve.wait_ge(nd["stored"], 48 * b + 48)

            def new_nodes(nd, s, b):
                cols = n_fm[:, bass.ds(b * NBLK, NBLK)]
                v.tensor_copy(agg_blk[:, :, :], agg[:, :, bass.ds(b * NBLK, NBLK)])
                if s == 2:
                    v.tensor_copy(agg2_blk[:, :], agg2[:, bass.ds(b * NBLK, NBLK)])
                v.tensor_copy(n_blk[:, :], cols).then_inc(nd["block_in"], 1)
                node_norm(nd, b)
                v.scalar_tensor_tensor(out=cols, in0=ps_zt[0][0:D, :], scalar=ngam[s][:, :], in1=cols,
                                       op0=ALU.mult, op1=ALU.add).then_inc(nd["scaled"], 1)
                dve.wait_ge(nd["scaled"], b + 1)
                v.tensor_scalar(n_blk[:, :], cols, nbet[s][:, :], None, ALU.add)
                v.tensor_scalar(cols, cols, nbet[s][:, :], None, ALU.add).then_inc(nd["n"], 1)

            def layer_norm(nd, b, src, resid, dst):
                n = [0]

                def step(ins):
                    n[0] += 1
                    ins.then_inc(nd["own"], 1)
                    dve.wait_ge(nd["own"], STEPS * b + n[0])

                step(v.tensor_tensor(xs[:, :, :], src, resid, ALU.add))
                step(v.tensor_reduce(out=xm[:, :], in_=xs[:, :, :], axis=AX.X, op=ALU.add))
                step(v.tensor_scalar(xm[:, :], xm[:, :], 1.0 / D_NODE, None, ALU.mult))
                step(v.tensor_tensor(xc[:, :, :], xs[:, :, :], bc(xm[:, :].unsqueeze(2), [P, J, D_NODE]), ALU.subtract))
                step(v.tensor_tensor(xq[:, :, :], xc[:, :, :], xc[:, :, :], ALU.mult))
                step(v.tensor_reduce(out=varn[:, :], in_=xq[:, :, :], axis=AX.X, op=ALU.add))
                step(v.tensor_scalar(varn[:, :], varn[:, :], 1.0 / D_NODE, EPS, ALU.mult, ALU.add))
                inverse_sqrt(rstdn[:, :], varn[:, :], nd["newton2"], b * NSTEP)
                return v.tensor_tensor(dst, xc[:, :, :], bc(rstdn[:, :].unsqueeze(2), [P, J, D_NODE]), ALU.mult)

            STEPS = 7

            def edge_phase(p, g):
                s = PH[p]
                rows = (P, D, D_NODE, D_NODE)[p]

                def receivers_one_hot(c, k, u):
                    wait(dve, s["rows_in"], c - 1)
                    dve.wait_ge(slot(s, "relb_in", u), 16 * k + 16)
                    v.tensor_scalar(ohf_ring[u][:, :], relb_ring[u][:, :], win_row[:, :], None,
                                    ALU.is_equal).then_inc(s["ohf"], 1)

                def sums_one_hot(c, k, u):
                    v.tensor_tensor(ohe_ring[u][:, :, :], bc(node_iota[:, 0:WCOLS].unsqueeze(1), [P, TILES, WCOLS]),
                                    bc(rel_em[:, bass.ds(c * TILES, TILES)].unsqueeze(2), [P, TILES, WCOLS]),
                                    ALU.is_equal).then_inc(s["ohe"], 1)

                def variance(i, sq, done, c):
                    dve.wait_ge(sq, c + 1)
                    v.tensor_reduce(out=var_buf[:, i, :], in_=sq_buf[i][:, :, :], axis=AX.X,
                                    op=ALU.add).then_inc(done, 1)

                def normalise(i, done, z):
                    v.tensor_tensor(z[:, :, :], ps_y[i][:, :].rearrange("p (t d) -> p t d", d=D),
                                    bc(rstd_buf[:, i, :].unsqueeze(2), [P, TILES, D]), ALU.mult).then_inc(done, 1)

                def make_e1(c, k, u):
                    wait(dve, slot(s, "e1_out", u), 16 * k)
                    dve.wait_ge(s["blk_zt"], c + 1)
                    v.scalar_tensor_tensor(out=e1_ring[u][:, :], in0=ps_zt[1][:, :], scalar=gam[1][:, :],
                                           in1=e0_ring[u][:, :], op0=ALU.mult, op1=ALU.add).then_inc(s["blk_e1"], 1)

                def target(cols):
                    return agg[:, :, cols] if p == 0 else agg2[0:rows, cols]

                def add_up(c):
                    if g:
                        return add_sweep(c)
                    b_at = [dve.value_load(base_i[0:1, bass.ds(2 * c + h, 1)], min_val=0, max_val=N_NODES - 1)
                            for h in range(2)]
                    dve.wait_ge(s["seg"], c + 1)
                    for h in range(2):
                        src = ps_seg[:, 2 * h * WCOLS:(2 * h + 2) * WCOLS].rearrange("p (a w) -> p a w", a=2)
                        src = src[:, :, 0:WIN] if p == 0 else src[0:rows, 0, 0:WIN]
                        tgt = target(bass.ds(b_at[h], WIN))
                        wait(dve, s["added"], 2 * c + h)
                        v.tensor_tensor(tgt, tgt, src, ALU.add).then_inc(s["added"], 1)

                def add_sweep(c):
                    with dve.Fori(0, NSW) as w:
                        v.tensor_tensor(sweep_oh[:, :, :],
                                        bc(node_iota[:, bass.ds(w * SWEEP, SWEEP)].unsqueeze(1), [P, TILES, SWEEP]),
                                        bc(dst_em[:, bass.ds(c * TILES, TILES)].unsqueeze(2), [P, TILES, SWEEP]),
                                        ALU.is_equal).then_inc(s["swept_oh"], 1)
                        dve.wait_ge(s["seg"], c * NSW + w + 1)
                        src = ps_seg[0:rows, 0:SWEEP]
                        if p == 0:
                            src = ps_seg[:, :].rearrange("p (a w) -> p a w", a=2)
                        tgt = target(bass.ds(w * SWEEP, SWEEP))
                        v.tensor_tensor(tgt, tgt, src, ALU.add).then_inc(s["added"], 1)
                        dve.wait_ge(s["added"], c * NSW + w + 1)

                def body_a(c, k, u):
                    enc, now, old = (chunk(c, k, u, d) for d in (2, 0, -1))
                    if now:
                        variance(1, s["blk_sq"], s["blk_var"], c)
                    if old:
                        make_e1(*old)
                    if enc:
                        variance(0, s["enc_sq"], s["enc_var"], enc[0])
                    fill = []
                    if enc and not g:
                        fill.append(lambda: receivers_one_hot(*enc))
                    if now and not g:
                        fill.append(lambda: sums_one_hot(*now))
                    if enc or now:
                        if now:
                            dve.wait_ge(s["blk_var"], c + 1)
                        if enc:
                            dve.wait_ge(s["enc_var"], enc[0] + 1)
                        inverse_sqrt(rstd_buf[:, :, :].rearrange("p a t -> p (a t)"),
                                     var_buf[:, :, :].rearrange("p a t -> p (a t)"), s["newton"], (c + 2) * NSTEP, fill)
                    if enc:
                        normalise(0, s["enc_z"], z_enc[enc[2]])
                    if now:
                        normalise(1, s["blk_z"], z_blk[now[2]])
                    if old:
                        add_up(old[0])

                def body_b(c, k, u):
                    new, nxt, now = (chunk(c, k, u, d) for d in (2, 1, 0))
                    if new and p == 1 and not g:
                        receivers_one_hot(*new)
                    if nxt and not g:
                        sums_one_hot(*nxt)
                    if now:
                        add_up(c)
                    if nxt and p == 1:
                        variance(1, s["blk_sq"], s["blk_var"], nxt[0])
                        dve.wait_ge(s["blk_var"], nxt[0] + 1)
                        inverse_sqrt(rstd_buf[:, 1, :], var_buf[:, 1, :], s["newton"], (c + 1) * NSTEP)
                        normalise(1, s["blk_z"], z_blk[nxt[2]])

                if p == 0:
                    rounds(dve, 1, 2, body_a)
                else:
                    rounds(dve, 0, 2 if p == 1 else 1, body_b)
                dve.wait_ge(s["added"], NCH * NSW if g else 2 * NCH)

            def pair_keys():
                s = PH[2]
                n = [0]

                def step(ins):
                    n[0] += 1
                    ins.then_inc(s["keyed"], 1)
                    dve.wait_ge(s["keyed"], n[0])

                dve.wait_ge(s["src_in"], 16)
                step(v.tensor_copy(pair_iota, node_iota[:, 0:PAIRS]))
                step(v.tensor_tensor(key_em[:, :].rearrange("p (c t) -> p c t", t=TILES),
                                     dst_em[:, :].rearrange("p (c t) -> p c t", t=TILES),
                                     bc(base_all[:, :, 0:1], [P, NCH, TILES]), ALU.subtract))
                step(v.tensor_scalar(src_bits, src_all, P - 1, None, ALU.bitwise_and))
                step(v.tensor_copy(lo_em[:, :], src_bits))
                step(v.tensor_scalar(src_bits, src_all, P.bit_length() - 1, None, ALU.logical_shift_right))
                step(v.scalar_tensor_tensor(out=key_em[:, :], in0=src_bits, scalar=float(WIN), in1=key_em[:, :],
                                            op0=ALU.mult, op1=ALU.add))

            def pair_one_hots(c, k, u):
                s, q = PH[2], u % 2
                n_free = value(dve, 2 * c)
                v.tensor_copy(now_key[q][:, :], key_em[:, bass.ds(c * TILES, TILES)]).then_inc(s["now"], 1)
                wait(dve, s["paired"], value(dve, 2 * c - 2))
                v.tensor_tensor(lo_oh[q], bc(node_iota[:, 0:P].unsqueeze(1), [P, TILES, P]),
                                bc(lo_em[:, bass.ds(c * TILES, TILES)].unsqueeze(2), [P, TILES, P]),
                                ALU.is_equal).then_inc(s["lo"], 1)
                for g in range(2):
                    wait(dve, s["paired"], 2 * c - 1 + g)
                    dve.wait_ge(s["now"], c + 1)
                    for i in range(GROUP):
                        t = g * GROUP + i
                        last = v.tensor_scalar(pair_oh[g][:, i, :], pair_iota, now_key[q][:, t:t + 1], None,
                                               ALU.is_equal)
                    last.then_inc(s["pair_oh"], 1)

            def add_sums(s, c, q):
                at = dve.value_load(base_i[0:1, bass.ds(2 * c, 1)], min_val=0, max_val=N_NODES - 1)
                dve.wait_ge(s["seg"], c + 1)
                wait(dve, s["added"], c)
                tgt = agg2[0:D_NODE, bass.ds(at, WIN)]
                v.tensor_tensor(tgt, tgt, ps_zt[q][0:D_NODE, 0:WIN], ALU.add).then_inc(s["added"], 1)

            def body_sage1(c, k, u):
                if now := chunk(c, k, u, 0):
                    pair_one_hots(*now)
                if old := chunk(c, k, u, -2):
                    add_sums(PH[2], old[0], old[2] % 2)

            def either(p):
                with dve.If(general):
                    edge_phase(p, 1)
                with dve.Else():
                    if p < 2:
                        edge_phase(p, 0)
                    elif p == 2:
                        pair_keys()
                        rounds(dve, 2, 0, body_sage1)
                        dve.wait_ge(PH[2]["added"], NCH)
                    else:
                        rounds(dve, 0, 0, lambda c, k, u: add_sums(PH[3], c, u % 2))
                        dve.wait_ge(PH[3]["added"], NCH)
                v.nop().then_inc(edges_done[p], 1)

            nd = ND[0]
            with dve.Fori(0, NB) as b:
                v.tensor_copy(x_blk[:, :], x_fm[:, bass.ds(b * NBLK, NBLK)]).then_inc(nd["block_in"], 1)
                node_norm(nd, b)
                for dst in (n_blk[:, :], n_fm[:, bass.ds(b * NBLK, NBLK)]):
                    last = v.tensor_scalar(dst, ps_zt[0][0:D, :], ngam[0][:, :], nbet[0][:, :], ALU.mult, ALU.add)
                last.then_inc(nd["n"], 1)
                tables(nd, b)
            either(0)
            nd = ND[1]
            with dve.Fori(0, NB) as b:
                new_nodes(nd, 1, b)
                tables(nd, b)
            either(1)
            nd = ND[2]
            with dve.Fori(0, NB) as b:
                new_nodes(nd, 2, b)
                dve.wait_ge(nd["parts"], nd["first"] + b + 1)
                layer_norm(nd, b, ps_y[1][:, 0:J * D_NODE].rearrange("p (j d) -> p j d", d=D_NODE),
                           x_em[:, bass.ds(b, 1), :].rearrange("p a (j d) -> p (a j) d", d=D_NODE),
                           xs[:, :, :]).then_inc(nd["x1"], 1)
                dve.wait_ge(nd["x1"], b + 1)
                v.tensor_copy(x1_em[:, bass.ds(b, 1), :].rearrange("p a (j d) -> p (a j) d", d=D_NODE),
                              xs[:, :, :])
                dve.wait_ge(nd["x1t"], b + 1)
                v.tensor_copy(x_blk[:, :], ps_zt[1][0:D_NODE, :]).then_inc(nd["copied"], 1)
                dve.wait_ge(st["chain"], chain[0])
                dve.wait_ge(nd["copied"], b + 1)
                v.tensor_copy(x1_fm[:, bass.ds(b * NBLK, NBLK)], x_blk[:, :]).then_inc(nd["blk"], 1)
                dve.wait_ge(nd["stored"], 16 * b + 16)
            link(v.tensor_scalar(rdeg[:, :], agg[0:D_NODE, 1, :], 1.0, None, ALU.max))
            v.reciprocal(rdeg[:, :], rdeg[:, :])
            link(v.memset(agg2[:, :], 0.0))
            either(2)
            nd = ND[3]
            with dve.Fori(0, NB) as b:
                cols = bass.ds(b * NBLK, NBLK)
                v.tensor_copy(x_blk[:, :], x1_fm[:, cols])
                v.tensor_tensor(aggd[:, :], agg2[0:D_NODE, cols], rdeg[:, cols], ALU.mult).then_inc(nd["aggd"], 1)
                dve.wait_ge(nd["tab"], nd["first"] + b + 1)
                v.tensor_copy(t2_em[:, bass.ds(b, 1), :].rearrange("p a w -> p (a w)"), ps_y[0][:, 0:J * D_NODE])
                v.tensor_copy(t2n[:, :, :].rearrange("p j d -> p (j d)"), ps_y[0][:, 0:J * D_NODE]).then_inc(nd["x1"], 1)
                dve.wait_ge(nd["stored"], 16 * b + 16)
            link(v.memset(agg2[:, :], 0.0))
            either(3)
            nd = ND[4]
            with dve.Fori(0, NB) as b:
                cols = bass.ds(b * NBLK, NBLK)
                v.tensor_copy(h_blk[:, :], h_fm[:, cols])
                v.tensor_tensor(aggd[:, :], agg2[0:D_NODE, cols], rdeg[:, cols], ALU.mult).then_inc(nd["aggd"], 1)
                dve.wait_ge(nd["parts"], nd["first"] + b + 1)
                layer_norm(nd, b, ps_y[0][:, 0:J * D_NODE].rearrange("p (j d) -> p j d", d=D_NODE),
                           x1_em[:, bass.ds(b, 1), :].rearrange("p a (j d) -> p (a j) d", d=D_NODE),
                           outn[:, :, :]).then_inc(nd["x1"], 1)
                dve.wait_ge(s_final, 16 * b + 16)


IN = {
    "edge_enc_w0": "L0_gnn_edge_enc_w0", "edge_enc_b0": "L0_gnn_edge_enc_b0", "edge_enc_w1": "L0_gnn_edge_enc_w1",
    "edge_enc_b1": "L0_gnn_edge_enc_b1", "edge_enc_g": "L0_gnn_edge_enc_g", "edge_enc_beta": "L0_gnn_edge_enc_beta",
    "node_enc_w0": "L0_gnn_node_enc_w0", "node_enc_b0": "L0_gnn_node_enc_b0", "node_enc_w1": "L0_gnn_node_enc_w1",
    "node_enc_b1": "L0_gnn_node_enc_b1", "node_enc_g": "L0_gnn_node_enc_g", "node_enc_beta": "L0_gnn_node_enc_beta",
    "edge_blk_w0": "L0_gnn_edge_blk_w0", "edge_blk_b0": "L0_gnn_edge_blk_b0", "edge_blk_w1": "L0_gnn_edge_blk_w1",
    "edge_blk_b1": "L0_gnn_edge_blk_b1", "edge_blk_g": "L0_gnn_edge_blk_g", "edge_blk_beta": "L0_gnn_edge_blk_beta",
    "node_blk_w0": "L0_gnn_node_blk_w0", "node_blk_b0": "L0_gnn_node_blk_b0", "node_blk_w1": "L0_gnn_node_blk_w1",
    "node_blk_b1": "L0_gnn_node_blk_b1", "node_blk_g": "L0_gnn_node_blk_g", "node_blk_beta": "L0_gnn_node_blk_beta",
    "dec_w0": "L0_gnn_dec_w0", "dec_b0": "L0_gnn_dec_b0", "dec_w1": "L0_gnn_dec_w1", "dec_b1": "L0_gnn_dec_b1",
    "W1_l": "L1_gnn_W1_l", "sage_b1": "L1_gnn_b1", "W1_r": "L1_gnn_W1_r", "W2_l": "L1_gnn_W2_l",
    "sage_b2": "L1_gnn_b2", "W2_r": "L1_gnn_W2_r",
}


def kernel(**inputs):
    import numpy as np
    import concourse.bacc as bacc
    from concourse.bass_utils import run_bass_kernel_spmd

    a = {n: np.ascontiguousarray(inputs[full]) for n, full in IN.items()}
    x, src, dst = (np.asarray(inputs[n]) for n in ("x", "src", "dst"))
    attr = np.asarray(inputs["edge_attr_8"])
    E = NCH * CHUNK
    pad = E - N_EDGES
    far = np.full(pad, 1 << 20, dst.dtype)
    zero = np.zeros(pad, src.dtype)

    def edge_major(v):
        return np.ascontiguousarray(v.reshape(NCH, 2, J, P).transpose(0, 3, 2, 1).reshape(NCH, P, TILES))

    a["src_em"] = edge_major(np.concatenate([src, zero]))
    a["src_all"] = np.ascontiguousarray(a["src_em"].transpose(1, 0, 2).reshape(P, -1))
    a["dst_idx"] = edge_major(np.concatenate([dst, zero]))
    a["dst_em"] = np.ascontiguousarray(edge_major(np.concatenate([dst, far])).transpose(1, 0, 2).reshape(P, -1))
    a["dst_rows"] = np.concatenate([dst, np.repeat(dst[-1:], pad)]).reshape(NCH, CHUNK)
    attr = np.concatenate([attr, np.zeros((pad, D_EDGE), attr.dtype)])
    a["attr_fm"] = np.ascontiguousarray(attr.reshape(NCH, 2, HALF, D_EDGE).transpose(0, 1, 3, 2)
                                        .reshape(NCH, 2 * D_EDGE, HALF))
    xp = np.concatenate([x, np.zeros((NPAD - N_NODES, D_NODE), x.dtype)])
    a["x_fm"] = np.ascontiguousarray(xp.T)
    a["x_em"] = np.ascontiguousarray(xp.reshape(NB, J, P, D_NODE).transpose(2, 0, 1, 3).reshape(P, NB, J * D_NODE))
    a["win_row"] = (np.arange(WROWS) // PARTS).astype(np.float32).reshape(WROWS, 1)

    nc = bacc.Bacc("TRN2", target_bir_lowering=False, num_devices=1)
    aps, arrays = {}, {}
    for n, v in a.items():
        arrays[f"in_{n}"] = v
        aps[n] = nc.dram_tensor(f"in_{n}", v.shape, mybir.dt.from_np(v.dtype), kind="ExternalInput").ap()
    out = nc.dram_tensor("out_nodes", (NPAD, D_NODE), mybir.dt.float32, kind="ExternalOutput").ap()
    build(nc, aps, out)
    r = run_bass_kernel_spmd(nc, [arrays], core_ids=[0])
    return r.results[0]["out_nodes"][:N_NODES]
```

```python
from contextlib import ExitStack

import concourse.bass as bass
from concourse import mybir
from concourse.alu_op_type import AluOpType as ALU

N_NODES = 3125
N_EDGES = 103125
D = 64
D_NODE, D_EDGE, D_SAGE = 16, 8, 32
EPS = 1e-5

P = 128
HALF = 512
CHUNK = 2 * HALF
TILES = CHUNK // P
J = HALF // P
NCH = -(-N_EDGES // CHUNK)
PARTS = 3
WIN = 38
WROWS = PARTS * WIN
RUN = 256
PROWS = PARTS * D_NODE
WCOLS = 64
NBLK = 512
NB = -(-N_NODES // NBLK)
NPAD = NB * NBLK
SWEEP = 256
NSW = NPAD // SWEEP
HI = -(-N_NODES // P)
PAIRS = HI * WIN
HI0 = -(-HI // 2)
GROUP = TILES // 2
SHARE = -(-N_NODES // (NCH // 4))
LOADS = 4
DEPTH = 2
NEWTON = 3
NSTEP = 2 + 3 * NEWTON

assert HALF == TILES * D and NCH * TILES <= 2 * HALF and HI0 * WIN <= 512 and WROWS <= P
assert LOADS == 4 and SHARE * (NCH // 4) <= NPAD
assert NCH % 2 == 1 and NCH >= 7

PIECES = ([(f"w1_{s}", P, D) for s in range(3)] + [(f"nw1_{s}", D, D) for s in range(3)] +
          [(f"b1_{s}", 1, D) for s in range(3)] + [(f"nb1_{s}", 1, D) for s in range(3)] +
          [(f"w_a{s}", P, D) for s in range(2)] + [("enc_w0", 2 * D_EDGE, P)] +
          [(f"w_e{s}", P, P) for s in range(2)] + [(f"w_sr{s}", D, 2 * D) for s in range(2)] +
          [(f"w_n{s}", D + 1, D) for s in range(2)] + [("nenc_w0", D_NODE, D), ("dec_w0", D, D), ("dec_w1", D, D_NODE)] +
          [("s_w1l", PROWS, D_SAGE), ("s_w1r", D_NODE, D_SAGE), ("eyes", PROWS, D_NODE)] +
          [(n, D_SAGE, D_NODE) for n in ("s_w2l", "s_w2r")] +
          [(n, 1, J * D_NODE) for n in ("dec_b1", "s_b2")] +
          [(f"{n}{s}", P, 1) for n in ("b0_", "gam", "bet") for s in range(3)] + [("gam_stack", P, 1)] +
          [(f"{n}{s}", D, 1) for n in ("nb0_", "ngam", "nbet") for s in range(3)] +
          [("dec_b0", D, 1), ("s_b1", D_SAGE, 1), ("win_row", WROWS, 1)])
PACKED = sum(c for _, _, c in PIECES)


def build(nc, I, out):
    f32, bf16, f16, i32 = mybir.dt.float32, mybir.dt.bfloat16, mybir.dt.float16, mybir.dt.int32
    ACT = mybir.ActivationFunctionType
    AX = mybir.AxisListType
    ctx = ExitStack()
    with ctx:
        def sb(name, shape, dt=f32):
            return ctx.enter_context(nc.sbuf_tensor(name, shape, dt))

        def bank(name):
            return ctx.enter_context(nc.psum_tensor(name, [P, 512], f32))

        def sem(name):
            return ctx.enter_context(nc.semaphore(name))

        def sems(prefix, names):
            return {n: sem(f"{prefix}_{n}") for n in names.split()}

        def dram(name, shape, dt=f32):
            return nc.dram_tensor(name, shape, dt, kind="Internal").ap()

        def bc(ap, shape):
            return ap.to_broadcast(shape)

        send_tab = [dram(f"send_tab{s}", (NPAD, D)) for s in range(2)]
        recv_tab = [dram(f"recv_tab{s}", (NPAD, D)) for s in range(2)]
        recv_parts = [dram(f"recv_parts{s}", (NPAD * PARTS, D), bf16) for s in range(2)]
        sage_tab = [dram(f"sage_tab{s}", (NPAD, D_NODE)) for s in range(2)]
        e1_dram = dram("e1_dram", (NCH, P, HALF))
        rel_dram = dram("rel_dram", (NCH, CHUNK), bf16)
        pairs_dram = dram("pairs_dram", (NCH, P, PAIRS), bf16)
        base_dram = dram("base_dram", (NCH, 2))
        span_dram = dram("span_dram", (NCH, 6))
        bias_dram = dram("bias_dram", (3, PARTS, D), bf16)

        ident = sb("ident", [P, P])
        ones = sb("ones", [P, P])
        ones_bf = sb("ones_bf", [P, P], bf16)
        node_iota = sb("node_iota", [P, NPAD])
        flag = sb("flag", [1, 1], i32)
        base_i = sb("base_i", [1, NCH * 2], i32)
        dst_em = sb("dst_em", [P, NCH * TILES])
        rel_em = sb("rel_em", [P, NCH * TILES])
        n_fm = sb("n_fm", [D, NPAD])
        agg = sb("agg", [P, 2, NPAD])
        agg2 = sb("agg2", [D, NPAD])
        x1_em = sb("x1_em", [P, NB, J * D_NODE])
        h_fm = sb("h_fm", [D_SAGE, NPAD])
        rdeg = n_fm[0:PROWS, :]
        x1_fm = agg[0:D_NODE, 0, :]
        x_fm = h_fm[0:D_NODE, :]
        x_em = sb("x_em", [P, NB, J * D_NODE])
        t2_em = x_em

        packed = sb("packed", [P, PACKED])
        W, col = {}, 0
        for name, n_rows, n_cols in PIECES:
            W[name] = packed[0:n_rows, col:col + n_cols]
            col += n_cols
        centred = packed[:, 0:12 * D].rearrange("p (m d) -> p m d", d=D)
        w_a_both = packed[:, 12 * D:14 * D].rearrange("p (s d) -> p s d", d=D)
        w_e, w_sr, w_n, w_a = ([W[f"{n}{s}"] for s in range(2)] for n in ("w_e", "w_sr", "w_n", "w_a"))
        b0, gam, bet, nb0, ngam, nbet, nw1 = (
            [W[f"{n}{s}"] for s in range(3)] for n in ("b0_", "gam", "bet", "nb0_", "ngam", "nbet", "nw1_"))
        enc_w0, nenc_w0, gam_stack, win_row = W["enc_w0"], W["nenc_w0"], W["gam_stack"], W["win_row"]
        dec_w0, dec_b0, dec_w1, dec_b1 = W["dec_w0"], W["dec_b0"], W["dec_w1"], W["dec_b1"]
        eyes = W["eyes"]
        s_w1l, s_w1r, s_b1, s_w2l, s_w2r, s_b2 = (W[n] for n in ("s_w1l", "s_w1r", "s_b1", "s_w2l", "s_w2r", "s_b2"))
        w1_bd_all = sb("w1_bd", [P, 3, P])
        w1_bd = [w1_bd_all[:, s, :] for s in range(3)]
        b1_part = sb("b1_part", [1, 3, PARTS, D], bf16)
        b1_rest = sb("b1_rest", [1, 3, D])
        b1_rows_all = sb("b1_rows", [PARTS, 3, TILES, D], bf16)
        b1_rows = [b1_rows_all[:, s, :, :] for s in range(3)]
        row_mean = sb("row_mean", [P, 12])
        nb1_row_all = sb("nb1_row", [1, 3, J, D])
        nb1_row = [nb1_row_all[:, s, :, :] for s in range(3)]
        w_ag_both = sb("w_ag", [P, 2, D])
        w_ag = [w_ag_both[:, s, :] for s in range(2)]
        w_ag2 = sb("w_ag2", [D, D])
        bet_sum = sb("bet_sum", [D, 2])

        idx_ring = [sb(f"idx_ring{u}", [P, TILES], i32) for u in range(DEPTH)]
        idxd_ring = [sb(f"idxd_ring{u}", [P, TILES], i32) for u in range(DEPTH)]
        edge_space = sb("edge_space", [P, 10, TILES * D])
        edge_slots = [edge_space[:, i, :].rearrange("p (t d) -> p t d", d=D) for i in range(10)]
        g_ring, gd_ring, z_enc, z_blk = edge_slots[0:2], edge_slots[2:4], edge_slots[4:8], edge_slots[8:10]
        gs_ring = [sb(f"gs_ring{u}", [P, TILES, D_NODE]) for u in range(DEPTH)]
        attr_ring = [sb(f"attr_ring{u}", [2 * D_EDGE, HALF]) for u in range(DEPTH)]
        relb_full = [sb(f"relb_ring{u}", [P, CHUNK], bf16) for u in range(DEPTH)]
        relb_ring = [r[0:WROWS, :] for r in relb_full]
        prw_ring = [sb(f"prw_ring{u}", [WROWS, 2, D], bf16) for u in range(DEPTH)]
        ohf_full = [sb(f"ohf_ring{u}", [P, CHUNK], bf16) for u in range(DEPTH)]
        ohf_ring = [r[0:WROWS, :] for r in ohf_full]
        ohe_ring = [sb(f"ohe_ring{u}", [P, TILES, WCOLS]) for u in range(DEPTH)]
        e0_ring = [sb(f"e0_ring{u}", [P, HALF]) for u in range(DEPTH)]
        e1_ring = [sb(f"e1_ring{u}", [P, HALF]) for u in range(DEPTH)]
        (idx_ring, idxd_ring, g_ring, gd_ring, gs_ring, attr_ring, relb_ring, prw_ring, ohf_ring, ohe_ring,
         z_blk, e0_ring, e1_ring) = (2 * ring for ring in (
             idx_ring, idxd_ring, g_ring, gd_ring, gs_ring, attr_ring, relb_ring, prw_ring, ohf_ring, ohe_ring,
             z_blk, e0_ring, e1_ring))
        sweep_oh = sb("sweep_oh", [P, TILES, SWEEP])
        h_buf_all = sb("h_buf", [P, 2, HALF])
        h_buf = [h_buf_all[:, i, :] for i in range(2)]
        sq_buf = [sb(f"sq_buf{i}", [P, TILES, D + 1]) for i in range(2)]
        var_buf = sb("var_buf", [P, 2, TILES])
        rstd_buf = sb("rstd_buf", [P, 2, TILES])
        newton_t = sb("newton_t", [P, 2 * TILES])
        newton_i = sb("newton_i", [P, 2 * TILES], i32)

        hn = sb("hn", [D, NBLK])
        x_blk = sb("x_blk", [D_NODE, NBLK])
        agg_blk = sb("agg_blk", [P, 2, NBLK])
        agg2_blk = sb("agg2_blk", [D, NBLK])
        n_blk = sb("n_blk", [D, NBLK])
        h_blk = sb("h_blk", [D_SAGE, NBLK])
        sqn = sb("sqn", [P, J, D + 1])
        varn = sb("varn", [P, 2, J])
        rstdn = sb("rstdn", [P, 2, J])
        zn = sb("zn", [P, J, D])
        tabn = sb("tabn", [P, J, 2, D])
        partn = sb("partn", [P, J, PARTS, D], bf16)
        restn = sb("restn", [P, J, D])
        xs = sb("xs", [P, J, D_NODE])
        xc = sb("xc", [P, J, D_NODE])
        xq = sb("xq", [P, J, D_NODE])
        xm = sb("xm", [P, J])
        t2n = sb("t2n", [P, J, D_NODE])
        aggd = sb("aggd", [PROWS, NBLK])
        outn = sb("outn", [P, J, D_NODE])
        x1_now = sb("x1_now", [P, J, D_NODE])
        n_in = edge_space[0:D + 1, 0, :]
        hd = edge_space[0:D, 1, :]

        words = edge_space[:, :, :].rearrange("p a w -> p (a w)")
        sweep_words = sweep_oh[:, :, :].rearrange("p t w -> p (t w)")
        at = GROUP * PAIRS // 2
        pair_oh = [w[:, 0:at].bitcast(bf16).rearrange("p (t k) -> p t k", t=GROUP)
                   for w in (words[:, 2 * HALF:6 * HALF], sweep_words)]
        pairs_out = [words[:, (6 + q) * HALF:(6 + q) * HALF + PAIRS // 2].bitcast(bf16) for q in range(2)]
        lo_oh = [e0_ring[q][:, :].bitcast(bf16).rearrange("p (t l) -> p t l", t=TILES) for q in range(2)]
        pair_iota = h_buf[0][:, 0:PAIRS // 2].bitcast(f16)
        now_key = [sb(f"now_key{q}", [P, TILES]) for q in range(2)]
        lo_em = dst_em
        key_em = agg_blk[:, :, :].rearrange("p a n -> p (a n)")[:, 0:NCH * TILES]
        src_all = words[:, 8 * HALF:8 * HALF + NCH * TILES].bitcast(i32)
        src_bits = words[:, 6 * HALF:6 * HALF + NCH * TILES].bitcast(i32)
        pairs_in = [words[:, i * PAIRS // 2:(i + 1) * PAIRS // 2].bitcast(bf16) for i in range(LOADS)]
        n_at, n_words = 4 * HALF, NB * J * PROWS // 2
        parts_flat = words[:, n_at:n_at + n_words].bitcast(bf16)
        row_parts = parts_flat.rearrange("p (n t d) -> p n t d", t=PARTS, d=D_NODE)
        row_rest = words[:, 6 * HALF:6 * HALF + NB * J * D_NODE].rearrange("p (n d) -> p n d", d=D_NODE)

        spare = sweep_oh[0:NCH, :, :].rearrange("c t w -> c (t w)")
        dst_rows = spare[:, 0:CHUNK].rearrange("c (h e) -> c h e", h=2)
        dst_rows_i = spare[:, CHUNK:2 * CHUNK].bitcast(i32)
        dst_next = words[0:NCH, 0:CHUNK].bitcast(i32)
        rises = words[0:NCH, CHUNK:2 * CHUNK]
        rel_rows = sb("rel_rows", [NCH, 2, HALF], bf16)
        dst_em_i = agg_blk[:, :, :].rearrange("p a n -> p (a n)")[:, 0:NCH * TILES].bitcast(i32)
        base_f = sb("base_f", [NCH, 2])
        top_f = sb("top_f", [NCH, 2])
        span_f = sb("span_f", [NCH, 6])
        span_row = sb("span_row", [1, NCH * 6])
        span_max = sb("span_max", [1, 1])
        base_row = sb("base_row", [1, NCH * 2])
        base_all = sb("base_all", [P, NCH, 2])

        ps_pre = [bank("ps_pre0"), bank("ps_pre1")]
        ps_y = [bank("ps_y0"), bank("ps_y1")]
        ps_zt = [bank("ps_zt0"), bank("ps_zt1")]
        ps_seg = bank("ps_seg")
        ps_misc = bank("ps_misc")

        st = sems("st", "loads consts ident chain rel_ready base_ready base_out base_in biases biasrow_in "
                        "mm folded flag_ready sent pool_set ready rows_out")
        names = ("attr_in0 attr_in1 idx_in0 idx_in1 idxd_in0 idxd_in1 relb_in0 relb_in1 prw_in0 prw_in1 "
                 "gathered0 gathered1 gathered_d0 gathered_d1 e1_out0 e1_out1 "
                 "enc_pre enc_h enc_y enc_sq enc_var enc_z enc_zt enc_e newton "
                 "ohf ohe rows_in blk_pre blk_h blk_y blk_sq blk_var blk_z blk_zt blk_e1 seg added swept_oh")
        sums = "idx_in0 idx_in1 gathered0 gathered1 seg added swept_oh table "
        block_only = " ".join(n for n in names.split()
                              if not n.startswith(("attr", "enc", "e1_out", "blk_zt", "blk_e1")))
        counting = " e1_in0 e1_in1 src_in keyed now lo pair_oh paired halved out0 out1"
        PH = [sems(f"p{p}", (names, block_only + counting, sums + "in0 in1 in2 in3 inverted",
                               sums + "in0 in1 in2 in3")[p]) for p in range(4)]
        edges_done = [sem(f"edges_done{p}") for p in range(4)]
        mlp = sems("mlp", "block_in pre h y sq var newton z zt n tab evac parts")
        ND = [{**(mlp if i < 3 else {}), "first": NB * i if i < 3 else 0, **sems(f"n{i}", own)}
              for i, own in enumerate(("split stored", "scaled split stored", "scaled blk own x1 x1t stored",
                                       "aggd pre h tab x1 stored", "aggd parts newton2 own x1"))]
        s_final = sem("s_final")

        block = ctx.enter_context(nc.Block())

        def y_bank(i, u):
            return ps_y[0] if i == 0 else (ps_y[1], ps_misc)[u % 2]

        def slot(s, name, u):
            return s[f"{name}{u % DEPTH}"]

        def wait(eng, s, v):
            if not (isinstance(v, int) and v <= 0):
                eng.wait_ge(s, v)

        def wait_all(eng, always, *pairs):
            values = [value(eng, v) for _, v in pairs]
            eng.wait_ge(*always)
            for (sem_of, _), v in zip(pairs, values):
                wait(eng, sem_of, v)

        def value(eng, v):
            return v if isinstance(v, int) else eng.to_reg(v)

        LOADED = 16 * 6

        def rounds(eng, back, ahead, body, unroll=None, n=NCH):
            unroll = unroll or (4 if back else 2)
            peeled = max(1, -(-back // unroll))
            for c in range(-ahead, unroll * peeled):
                body(c, c // 2, c % 4)
            top = (n - ahead) // unroll
            with eng.Fori(peeled, top) as k:
                for u in range(unroll):
                    body(unroll * k + u, unroll // 2 * k + u // 2, u)
            for c in range(unroll * top, n + back):
                body(c, c // 2, c % 4)

        def near(c, d):
            return None if isinstance(c, int) and not 0 <= c + d < NB else c + d

        def block_rounds(eng, back, body):
            rounds(eng, back, 1, lambda b, k, u: body(b, u % 2), 2, NB)

        def chunk(c, k, u, d):
            if isinstance(c, int) and not 0 <= c + d < NCH:
                return None
            return c + d, k + (u % 2 + d) // 2, (u + d) % 4

        def counts_in(s, c, u):
            return s[f"in{u}"], 4 * (c - u) + 16

        BANKS = [(0, HI0 * WIN), (HI0 * WIN, PAIRS)]

        def pair_bank(q, bk):
            return ((ps_pre[0], ps_y[0]), ps_zt)[q][bk]

        @block.sync
        def _(sp):
            sp.dma_start(dst_rows_i[:, :], I["dst_rows"]).then_inc(st["loads"], 16)
            sp.dma_start(dst_next, I["dst_next"]).then_inc(st["loads"], 16)
            sp.dma_start(dst_em_i, I["dst_em"]).then_inc(st["loads"], 16)
            for dst, src in ((packed[:, :], I["packed"]), (x_fm[:, :], I["x_fm"]), (x_em[:, :, :], I["x_em"])):
                sp.dma_start(dst, src).then_inc(st["loads"], 16)
            sp.wait_ge(st["base_ready"], 1)
            sp.dma_start(base_dram, base_f[:, :]).then_inc(st["base_out"], 16)
            sp.wait_ge(st["base_ready"], 2)
            sp.dma_start(span_dram, span_f[:, :]).then_inc(st["base_out"], 16)
            sp.wait_ge(st["rel_ready"], 1)
            sp.dma_start(rel_dram, rel_rows[:, :, :].rearrange("c h e -> c (h e)")).then_inc(st["rows_out"], 16)
            sp.wait_ge(st["base_out"], 32)
            sp.dma_start(base_row[:, :], base_dram.rearrange("(a c) h -> a (c h)", a=1)).then_inc(st["base_in"], 16)
            sp.dma_start(span_row[:, :], span_dram.rearrange("(a c) h -> a (c h)", a=1)).then_inc(st["base_in"], 16)
            sp.dma_start(base_all[:, :, :].rearrange("p c h -> p (c h)"),
                         base_dram.rearrange("(a c) h -> a (c h)", a=1).to_broadcast([P, NCH * 2])
                         ).then_inc(st["base_in"], 16)
            sp.wait_ge(st["biases"], 1)
            sp.dma_start(bias_dram.rearrange("(a s) t d -> a s t d", a=1), b1_part[:, :, :, :]).then_inc(st["sent"], 16)
            sp.wait_ge(st["sent"], 16)
            for t in range(TILES):
                sp.dma_start(b1_rows_all[:, :, t, :], bias_dram.rearrange("s a d -> a s d")).then_inc(st["biasrow_in"], 16)
            sp.wait_ge(st["rows_out"], 16)
            sp.wait_ge(st["flag_ready"], 1)
            general = sp.value_load(flag[0:1, 0:1], min_val=0, max_val=1)

            def store_tables(s):
                nd = ND[s]
                with sp.Fori(0, NB) as b:
                    sp.wait_ge(nd["parts"], nd["first"] + b + 1)
                    sp.dma_start(send_tab[s].rearrange("(b j p) d -> b p j d", j=J, p=P)[bass.ds(b, 1)]
                                 .rearrange("a p j d -> (a p) j d"), tabn[:, :, 0, :]).then_inc(nd["stored"], 16)
                    sp.dma_start(recv_tab[s].rearrange("(b j p) d -> b p j d", j=J, p=P)[bass.ds(b, 1)]
                                 .rearrange("a p j d -> (a p) j d"), tabn[:, :, 1, :]).then_inc(nd["stored"], 16)
                    sp.dma_start(recv_parts[s].rearrange("(b j p t) d -> b p j (t d)", j=J, p=P, t=PARTS)[bass.ds(b, 1)]
                                 .rearrange("a p j d -> (a p) j d"),
                                 partn[:, :, :, :].rearrange("p j t d -> p j (t d)")).then_inc(nd["stored"], 16)

            def store_sage(s, nd, src):
                with sp.Fori(0, NB) as b:
                    sp.wait_ge(nd["x1"], b + 1)
                    sp.dma_start(sage_tab[s].rearrange("(b j p) d -> b p j d", j=J, p=P)[bass.ds(b, 1)]
                                 .rearrange("a p j d -> (a p) j d"), src).then_inc(nd["stored"], 16)

            def edge_phase(p, g):
                s = PH[p]
                tab = p

                def windows(c, k, u):
                    h0 = sp.value_load(base_i[0:1, bass.ds(2 * c, 1)], min_val=0, max_val=N_NODES - 1)
                    h1 = sp.value_load(base_i[0:1, bass.ds(2 * c + 1, 1)], min_val=0, max_val=N_NODES - 1)
                    n_free = value(sp, c - 1)
                    sp.wait_ge(st["ready"], 1)
                    sp.wait_ge(st["rows_out"], 16)
                    wait(sp, s["ohf"], n_free)
                    sp.dma_start(relb_ring[u][:, :], rel_dram[bass.ds(c, 1)].to_broadcast([WROWS, CHUNK])
                                 ).then_inc(slot(s, "relb_in", u), 16)
                    wait(sp, s["rows_in"], c - 1)
                    for h, v in enumerate((h0, h1)):
                        sp.dma_start(prw_ring[u][:, h, :], recv_parts[tab][bass.ds(v * PARTS, WROWS)]
                                     ).then_inc(slot(s, "prw_in", u), 16)

                def indices(c, k, u):
                    wait(sp, slot(s, "gathered", u), 128 * k)
                    sp.dma_start(idx_ring[u][:, :], I["src_em"][bass.ds(c, 1)].rearrange("a p t -> (a p) t")
                                 ).then_inc(slot(s, "idx_in", u), 16)
                    if g and p < 2:
                        wait(sp, slot(s, "gathered_d", u), 128 * k)
                        sp.dma_start(idxd_ring[u][:, :], I["dst_idx"][bass.ds(c, 1)].rearrange("a p t -> (a p) t")
                                     ).then_inc(slot(s, "idxd_in", u), 16)

                def attrs(c, k, u):
                    n_free = value(sp, c - 1)
                    sp.wait_ge(st["ready"], 1)
                    wait(sp, s["enc_pre"], n_free)
                    sp.dma_start(attr_ring[u][:, :], I["attr_fm"][bass.ds(c, 1)].rearrange("a p t -> (a p) t")
                                 ).then_inc(slot(s, "attr_in", u), 16)

                def load_e1(c, k, u):
                    wait(sp, s["blk_pre"], c - 1)
                    sp.dma_start(e1_ring[u][:, :], e1_dram[bass.ds(c, 1)].rearrange("a p t -> (a p) t")
                                 ).then_inc(slot(s, "e1_in", u), 16)

                def store_pairs(c, k, u):
                    sp.wait_ge(s["halved"], c + 1)
                    sp.dma_start(pairs_dram[bass.ds(c, 1)].rearrange("a p t -> (a p) t"), pairs_out[u % 2]
                                 ).then_inc(s[f"out{u % 2}"], 16)

                def store_e1(c, k, u):
                    sp.wait_ge(s["blk_e1"], c + 1)
                    sp.dma_start(e1_dram[bass.ds(c, 1)].rearrange("a p t -> (a p) t"), e1_ring[u][:, :]
                                 ).then_inc(slot(s, "e1_out", u), 16)

                def body(c, k, u):
                    if ahead := chunk(c, k, u, 2):
                        indices(*ahead)
                        if p == 1:
                            load_e1(*ahead)
                        if p < 2 and not g:
                            windows(*ahead)
                    if p == 0 and (ahead := chunk(c, k, u, 4)):
                        attrs(*ahead)
                    if p == 0 and (done := chunk(c, k, u, -2)):
                        store_e1(*done)
                    if p == 1 and not g and (done := chunk(c, k, u, -1)):
                        store_pairs(*done)

                rounds(sp, 1, 4 if p == 0 else 2, body)
                if p == 0:
                    store_e1(NCH - 1, NCH // 2, 0)
                    sp.wait_ge(s["e1_out0"], 16 * (NCH // 2 + 1))
                    sp.wait_ge(s["e1_out1"], 16 * (NCH // 2))
                if p == 1 and not g:
                    sp.wait_ge(s["out0"], 16 * (NCH // 2 + 1))
                    sp.wait_ge(s["out1"], 16 * (NCH // 2))

            def load_pairs(p):
                s = PH[p]

                def body(c, k, u):
                    if n := chunk(c, k, u, LOADS - 1):
                        wait(sp, s["seg"], value(sp, c))
                        sem_in, _ = counts_in(s, n[0], n[2])
                        sp.dma_start(pairs_in[n[2]], pairs_dram[bass.ds(n[0], 1)].rearrange("a p t -> (a p) t")
                                     ).then_inc(sem_in, 16)

                rounds(sp, 0, LOADS - 1, body, LOADS)

            def either(p):
                with sp.If(general):
                    edge_phase(p, 1)
                with sp.Else():
                    if p < 2:
                        edge_phase(p, 0)
                    else:
                        load_pairs(p)
                sp.nop()

            store_tables(0)
            either(0)
            sp.wait_ge(edges_done[0], 1)
            sp.dma_start(src_all, I["src_all"]).then_inc(PH[1]["src_in"], 16)
            store_tables(1)
            either(1)
            store_sage(0, ND[2], x1_now[:, :, :])
            either(2)
            store_sage(1, ND[3], t2n[:, :, :])
            either(3)
            with sp.Fori(0, NB) as b:
                sp.wait_ge(ND[4]["x1"], b + 1)
                sp.dma_start(out.rearrange("(b j p) d -> b p j d", j=J, p=P)[bass.ds(b, 1)]
                             .rearrange("a p j d -> (a p) j d"), outn[:, :, :]).then_inc(s_final, 16)
            sp.wait_ge(s_final, 16 * NB)

        @block.gpsimd
        def _(pool):
            nc.gpsimd.memset(ident[:, :], 0.0).then_inc(st["ident"], 1)
            pool.wait_ge(st["ident"], 1)
            nc.gpsimd.affine_select(out=ident[:, :], in_=ident[:, :], compare_op=ALU.not_equal, fill=1.0,
                                    base=0, pattern=[[-1, P]], channel_multiplier=1).then_inc(st["ident"], 1)
            nc.gpsimd.iota(node_iota[:, :], pattern=[[1, NPAD]], base=0, channel_multiplier=0,
                           allow_small_or_imprecise_dtypes=True).then_inc(st["pool_set"], 1)
            for sums in (agg[:, 0, :], agg[:, 1, :], agg2[:, :]):
                nc.gpsimd.memset(sums, 0.0).then_inc(st["pool_set"], 1)
            pool.wait_ge(st["flag_ready"], 1)
            general = pool.value_load(flag[0:1, 0:1], min_val=0, max_val=1)

            def edge_phase(p, g):
                s = PH[p]
                tab = (send_tab + sage_tab)[p]
                ring = g_ring if p < 2 else gs_ring
                used = s["rows_in"] if p < 2 else s["seg"]
                per = NSW if g and p >= 2 else 1
                stored = ND[p]["stored"]
                stored_n = 16 * NB * (PARTS if p < 2 else 1)

                def gather(c, k, u):
                    n_idx, n_used = value(pool, 16 * k + 16), value(pool, (c - 1) * per)
                    pool.wait_ge(stored, stored_n)
                    pool.wait_ge(slot(s, "idx_in", u), n_idx)
                    wait(pool, used, n_used)
                    for t in range(TILES):
                        nc.gpsimd.indirect_dma_start(
                            out=ring[u][:, t, :], out_offset=None, in_=tab,
                            in_offset=bass.IndirectOffsetOnAxis(ap=idx_ring[u][:, t:t + 1], axis=0),
                        ).then_inc(slot(s, "gathered", u), 16)
                    if g and p < 2:
                        pool.wait_ge(stored, stored_n)
                        pool.wait_ge(slot(s, "idxd_in", u), n_idx)
                        for t in range(TILES):
                            nc.gpsimd.indirect_dma_start(
                                out=gd_ring[u][:, t, :], out_offset=None, in_=recv_tab[p],
                                in_offset=bass.IndirectOffsetOnAxis(ap=idxd_ring[u][:, t:t + 1], axis=0),
                            ).then_inc(slot(s, "gathered_d", u), 16)

                rounds(pool, 0, 0, gather)

            def either(p):
                with pool.If(general):
                    edge_phase(p, 1)
                with pool.Else():
                    if p < 2:
                        edge_phase(p, 0)
                pool.nop()

            for p in range(4):
                either(p)

        @block.scalar
        def _(act):
            act.wait_ge(st["loads"], LOADED)
            act.wait_ge(st["consts"], 1)

            def operands(i, b):
                nd = ND[i]
                wait(act, nd["pre"], nd["first"] + b)
                cols = bass.ds(b * NBLK, NBLK)
                if i == 0:
                    last = nc.scalar.activation(x_blk[:, :], x_fm[:, cols], ACT.Copy)
                else:
                    nc.scalar.activation(agg_blk[:, 0, :], agg[:, 0, cols], ACT.Copy)
                    nc.scalar.activation(n_in[D:D + 1, :], agg[D:D + 1, 1, cols], ACT.Copy)
                    if i == 2:
                        nc.scalar.activation(agg2_blk[:, :], agg2[:, cols], ACT.Copy)
                    last = nc.scalar.activation(n_in[0:D, :], n_fm[:, cols], ACT.Copy)
                last.then_inc(nd["block_in"], 1)

            def hidden(i, b):
                nd = ND[i]
                wait(act, nd["y"], nd["first"] + b)
                act.wait_ge(nd["pre"], nd["first"] + b + 1)
                nc.scalar.activation(hn[:, :], ps_pre[0][0:D, :], ACT.Silu, bias=nb0[i][:, :]).then_inc(nd["h"], 1)

            def squares(i, b, q):
                nd = ND[i]
                wait(act, nd["var"], nd["first"] + b)
                act.wait_ge(nd["y"], nd["first"] + b + 1)
                nc.scalar.activation(sqn[:, :, 0:D], ps_y[q][:, 0:J * D].rearrange("p (j d) -> p j d", d=D),
                                     ACT.Square, scale=D ** -0.5).then_inc(nd["sq"], 1)

            def tables(i, b):
                nd = ND[i]
                wait(act, nd["stored"], 48 * b)
                act.wait_ge(nd["tab"], nd["first"] + b + 1)
                nc.scalar.activation(tabn[:, :, :, :], ps_zt[1][:, :].rearrange("p (j s d) -> p j s d", s=2, d=D),
                                     ACT.Copy).then_inc(nd["evac"], 1)

            def decoder_hidden(b):
                nd = ND[2]
                wait(act, nd["parts"], nd["first"] + b)
                act.wait_ge(nd["tab"], nd["first"] + b + 1)
                nc.scalar.activation(hd, ps_pre[1][0:D, :], ACT.Silu, bias=dec_b0[:, :]).then_inc(nd["evac"], 1)

            def node_phase(i):
                nd = ND[i]
                if i:
                    act.wait_ge(edges_done[i - 1], 1)

                def body(b, q):
                    nxt, now, older, last = (near(b, d) for d in (1, 0, -2, -3))
                    if now is not None:
                        hidden(i, b)
                    if nxt is not None:
                        operands(i, nxt)
                    if now is not None:
                        squares(i, b, q)
                    if older is not None and i < 2:
                        tables(i, older)
                    if older is not None and i == 2:
                        decoder_hidden(older)
                    if last is not None and i == 2:
                        act.wait_ge(nd["x1t"], last + 1)
                        nc.scalar.activation(x1_fm[:, bass.ds(last * NBLK, NBLK)], ps_seg[0:D_NODE, :],
                                             ACT.Copy).then_inc(nd["blk"], 1)

                block_rounds(act, 3 if i == 2 else 2, body)

            def keep_pairs(c, k, u):
                s, q = PH[1], u % 2
                wait(act, s[f"out{q}"], 16 * k)
                act.wait_ge(s["paired"], 2 * c + 2)
                for bk, (lo, hi) in enumerate(BANKS):
                    last = nc.scalar.activation(pairs_out[q][:, lo:hi], pair_bank(q, bk)[:, 0:hi - lo], ACT.Copy)
                last.then_inc(s["halved"], 1)

            def edge_phase(p, g):
                s = PH[p]

                def silu(i, pre, h, hfree, bias, c):
                    wait(act, hfree, c)
                    act.wait_ge(pre, c + 1)
                    nc.scalar.activation(h_buf[i], ps_pre[i][:, :], ACT.Silu, bias=bias).then_inc(h, 1)

                def square(i, y, sq, free, c, u):
                    wait(act, free, c)
                    act.wait_ge(y, c + 1)
                    nc.scalar.activation(sq_buf[i][:, :, 0:D], y_bank(i, u)[:, :].rearrange("p (t d) -> p t d", d=D),
                                         ACT.Square, scale=D ** -0.5).then_inc(sq, 1)

                def to_e0(c, k, u):
                    wait(act, s["blk_e1"], c - 1)
                    act.wait_ge(s["enc_zt"], c + 1)
                    nc.scalar.activation(e0_ring[u][:, :], ps_zt[0][:, :], ACT.Identity,
                                         bias=bet[0][:, :], scale=gam[0][:, :]).then_inc(s["enc_e"], 1)

                def body(c, k, u):
                    first, enc, nxt, now = (chunk(c, k, u, d) for d in (3, 2, 1, 0))
                    if p == 0:
                        if enc:
                            square(0, s["enc_y"], s["enc_sq"], s["enc_var"], enc[0], enc[2])
                        if now:
                            square(1, s["blk_y"], s["blk_sq"], s["blk_var"], c, u)
                        if first:
                            silu(0, s["enc_pre"], s["enc_h"], s["enc_y"], b0[0][:, :], first[0])
                        if nxt:
                            to_e0(*nxt)
                            silu(1, s["blk_pre"], s["blk_h"], s["blk_y"], b0[1][:, :], nxt[0])
                        return
                    if nxt:
                        silu(1, s["blk_pre"], s["blk_h"], s["blk_y"], b0[2][:, :], nxt[0])
                        square(1, s["blk_y"], s["blk_sq"], s["blk_var"], nxt[0], nxt[2])
                    if now and not g:
                        keep_pairs(*now)

                if p < 2:
                    rounds(act, 1, (3, 1)[p], body)

            def either(p):
                with act.If(general):
                    edge_phase(p, 1)
                with act.Else():
                    if p < 2:
                        edge_phase(p, 0)
                act.nop()

            node_phase(0)
            act.wait_ge(st["flag_ready"], 1)
            general = act.value_load(flag[0:1, 0:1], min_val=0, max_val=1)
            either(0)
            node_phase(1)
            either(1)
            node_phase(2)
            either(2)

            def relu_round(b, q):
                nd = ND[3]
                if near(b, 0) is not None:
                    wait(act, nd["tab"], value(act, b))
                    act.wait_ge(nd["pre"], b + 1)
                    for dst in (h_blk[:, :], h_fm[:, bass.ds(b * NBLK, NBLK)]):
                        last = nc.scalar.activation(dst, ps_pre[0][0:D_SAGE, :], ACT.Relu, bias=s_b1[:, :])
                    last.then_inc(nd["h"], 1)

            block_rounds(act, 1, relu_round)
            either(3)

        @block.tensor
        def _(pe):
            mm = nc.tensor.matmul
            IDENT = (st["ident"], 2)
            pe.wait_ge(st["ident"], 2)
            pe.wait_ge(st["folded"], 1)
            for s in range(2):
                mm(ps_misc[D:D + 1, s * D:(s + 1) * D], bet_sum[:, s:s + 1], w_a[s][0:D, :], start=True, stop=True)
            mm(ps_misc[:, P:P + 1], w_e[1][:, :], bet[1][:, :], start=True, stop=True).then_inc(st["mm"], 1)

            def first_product(i, b):
                nd = ND[i]
                wait_all(pe, IDENT, (nd["h"], nd["first"] + b), (nd["block_in"], nd["first"] + b + 1))
                if i == 0:
                    mm(ps_pre[0][0:D, :], nenc_w0[:, :], x_blk[:, :], start=True, stop=True).then_inc(nd["pre"], 1)
                    return
                s = i - 1
                mm(ps_pre[0][0:D, :], w_n[s][:, :], n_in, start=True, stop=False)
                if s == 1:
                    mm(ps_pre[0][0:D, :], w_ag2[:, :], agg2_blk[:, :], start=False, stop=False)
                mm(ps_pre[0][0:D, :], w_ag[s][:, :], agg_blk[:, 0, :], start=False, stop=True).then_inc(nd["pre"], 1)

            def second_product(i, b, q):
                nd = ND[i]
                pe.wait_ge(nd["h"], nd["first"] + b + 1)
                mm(ps_y[q][:, 0:J * D], ones[0:1, :], nb1_row[i][:, :, :].rearrange("a j d -> a (j d)"),
                   start=True, stop=False)
                for j in range(J):
                    last = mm(ps_y[q][:, j * D:(j + 1) * D], hn[:, j * P:(j + 1) * P], nw1[i][:, :],
                              start=False, stop=j == J - 1)
                last.then_inc(nd["y"], 1)

            def turn_back(i, b):
                nd = ND[i]
                wait_all(pe, IDENT, (nd["z"], nd["first"] + b + 1))
                for j in range(J):
                    last = nc.tensor.transpose(ps_zt[0][0:D, j * P:(j + 1) * P], zn[:, j, :], ident[:, :])
                last.then_inc(nd["zt"], 1)

            def tables(i, b):
                nd = ND[i]
                wait(pe, nd["evac"], nd["first"] + b)
                pe.wait_ge(nd["n"], nd["first"] + b + 1)
                for j in range(J):
                    last = mm(ps_zt[1][:, j * 2 * D:(j + 1) * 2 * D], n_blk[:, j * P:(j + 1) * P],
                              w_sr[i][:, :], start=True, stop=True)
                last.then_inc(nd["tab"], 1)

            def decoder_first(b):
                nd = ND[2]
                wait_all(pe, IDENT, (nd["evac"], nd["first"] + b), (nd["n"], nd["first"] + b + 1))
                mm(ps_pre[1][0:D, :], dec_w0[:, :], n_blk[:, :], start=True, stop=True).then_inc(nd["tab"], 1)

            def decoder_second(b):
                nd = ND[2]
                wait_all(pe, IDENT, (nd["x1"], b), (nd["evac"], nd["first"] + b + 1))
                mm(ps_misc[:, 0:J * D_NODE], ones[0:1, :], dec_b1,
                   start=True, stop=False)
                for j in range(J):
                    last = mm(ps_misc[:, j * D_NODE:(j + 1) * D_NODE], hd[:, j * P:(j + 1) * P], dec_w1[:, :],
                              start=False, stop=j == J - 1)
                last.then_inc(nd["parts"], 1)

            def turn_x1(b):
                nd = ND[2]
                wait_all(pe, IDENT, (nd["blk"], b), (nd["x1"], b + 1))
                for j in range(J):
                    last = nc.tensor.transpose(ps_seg[0:D_NODE, j * P:(j + 1) * P], x1_now[:, j, :], ident[:, :])
                last.then_inc(nd["x1t"], 1)

            def node_phase(i):
                nd = ND[i]

                def body(b, q):
                    now, old, older, last = (near(b, d) for d in (0, -1, -2, -3))
                    if now is not None:
                        first_product(i, b)
                    if last is not None and i == 2:
                        decoder_second(last)
                    if older is not None and i < 2:
                        tables(i, older)
                    if older is not None and i == 2:
                        decoder_first(older)
                    if old is not None:
                        turn_back(i, old)
                    if now is not None:
                        second_product(i, b, q)
                    if last is not None and i == 2:
                        turn_x1(last)

                block_rounds(pe, 3 if i == 2 else 2, body)
                pe.wait_ge(nd["evac"], nd["first"] + NB)
                if i == 2:
                    pe.wait_ge(nd["blk"], NB)

            def count_pairs(g, c, k, u):
                s, q = PH[1], u % 2
                if g == 0:
                    wait(pe, s["halved"], value(pe, c - 1))
                pe.wait_ge(s["lo"], c + 1)
                pe.wait_ge(s["pair_oh"], 2 * c + g + 1)
                for i in range(GROUP):
                    t = g * GROUP + i
                    for bk, (lo, hi) in enumerate(BANKS):
                        last = mm(pair_bank(q, bk)[:, 0:hi - lo], lo_oh[q][:, t, :], pair_oh[g][:, i, lo:hi],
                                  start=t == 0, stop=t == TILES - 1)
                last.then_inc(s["paired"], 1)

            def edge_phase(p, g):
                s = PH[p]
                def enc_pre(c, k, u):
                    wait(pe, s["enc_h"], c)
                    pe.wait_ge(slot(s, "attr_in", u), 16 * k + 16)
                    mm(ps_pre[0][:, :], enc_w0[:, :], attr_ring[u][:, :], start=True, stop=True).then_inc(s["enc_pre"], 1)

                def second(i, h, z, done, c, u):
                    wait(pe, z, c - i)
                    pe.wait_ge(h, c + 1)
                    w = 0 if i == 0 else 1 + p
                    mm(y_bank(i, u)[:, :], ones_bf[0:PARTS, :], b1_rows[w][:, :, :].rearrange("a t d -> a (t d)"),
                       start=True, stop=False)
                    for j in range(J):
                        last = mm(y_bank(i, u)[:, j * P:(j + 1) * P], h_buf[i][:, j * P:(j + 1) * P], w1_bd[w][:, :],
                                  start=False, stop=j == J - 1)
                    last.then_inc(done, 1)

                def back(i, z, free, done, c, z_tile):
                    wait(pe, free, c)
                    pe.wait_ge(z, c + 1)
                    for j in range(J):
                        last = nc.tensor.transpose(
                            ps_zt[i][:, j * P:(j + 1) * P],
                            z_tile[:, 2 * j:2 * j + 2, :].rearrange("p t d -> p (t d)"), ident[:, :])
                    last.then_inc(done, 1)

                def gathered_rows(c, k, u):
                    wait(pe, s["blk_h"], c)
                    pe.wait_ge(slot(s, "gathered", u), 128 * k + 128)
                    if g:
                        pe.wait_ge(slot(s, "gathered_d", u), 128 * k + 128)
                    for ring in ([g_ring, gd_ring] if g else [g_ring]):
                        for j in range(J):
                            last = mm(ps_pre[1][:, j * P:(j + 1) * P],
                                      ring[u][:, 2 * j:2 * j + 2, :].rearrange("p t d -> p (t d)"), ident[:, :],
                                      is_transpose=ring is g_ring, start=ring is g_ring and j == 0, stop=False)
                    if not g:
                        pe.wait_ge(slot(s, "prw_in", u), 32 * k + 32)
                        pe.wait_ge(s["ohf"], c + 1)
                        for hf in range(2):
                            last = mm(ps_pre[1][hf * D:(hf + 1) * D, :], prw_ring[u][:, hf, :],
                                      ohf_ring[u][:, hf * HALF:(hf + 1) * HALF], start=False, stop=False)
                    last.then_inc(s["rows_in"], 1)

                def edge_rows(c, k, u):
                    if p == 0:
                        pe.wait_ge(s["enc_e"], c + 1)
                        e = e0_ring[u]
                    else:
                        pe.wait_ge(slot(s, "e1_in", u), 16 * k + 16)
                        e = e1_ring[u]
                    mm(ps_pre[1][:, :], w_e[p][:, :], e[:, :], start=False, stop=True).then_inc(s["blk_pre"], 1)

                def summed(u, t):
                    if p == 0:
                        return [(0, z_enc[u][:, t, :]), (D, z_blk[u][:, t, :])]
                    return [(0, z_blk[u][:, t, :] if p == 1 else gs_ring[u][:, t, :])]

                rows = D if p < 2 else D_NODE

                def seg(c, k, u):
                    if g:
                        return seg_sweep(c, k, u)
                    wait(pe, s["added"], 2 * c)
                    if p < 2:
                        pe.wait_ge(s["blk_z"], c + 1)
                    else:
                        pe.wait_ge(slot(s, "gathered", u), 128 * k + 128)
                    pe.wait_ge(s["ohe"], c + 1)
                    for hf in range(2):
                        for n in range(len(summed(u, 0))):
                            for j in range(J):
                                t = 2 * j + hf
                                at, z = summed(u, t)[n]
                                last = mm(ps_seg[at:at + rows, 2 * hf * WCOLS:(2 * hf + 1) * WCOLS], z,
                                          ohe_ring[u][:, t, :], start=j == 0, stop=j == J - 1)
                        if p == 0:
                            for j in range(J):
                                t = 2 * j + hf
                                last = mm(ps_seg[:, (2 * hf + 1) * WCOLS:(2 * hf + 2) * WCOLS], ones_bf[:, :],
                                          ohe_ring[u][:, t, :].bitcast(bf16).rearrange("p (w h) -> p w h", h=2)[:, :, 1],
                                          start=j == 0, stop=j == J - 1)
                    last.then_inc(s["seg"], 1)

                def seg_sweep(c, k, u):
                    with pe.Fori(0, NSW) as w:
                        if p < 2:
                            pe.wait_ge(s["blk_z"], c + 1)
                        else:
                            pe.wait_ge(slot(s, "gathered", u), 128 * k + 128)
                        pe.wait_ge(s["swept_oh"], c * NSW + w + 1)
                        for n in range(len(summed(u, 0))):
                            for t in range(TILES):
                                at, z = summed(u, t)[n]
                                last = mm(ps_seg[at:at + rows, 0:SWEEP], z, sweep_oh[:, t, :],
                                          start=t == 0, stop=t == TILES - 1)
                        if p == 0:
                            for t in range(TILES):
                                last = mm(ps_seg[:, SWEEP:2 * SWEEP], ones[:, :], sweep_oh[:, t, :],
                                          start=t == 0, stop=t == TILES - 1)
                        last.then_inc(s["seg"], 1)

                def body(c, k, u):
                    first, enc, nxt, now, old = (chunk(c, k, u, d) for d in (3, 2, 1, 0, -1))
                    if p == 0:
                        if enc:
                            second(0, s["enc_h"], s["enc_z"], s["enc_y"], enc[0], enc[2])
                        if now:
                            second(1, s["blk_h"], s["blk_z"], s["blk_y"], c, u)
                        if nxt:
                            gathered_rows(*nxt)
                            back(0, s["enc_z"], s["enc_e"], s["enc_zt"], nxt[0], z_enc[nxt[2]])
                        if old:
                            back(1, s["blk_z"], s["blk_e1"], s["blk_zt"], old[0], z_blk[old[2]])
                        if first:
                            enc_pre(*first)
                        if old:
                            seg(*old)
                        if nxt:
                            edge_rows(*nxt)
                        return
                    if p == 1 and nxt:
                        gathered_rows(*nxt)
                        edge_rows(*nxt)
                    summing = old if p == 1 else now
                    if summing:
                        seg(*summing)
                    if p == 1 and nxt:
                        second(1, s["blk_h"], s["blk_z"], s["blk_y"], nxt[0], nxt[2])
                    if p == 1 and now and not g:
                        for half in range(2):
                            count_pairs(half, *now)

                rounds(pe, *((1, 3), (1, 1), (0, 0), (0, 0))[p], body)

            def weigh(s, c, u):
                wait_all(pe, IDENT, (s["added"], c - 1), counts_in(s, c, u))
                for hi in range(HI):
                    last = mm(ps_zt[u % 2][0:PROWS, 0:WIN], parts_flat[:, hi * PROWS:(hi + 1) * PROWS],
                              pairs_in[u][:, hi * WIN:(hi + 1) * WIN], start=hi == 0, stop=hi == HI - 1)
                last.then_inc(s["seg"], 1)

            def either(p):
                with pe.If(general):
                    edge_phase(p, 1)
                with pe.Else():
                    if p < 2:
                        edge_phase(p, 0)
                    else:
                        pe.wait_ge(PH[p]["table"], 5)
                        rounds(pe, 0, 0, lambda c, k, u: weigh(PH[p], c, u), LOADS)
                pe.nop()

            node_phase(0)
            pe.wait_ge(st["flag_ready"], 1)
            general = pe.value_load(flag[0:1, 0:1], min_val=0, max_val=1)
            pe.wait_ge(st["biasrow_in"], 16 * TILES)
            pe.wait_ge(st["ready"], 1)
            either(0)
            pe.wait_ge(edges_done[0], 1)
            node_phase(1)
            either(1)
            pe.wait_ge(edges_done[1], 1)
            node_phase(2)
            either(2)
            pe.wait_ge(edges_done[2], 1)

            def sage_round(b, q):
                nd = ND[3]
                if near(b, 0) is not None:
                    wait_all(pe, IDENT, (nd["h"], b), (nd["aggd"], b + 1))
                    mm(ps_pre[0][0:D_SAGE, :], s_w1r[:, :], x_blk[:, :], start=True, stop=False)
                    mm(ps_pre[0][0:D_SAGE, :], s_w1l[:, :], aggd[:, :], start=False, stop=True).then_inc(nd["pre"], 1)
                old = near(b, -1)
                if old is not None:
                    y = ps_y[1 - q]
                    wait_all(pe, IDENT, (nd["x1"], old - 1), (nd["h"], old + 1))
                    for j in range(J):
                        last = mm(y[:, j * D_NODE:(j + 1) * D_NODE], h_blk[:, j * P:(j + 1) * P],
                                  s_w2l[:, :], start=True, stop=True)
                    last.then_inc(nd["tab"], 1)

            block_rounds(pe, 1, sage_round)
            pe.wait_ge(ND[3]["x1"], NB)
            either(3)
            pe.wait_ge(edges_done[3], 1)

            def last_round(b, q):
                nd = ND[4]
                if near(b, 0) is not None:
                    wait_all(pe, IDENT, (nd["x1"], b - 1))
                    mm(ps_y[q][:, 0:J * D_NODE], ones[0:1, :], s_b2,
                       start=True, stop=False)
                    pe.wait_ge(nd["aggd"], b + 1)
                    for j in range(J):
                        y = ps_y[q][:, j * D_NODE:(j + 1) * D_NODE]
                        mm(y, aggd[:, j * P:(j + 1) * P], eyes, start=False, stop=False)
                        last = mm(y, h_blk[:, j * P:(j + 1) * P], s_w2r[:, :], start=False, stop=j == J - 1)
                    last.then_inc(nd["parts"], 1)

            block_rounds(pe, 1, last_round)

        @block.vector
        def _(dve):
            v = nc.vector
            chain = [0]
            zero = node_iota[0:PROWS, 0:1]

            def link(ins):
                chain[0] += 1
                ins.then_inc(st["chain"], 1)
                dve.wait_ge(st["chain"], chain[0])

            v.memset(w1_bd_all[:, :, :], 0.0)
            for t in sq_buf:
                v.memset(t[:, :, D:D + 1], EPS)
            v.memset(sqn[:, :, D:D + 1], EPS)
            v.memset(var_buf[:, :, :], 1.0)
            v.memset(varn[:, :, :], 1.0)
            v.memset(ones_bf[:, :], 1.0)
            v.memset(ones[:, :], 1.0).then_inc(st["consts"], 1)
            dve.wait_ge(st["consts"], 1)
            dve.wait_ge(st["loads"], LOADED)
            link(v.tensor_copy(dst_rows[:, :, :].rearrange("c h e -> c (h e)"), dst_rows_i[:, :]))
            link(v.tensor_reduce(out=base_f[:, :], in_=dst_rows[:, :, :], axis=AX.X, op=ALU.min))
            link(v.tensor_reduce(out=top_f[:, :], in_=dst_rows[:, :, :], axis=AX.X, op=ALU.max))
            link(v.tensor_tensor(span_f[:, 0:2], top_f[:, :], base_f[:, :], ALU.subtract))
            link(v.tensor_tensor(span_f[:, 2:3], top_f[:, 1:2], base_f[:, 0:1], ALU.subtract))
            link(v.tensor_tensor(span_f[:, 3:4], base_f[:, 0:1], base_f[:, 1:2], ALU.subtract))
            v.tensor_scalar(span_f[:, 3:4], span_f[:, 3:4], float(WIN), None, ALU.mult).then_inc(st["base_ready"], 1)
            link(v.tensor_tensor(rises[:, 0:CHUNK - 1], dst_next[:, 0:CHUNK - 1], dst_next[:, 1:CHUNK], ALU.subtract))
            link(v.tensor_reduce(out=span_f[:, 4:5], in_=rises[:, 0:CHUNK - 1], axis=AX.X, op=ALU.max))
            link(v.tensor_tensor(rises[:, 0:CHUNK - RUN], dst_next[:, 0:CHUNK - RUN], dst_next[:, RUN:CHUNK],
                                 ALU.subtract))
            link(v.tensor_reduce(out=span_f[:, 5:6], in_=rises[:, 0:CHUNK - RUN], axis=AX.X, op=ALU.max))
            link(v.tensor_scalar(span_f[:, 4:5], span_f[:, 4:5], float(WIN), None, ALU.mult))
            v.tensor_scalar(span_f[:, 5:6], span_f[:, 5:6], 1.0, float(WIN), ALU.add,
                            ALU.mult).then_inc(st["base_ready"], 1)
            for h in range(2):
                last = v.tensor_scalar(rel_rows[:, h, :], dst_rows[:, h, :], base_f[:, h:h + 1], None, ALU.subtract)
            last.then_inc(st["rel_ready"], 1)
            link(v.tensor_reduce(out=row_mean[:, :], in_=centred, axis=AX.X, op=ALU.add))
            link(v.tensor_scalar(row_mean[:, :], row_mean[:, :], 1.0 / D, None, ALU.mult))
            link(v.tensor_tensor(centred, centred, bc(row_mean[:, :].unsqueeze(2), [P, 12, D]), ALU.subtract))
            for h in range(2):
                v.tensor_copy(w1_bd_all[h * D:(h + 1) * D, :, h * D:(h + 1) * D], centred[h * D:(h + 1) * D, 0:3, :])
            v.tensor_copy(nb1_row_all[:, :, :, :], bc(centred[0:1, 9:12, :].unsqueeze(2), [1, 3, J, D]))
            b1 = centred[0:1, 6:9, :]
            link(v.tensor_copy(b1_part[:, :, 0, :], b1))
            link(v.tensor_tensor(b1_rest[:, :, :], b1, b1_part[:, :, 0, :], ALU.subtract))
            link(v.tensor_copy(b1_part[:, :, 1, :], b1_rest[:, :, :]))
            link(v.tensor_tensor(b1_rest[:, :, :], b1_rest[:, :, :], b1_part[:, :, 1, :], ALU.subtract))
            link(v.tensor_copy(b1_part[:, :, 2, :], b1_rest[:, :, :]))
            v.nop().then_inc(st["biases"], 1)
            v.tensor_scalar(w_ag_both[:, :, :], w_a_both, gam_stack, None, ALU.mult)
            link(v.tensor_scalar(w_ag2[:, :], w_a[1][0:D, :], gam[2][0:D, :], None, ALU.mult))
            link(v.tensor_tensor(bet_sum[:, 0:1], bet[0][0:D, :], bet[1][0:D, :], ALU.add))
            link(v.tensor_tensor(bet_sum[:, 1:2], bet_sum[:, 0:1], bet[2][0:D, :], ALU.add))
            v.nop().then_inc(st["folded"], 1)
            dve.wait_ge(st["mm"], 1)
            for s in range(2):
                link(v.tensor_copy(w_n[s][D:D + 1, :], ps_misc[D:D + 1, s * D:(s + 1) * D]))
            link(v.tensor_tensor(b0[2][:, :], b0[2][:, :], ps_misc[:, P:P + 1], ALU.add))
            dve.wait_ge(st["base_in"], 48)
            link(v.tensor_copy(dst_em[:, :], dst_em_i))
            link(v.tensor_copy(base_i[:, :], base_row[:, :]))
            for h in range(2):
                link(v.tensor_tensor(
                    rel_em[:, :].rearrange("p (c j h) -> p c j h", j=J, h=2)[:, :, :, h],
                    dst_em[:, :].rearrange("p (c j h) -> p c j h", j=J, h=2)[:, :, :, h],
                    bc(base_all[:, :, h:h + 1], [P, NCH, J]), ALU.subtract))
            link(v.tensor_reduce(out=span_max[:, :], in_=span_row[:, :], axis=AX.X, op=ALU.max))
            link(v.tensor_scalar(flag[:, :], span_max[:, :], float(WIN), None, ALU.is_ge))
            dve.wait_ge(st["pool_set"], 1)
            v.nop().then_inc(st["ready"], 1)
            v.nop().then_inc(st["flag_ready"], 1)
            general = dve.value_load(flag[0:1, 0:1], min_val=0, max_val=1)

            def inverse_sqrt(y, x, counter, at, between=()):
                n = [0]
                between = list(between)

                def step(ins):
                    n[0] += 1
                    ins.then_inc(counter, 1)
                    if between:
                        between.pop(0)()
                    dve.wait_ge(counter, at + n[0])

                width = y.free_size()
                t, bits = newton_t[:, 0:width], newton_i[:, 0:width]
                step(v.tensor_scalar(bits, x.bitcast(i32), 1, None, ALU.logical_shift_right))
                step(v.tensor_scalar(y.bitcast(i32), bits, -1.0, float(0x5f3759df), ALU.mult, ALU.add))
                for i in range(NEWTON):
                    step(v.tensor_tensor(t, y, y, ALU.mult))
                    step(v.scalar_tensor_tensor(out=t, in0=t, scalar=-0.5, in1=x, op0=ALU.mult, op1=ALU.mult))
                    step(v.scalar_tensor_tensor(out=y, in0=t, scalar=1.5, in1=y, op0=ALU.add, op1=ALU.mult))

            def split_tables(i, b):
                nd = ND[i]
                rows = tabn[:, :, 1, :]

                def first():
                    dve.wait_ge(nd["evac"], nd["first"] + b + 1)
                    v.tensor_copy(partn[:, :, 0, :], rows).then_inc(nd["split"], 1)

                def rest():
                    dve.wait_ge(nd["split"], 4 * b + 1)
                    v.tensor_tensor(restn[:, :, :], rows, partn[:, :, 0, :], ALU.subtract).then_inc(nd["split"], 1)

                def second():
                    dve.wait_ge(nd["split"], 4 * b + 2)
                    v.tensor_copy(partn[:, :, 1, :], restn[:, :, :]).then_inc(nd["split"], 1)

                def rest_again():
                    dve.wait_ge(nd["split"], 4 * b + 3)
                    v.tensor_tensor(restn[:, :, :], restn[:, :, :], partn[:, :, 1, :],
                                    ALU.subtract).then_inc(nd["split"], 1)

                def third():
                    dve.wait_ge(nd["split"], 4 * b + 4)
                    v.tensor_copy(partn[:, :, 2, :], restn[:, :, :]).then_inc(nd["parts"], 1)

                return [first, rest, second, rest_again, third]

            def node_variance(i, b):
                nd = ND[i]
                dve.wait_ge(nd["sq"], nd["first"] + b + 1)
                v.tensor_reduce(out=varn[:, 0, :], in_=sqn[:, :, :], axis=AX.X, op=ALU.add).then_inc(nd["var"], 1)

            def node_z(i, b, q):
                v.tensor_tensor(zn[:, :, :], ps_y[q][:, 0:J * D].rearrange("p (j d) -> p j d", d=D),
                                bc(rstdn[:, 0, :].unsqueeze(2), [P, J, D]), ALU.mult).then_inc(ND[i]["z"], 1)

            def new_nodes(i, b):
                nd = ND[i]
                cols = n_fm[:, bass.ds(b * NBLK, NBLK)]
                n_free, n_zt = value(dve, nd["first"] + b), value(dve, nd["first"] + b + 1)
                dve.wait_ge(st["consts"], 1)
                wait(dve, nd["tab"], n_free)
                dve.wait_ge(nd["zt"], n_zt)
                if i == 0:
                    for dst in (n_blk[:, :], cols):
                        last = v.tensor_scalar(dst, ps_zt[0][0:D, :], ngam[0][:, :], nbet[0][:, :], ALU.mult, ALU.add)
                    last.then_inc(nd["n"], 1)
                    return
                v.scalar_tensor_tensor(out=cols, in0=ps_zt[0][0:D, :], scalar=ngam[i][:, :], in1=cols,
                                       op0=ALU.mult, op1=ALU.add).then_inc(nd["scaled"], 1)
                dve.wait_ge(nd["scaled"], b + 1)
                v.tensor_scalar(n_blk[:, :], cols, nbet[i][:, :], None, ALU.add)
                v.tensor_scalar(cols, cols, nbet[i][:, :], None, ALU.add).then_inc(nd["n"], 1)
                if i == 2:
                    v.tensor_copy(agg2[0:PROWS, bass.ds(b * NBLK, NBLK)], bc(zero, [PROWS, NBLK]))

            def residual_variance(nd, b, src, resid, var):
                n = [0]

                def step(ins):
                    n[0] += 1
                    ins.then_inc(nd["own"], 1)
                    dve.wait_ge(nd["own"], STEPS * b + n[0])

                step(v.tensor_tensor(xs[:, :, :], src, resid, ALU.add))
                step(v.tensor_reduce(out=xm[:, :], in_=xs[:, :, :], axis=AX.X, op=ALU.add))
                step(v.tensor_scalar(xm[:, :], xm[:, :], 1.0 / D_NODE, None, ALU.mult))
                step(v.tensor_tensor(xc[:, :, :], xs[:, :, :], bc(xm[:, :].unsqueeze(2), [P, J, D_NODE]), ALU.subtract))
                step(v.tensor_tensor(xq[:, :, :], xc[:, :, :], xc[:, :, :], ALU.mult))
                step(v.tensor_reduce(out=var, in_=xq[:, :, :], axis=AX.X, op=ALU.add))
                step(v.tensor_scalar(var, var, 1.0 / D_NODE, EPS, ALU.mult, ALU.add))

            STEPS = 7

            def scaled_rows(dst, rstd):
                return v.tensor_tensor(dst, xc[:, :, :], bc(rstd.unsqueeze(2), [P, J, D_NODE]), ALU.mult)

            def of_block(t, b):
                return t[:, bass.ds(b, 1), :].rearrange("p a (j d) -> p (a j) d", d=D_NODE)

            def node_phase(i):
                nd = ND[i]

                def body(b, q):
                    old, older, last = (near(b, d) for d in (-1, -2, -3))
                    split = split_tables(i, older) if older is not None and i < 2 else []
                    decoded = i == 2 and last is not None
                    if older is not None:
                        new_nodes(i, older)
                    if decoded:
                        dve.wait_ge(nd["parts"], nd["first"] + last + 1)
                        residual_variance(nd, last, ps_misc[:, 0:J * D_NODE].rearrange("p (j d) -> p j d", d=D_NODE),
                                          of_block(x_em, last), varn[:, 1, :])
                    if old is not None:
                        node_variance(i, old)
                        dve.wait_ge(nd["var"], nd["first"] + old + 1)
                    if i == 2 and (decoded or old is not None):
                        inverse_sqrt(rstdn[:, :, :].rearrange("p a j -> p (a j)"),
                                     varn[:, :, :].rearrange("p a j -> p (a j)"),
                                     nd["newton"], (nd["first"] + b - 1) * NSTEP)
                    elif old is not None:
                        inverse_sqrt(rstdn[:, 0, :], varn[:, 0, :], nd["newton"],
                                     (nd["first"] + old) * NSTEP)
                    if old is not None:
                        node_z(i, old, 1 - q)
                    for step_of in split:
                        step_of()
                    if decoded:
                        wait(dve, nd["stored"], 16 * last)
                        wait(dve, nd["x1t"], last)
                        scaled_rows(of_block(x1_em, last), rstdn[:, 1, :])
                        scaled_rows(x1_now[:, :, :], rstdn[:, 1, :]).then_inc(nd["x1"], 1)

                block_rounds(dve, 3 if i == 2 else 2, body)

            def pair_keys():
                s = PH[1]
                n = [0]

                def step(ins):
                    n[0] += 1
                    ins.then_inc(s["keyed"], 1)
                    dve.wait_ge(s["keyed"], n[0])

                step(v.tensor_copy(pair_iota, node_iota[:, 0:PAIRS]))
                step(v.tensor_tensor(key_em.rearrange("p (c t) -> p c t", t=TILES),
                                     dst_em[:, :].rearrange("p (c t) -> p c t", t=TILES),
                                     bc(base_all[:, :, 0:1], [P, NCH, TILES]), ALU.subtract))
                step(v.tensor_scalar(src_bits, src_all, P - 1, None, ALU.bitwise_and))
                step(v.tensor_copy(lo_em[:, :], src_bits))
                step(v.tensor_scalar(src_bits, src_all, P.bit_length() - 1, None, ALU.logical_shift_right))
                step(v.scalar_tensor_tensor(out=key_em, in0=src_bits, scalar=float(WIN), in1=key_em,
                                            op0=ALU.mult, op1=ALU.add))

            def pair_one_hots(c, k, u):
                s, q = PH[1], u % 2

                def lo_rows():
                    v.tensor_copy(now_key[q][:, :], key_em[:, bass.ds(c * TILES, TILES)]).then_inc(s["now"], 1)
                    wait(dve, s["paired"], value(dve, 2 * c - 2))
                    v.tensor_tensor(lo_oh[q], bc(node_iota[:, 0:P].unsqueeze(1), [P, TILES, P]),
                                    bc(lo_em[:, bass.ds(c * TILES, TILES)].unsqueeze(2), [P, TILES, P]),
                                    ALU.is_equal).then_inc(s["lo"], 1)

                def tile(t):
                    g, i = divmod(t, GROUP)
                    if i == 0:
                        wait(dve, s["paired"], 2 * c - 1 + g)
                        dve.wait_ge(s["now"], c + 1)
                    ins = v.tensor_scalar(pair_oh[g][:, i, :], pair_iota, now_key[q][:, t:t + 1], None, ALU.is_equal)
                    if i == GROUP - 1:
                        ins.then_inc(s["pair_oh"], 1)

                return [lo_rows] + [lambda t=t: tile(t) for t in range(TILES)]

            def add_sums(s, c, q):
                at = dve.value_load(base_i[0:1, bass.ds(2 * c, 1)], min_val=0, max_val=N_NODES - 1)
                dve.wait_ge(s["seg"], c + 1)
                wait(dve, s["added"], c)
                tgt = agg2[0:PROWS, bass.ds(at, WIN)]
                v.tensor_tensor(tgt, tgt, ps_zt[q][0:PROWS, 0:WIN], ALU.add).then_inc(s["added"], 1)

            def split_rows(p):
                s, n = PH[p], [0]
                rows_of = (x1_em, t2_em)[p - 2][:, :, :].rearrange("p b (j d) -> p (b j) d", d=D_NODE)

                def step(ins):
                    n[0] += 1
                    ins.then_inc(s["table"], 1)
                    dve.wait_ge(s["table"], n[0])

                dve.wait_ge(ND[p]["x1"], NB)
                step(v.tensor_copy(row_parts[:, :, 0, :], rows_of))
                step(v.tensor_tensor(row_rest, rows_of, row_parts[:, :, 0, :], ALU.subtract))
                step(v.tensor_copy(row_parts[:, :, 1, :], row_rest))
                step(v.tensor_tensor(row_rest, row_rest, row_parts[:, :, 1, :], ALU.subtract))
                step(v.tensor_copy(row_parts[:, :, 2, :], row_rest))

            def sage_body(p, c, k, u):
                add_sums(PH[p], c, u % 2)
                if p == 2 and u == 3:
                    round_of = (c - 3) // 4 if isinstance(c, int) else k // 2
                    cols = bass.ds(round_of * SHARE, SHARE)
                    v.tensor_scalar(rdeg[:, cols], agg[0:PROWS, 1, cols], 1.0, None,
                                    ALU.max).then_inc(PH[2]["inverted"], 1)
                    wait_all(dve, (st["consts"], 1), (PH[2]["inverted"], round_of + 1))
                    v.reciprocal(rdeg[:, cols], rdeg[:, cols])

            def edge_phase(p, g):
                s = PH[p]
                rows = (P, D, D_NODE, D_NODE)[p]

                def receivers_one_hot(c, k, u):
                    wait(dve, s["rows_in"], c - 1)
                    dve.wait_ge(slot(s, "relb_in", u), 16 * k + 16)
                    v.tensor_scalar(ohf_ring[u][:, :], relb_ring[u][:, :], win_row[:, :], None,
                                    ALU.is_equal).then_inc(s["ohf"], 1)

                def sums_one_hot(c, k, u):
                    v.tensor_tensor(ohe_ring[u][:, :, :], bc(node_iota[:, 0:WCOLS].unsqueeze(1), [P, TILES, WCOLS]),
                                    bc(rel_em[:, bass.ds(c * TILES, TILES)].unsqueeze(2), [P, TILES, WCOLS]),
                                    ALU.is_equal).then_inc(s["ohe"], 1)

                def variance(i, sq, done, c):
                    dve.wait_ge(sq, c + 1)
                    v.tensor_reduce(out=var_buf[:, i, :], in_=sq_buf[i][:, :, :], axis=AX.X,
                                    op=ALU.add).then_inc(done, 1)

                def normalise(i, done, z, u):
                    v.tensor_tensor(z[:, :, :], y_bank(i, u)[:, :].rearrange("p (t d) -> p t d", d=D),
                                    bc(rstd_buf[:, i, :].unsqueeze(2), [P, TILES, D]), ALU.mult).then_inc(done, 1)

                def make_e1(c, k, u):
                    wait(dve, slot(s, "e1_out", u), 16 * k)
                    dve.wait_ge(s["blk_zt"], c + 1)
                    v.scalar_tensor_tensor(out=e1_ring[u][:, :], in0=ps_zt[1][:, :], scalar=gam[1][:, :],
                                           in1=e0_ring[u][:, :], op0=ALU.mult, op1=ALU.add).then_inc(s["blk_e1"], 1)

                def target(cols):
                    return agg[:, :, cols] if p == 0 else agg2[0:rows, cols]

                def add_up(c):
                    if g:
                        return add_sweep(c)
                    b_at = [dve.value_load(base_i[0:1, bass.ds(2 * c + h, 1)], min_val=0, max_val=N_NODES - 1)
                            for h in range(2)]
                    dve.wait_ge(s["seg"], c + 1)
                    for h in range(2):
                        src = ps_seg[:, 2 * h * WCOLS:(2 * h + 2) * WCOLS].rearrange("p (a w) -> p a w", a=2)
                        src = src[:, :, 0:WIN] if p == 0 else src[0:rows, 0, 0:WIN]
                        tgt = target(bass.ds(b_at[h], WIN))
                        wait(dve, s["added"], 2 * c + h)
                        v.tensor_tensor(tgt, tgt, src, ALU.add).then_inc(s["added"], 1)

                def add_sweep(c):
                    with dve.Fori(0, NSW) as w:
                        v.tensor_tensor(sweep_oh[:, :, :],
                                        bc(node_iota[:, bass.ds(w * SWEEP, SWEEP)].unsqueeze(1), [P, TILES, SWEEP]),
                                        bc(dst_em[:, bass.ds(c * TILES, TILES)].unsqueeze(2), [P, TILES, SWEEP]),
                                        ALU.is_equal).then_inc(s["swept_oh"], 1)
                        dve.wait_ge(s["seg"], c * NSW + w + 1)
                        src = ps_seg[0:rows, 0:SWEEP]
                        if p == 0:
                            src = ps_seg[:, :].rearrange("p (a w) -> p a w", a=2)
                        tgt = target(bass.ds(w * SWEEP, SWEEP))
                        v.tensor_tensor(tgt, tgt, src, ALU.add).then_inc(s["added"], 1)
                        dve.wait_ge(s["added"], c * NSW + w + 1)

                def body_a(c, k, u):
                    enc, now, old = (chunk(c, k, u, d) for d in (2, 0, -1))
                    if enc:
                        variance(0, s["enc_sq"], s["enc_var"], enc[0])
                    if now:
                        variance(1, s["blk_sq"], s["blk_var"], c)
                    fill = []
                    if old and (enc or now):
                        fill.append(lambda: make_e1(*old))
                    elif old:
                        make_e1(*old)
                    if enc and not g:
                        fill.append(lambda: receivers_one_hot(*enc))
                    if now and not g:
                        fill.append(lambda: sums_one_hot(*now))
                    if enc or now:
                        if now:
                            dve.wait_ge(s["blk_var"], c + 1)
                        if enc:
                            dve.wait_ge(s["enc_var"], enc[0] + 1)
                        inverse_sqrt(rstd_buf[:, :, :].rearrange("p a t -> p (a t)"),
                                     var_buf[:, :, :].rearrange("p a t -> p (a t)"), s["newton"], (c + 2) * NSTEP, fill)
                    if enc:
                        normalise(0, s["enc_z"], z_enc[enc[2]], enc[2])
                    if now:
                        normalise(1, s["blk_z"], z_blk[now[2]], now[2])
                    if old:
                        add_up(old[0])

                def body_b(c, k, u):
                    new, nxt, now, old = (chunk(c, k, u, d) for d in (2, 1, 0, -1))
                    if new and not g:
                        receivers_one_hot(*new)
                    pairs = pair_one_hots(*nxt) if nxt and not g else []
                    if pairs:
                        pairs.pop(0)()
                    if old:
                        add_up(old[0])
                    if nxt:
                        variance(1, s["blk_sq"], s["blk_var"], nxt[0])
                        dve.wait_ge(s["blk_var"], nxt[0] + 1)
                        inverse_sqrt(rstd_buf[:, 1, :], var_buf[:, 1, :], s["newton"], (c + 1) * NSTEP,
                                     pairs)
                        normalise(1, s["blk_z"], z_blk[nxt[2]], nxt[2])
                        if not g:
                            sums_one_hot(*nxt)

                if p == 1 and not g:
                    pair_keys()
                if p == 0:
                    rounds(dve, 1, 2, body_a)
                elif p == 1:
                    rounds(dve, 1, 2, body_b)
                else:
                    rounds(dve, 0, 0, lambda c, k, u: add_up(c))
                dve.wait_ge(s["added"], NCH * NSW if g else 2 * NCH)

            def either(p):
                with dve.If(general):
                    if p == 2:
                        v.tensor_scalar(rdeg[:, :], agg[0:PROWS, 1, :], 1.0, None,
                                        ALU.max).then_inc(PH[2]["inverted"], 1)
                        dve.wait_ge(PH[2]["inverted"], 1)
                        v.reciprocal(rdeg[:, :], rdeg[:, :])
                    edge_phase(p, 1)
                with dve.Else():
                    if p < 2:
                        edge_phase(p, 0)
                    else:
                        split_rows(p)
                        rounds(dve, 0, 0, lambda c, k, u: sage_body(p, c, k, u), LOADS)
                        dve.wait_ge(PH[p]["added"], NCH)
                v.nop().then_inc(edges_done[p], 1)

            node_phase(0)
            dve.wait_ge(st["pool_set"], 4)
            either(0)
            node_phase(1)
            dve.wait_ge(PH[1]["src_in"], 16)
            either(1)
            node_phase(2)
            dve.wait_ge(ND[2]["blk"], NB)
            either(2)

            def sage_round(b, q):
                nd = ND[3]
                nxt, old = near(b, 1), near(b, -1)
                if nxt is not None:
                    cols = bass.ds(nxt * NBLK, NBLK)
                    wait(dve, nd["pre"], nxt)
                    v.tensor_copy(x_blk[:, :], x1_fm[:, cols])
                    v.tensor_tensor(aggd[:, :], agg2[0:PROWS, cols], rdeg[:, cols], ALU.mult).then_inc(nd["aggd"], 1)
                    wait_all(dve, (st["consts"], 1), (nd["aggd"], nxt + 1))
                    v.tensor_copy(agg2[0:PROWS, cols], bc(zero, [PROWS, NBLK]))
                if old is not None:
                    y = ps_y[1 - q][:, 0:J * D_NODE]
                    wait(dve, nd["stored"], 16 * old)
                    dve.wait_ge(nd["tab"], old + 1)
                    v.tensor_copy(t2_em[:, bass.ds(old, 1), :].rearrange("p a w -> p (a w)"), y)
                    v.tensor_copy(t2n[:, :, :].rearrange("p j d -> p (j d)"), y).then_inc(nd["x1"], 1)

            block_rounds(dve, 1, sage_round)
            either(3)

            def last_round(b, q):
                nd = ND[4]
                nxt, old = near(b, 1), near(b, -1)
                fill = []

                def h_in():
                    wait(dve, nd["parts"], nxt)
                    v.tensor_copy(h_blk[:, :], h_fm[:, bass.ds(nxt * NBLK, NBLK)])

                def mean_in():
                    cols = bass.ds(nxt * NBLK, NBLK)
                    v.tensor_tensor(aggd[:, :], agg2[0:PROWS, cols], rdeg[:, cols], ALU.mult).then_inc(nd["aggd"], 1)

                if nxt is not None:
                    fill = [h_in, mean_in]
                if old is not None:
                    dve.wait_ge(nd["parts"], old + 1)
                    residual_variance(nd, old, ps_y[1 - q][:, 0:J * D_NODE].rearrange("p (j d) -> p j d", d=D_NODE),
                                      of_block(x1_em, old), varn[:, 0, :])
                    inverse_sqrt(rstdn[:, 0, :], varn[:, 0, :], nd["newton2"], old * NSTEP, fill)
                    wait(dve, s_final, 16 * old)
                    scaled_rows(outn[:, :, :], rstdn[:, 0, :]).then_inc(nd["x1"], 1)
                else:
                    for f in fill:
                        f()

            block_rounds(dve, 1, last_round)


IN = {
    "edge_enc_w0": "L0_gnn_edge_enc_w0", "edge_enc_b0": "L0_gnn_edge_enc_b0", "edge_enc_w1": "L0_gnn_edge_enc_w1",
    "edge_enc_b1": "L0_gnn_edge_enc_b1", "edge_enc_g": "L0_gnn_edge_enc_g", "edge_enc_beta": "L0_gnn_edge_enc_beta",
    "node_enc_w0": "L0_gnn_node_enc_w0", "node_enc_b0": "L0_gnn_node_enc_b0", "node_enc_w1": "L0_gnn_node_enc_w1",
    "node_enc_b1": "L0_gnn_node_enc_b1", "node_enc_g": "L0_gnn_node_enc_g", "node_enc_beta": "L0_gnn_node_enc_beta",
    "edge_blk_w0": "L0_gnn_edge_blk_w0", "edge_blk_b0": "L0_gnn_edge_blk_b0", "edge_blk_w1": "L0_gnn_edge_blk_w1",
    "edge_blk_b1": "L0_gnn_edge_blk_b1", "edge_blk_g": "L0_gnn_edge_blk_g", "edge_blk_beta": "L0_gnn_edge_blk_beta",
    "node_blk_w0": "L0_gnn_node_blk_w0", "node_blk_b0": "L0_gnn_node_blk_b0", "node_blk_w1": "L0_gnn_node_blk_w1",
    "node_blk_b1": "L0_gnn_node_blk_b1", "node_blk_g": "L0_gnn_node_blk_g", "node_blk_beta": "L0_gnn_node_blk_beta",
    "dec_w0": "L0_gnn_dec_w0", "dec_b0": "L0_gnn_dec_b0", "dec_w1": "L0_gnn_dec_w1", "dec_b1": "L0_gnn_dec_b1",
    "W1_l": "L1_gnn_W1_l", "sage_b1": "L1_gnn_b1", "W1_r": "L1_gnn_W1_r", "W2_l": "L1_gnn_W2_l",
    "sage_b2": "L1_gnn_b2", "W2_r": "L1_gnn_W2_r",
}


def pack(w, np):
    def twice(m):
        return np.concatenate([m, m])

    def diagonal(m):
        out = np.zeros((2 * m.shape[0], 2 * m.shape[1]), m.dtype)
        out[:m.shape[0], :m.shape[1]] = m
        out[m.shape[0]:, m.shape[1]:] = m
        return out

    piece = {"enc_w0": diagonal(w["edge_enc_w0"]), "w1_0": twice(w["edge_enc_w1"]), "nw1_0": w["node_enc_w1"],
             "b1_0": w["edge_enc_b1"], "nb1_0": w["node_enc_b1"], "b0_0": twice(w["edge_enc_b0"]),
             "gam0": twice(w["edge_enc_g"]), "bet0": twice(w["edge_enc_beta"]), "nb0_0": w["node_enc_b0"],
             "ngam0": w["node_enc_g"], "nbet0": w["node_enc_beta"], "nenc_w0": w["node_enc_w0"],
             "dec_w0": w["dec_w0"], "dec_b0": w["dec_b0"], "dec_w1": w["dec_w1"],
             "dec_b1": np.tile(w["dec_b1"], J), "s_w1l": np.concatenate([w["W1_l"]] * PARTS),
             "eyes": np.concatenate([np.eye(D_NODE, dtype=np.float32)] * PARTS), "s_w1r": w["W1_r"], "s_b1": w["sage_b1"],
             "s_w2l": w["W2_l"], "s_w2r": w["W2_r"], "s_b2": np.tile(w["sage_b2"], J),
             "gam_stack": np.concatenate([w["edge_enc_g"], w["edge_blk_g"][0]]),
             "win_row": (np.arange(WROWS) // PARTS).astype(np.float32)}
    for s in range(2):
        e0, n0 = w["edge_blk_w0"][s], w["node_blk_w0"][s]
        piece.update({
            f"w_e{s}": diagonal(e0[0:D]), f"w_sr{s}": np.concatenate([e0[D:2 * D], e0[2 * D:3 * D]], axis=1),
            f"w1_{1 + s}": twice(w["edge_blk_w1"][s]), f"b1_{1 + s}": w["edge_blk_b1"][s],
            f"b0_{1 + s}": twice(w["edge_blk_b0"][s]), f"gam{1 + s}": twice(w["edge_blk_g"][s]),
            f"bet{1 + s}": twice(w["edge_blk_beta"][s]), f"w_n{s}": np.concatenate([n0[0:D], np.zeros((1, D), n0.dtype)]), f"w_a{s}": twice(n0[D:2 * D]),
            f"nw1_{1 + s}": w["node_blk_w1"][s], f"nb1_{1 + s}": w["node_blk_b1"][s],
            f"nb0_{1 + s}": w["node_blk_b0"][s], f"ngam{1 + s}": w["node_blk_g"][s],
            f"nbet{1 + s}": w["node_blk_beta"][s]})
    out = np.zeros((P, PACKED), np.float32)
    at = 0
    for name, rows, cols in PIECES:
        out[0:rows, at:at + cols] = piece[name].reshape(rows, cols)
        at += cols
    return out


def kernel(**inputs):
    import numpy as np
    import concourse.bacc as bacc
    from concourse.bass_utils import run_bass_kernel_spmd

    w = {n: np.asarray(inputs[full]) for n, full in IN.items()}
    a = {}
    x, src, dst = (np.asarray(inputs[n]) for n in ("x", "src", "dst"))
    attr = np.asarray(inputs["edge_attr_8"])
    E = NCH * CHUNK
    pad = E - N_EDGES
    far = np.full(pad, 1 << 20, dst.dtype)
    zero = np.zeros(pad, src.dtype)

    def edge_major(v):
        return np.ascontiguousarray(v.reshape(NCH, 2, J, P).transpose(0, 3, 2, 1).reshape(NCH, P, TILES))

    a["src_em"] = edge_major(np.concatenate([src, zero]))
    a["src_all"] = np.ascontiguousarray(a["src_em"].transpose(1, 0, 2).reshape(P, -1))
    a["dst_idx"] = edge_major(np.concatenate([dst, zero]))
    a["dst_em"] = np.ascontiguousarray(edge_major(np.concatenate([dst, far])).transpose(1, 0, 2).reshape(P, -1))
    a["dst_next"] = np.concatenate([dst, far + np.arange(pad, dtype=dst.dtype)]).reshape(NCH, CHUNK)
    a["dst_rows"] = np.concatenate([dst, np.repeat(dst[-1:], pad)]).reshape(NCH, CHUNK)
    attr = np.concatenate([attr, np.zeros((pad, D_EDGE), attr.dtype)])
    a["attr_fm"] = np.ascontiguousarray(attr.reshape(NCH, 2, HALF, D_EDGE).transpose(0, 1, 3, 2)
                                        .reshape(NCH, 2 * D_EDGE, HALF))
    xp = np.concatenate([x, np.zeros((NPAD - N_NODES, D_NODE), x.dtype)])
    a["x_fm"] = np.ascontiguousarray(xp.T)
    a["x_em"] = np.ascontiguousarray(xp.reshape(NB, J, P, D_NODE).transpose(2, 0, 1, 3).reshape(P, NB, J * D_NODE))
    a["packed"] = pack(w, np)

    nc = bacc.Bacc("TRN2", target_bir_lowering=False, num_devices=1)
    aps, arrays = {}, {}
    for n, v in a.items():
        arrays[f"in_{n}"] = v
        aps[n] = nc.dram_tensor(f"in_{n}", v.shape, mybir.dt.from_np(v.dtype), kind="ExternalInput").ap()
    out = nc.dram_tensor("out_nodes", (NPAD, D_NODE), mybir.dt.float32, kind="ExternalOutput").ap()
    build(nc, aps, out)
    r = run_bass_kernel_spmd(nc, [arrays], core_ids=[0])
    return r.results[0]["out_nodes"][:N_NODES]
```
